# Optimizing a Trainium2 kernel written in Bass

```python
import numpy as np
import jax
import jax.numpy as jnp

def _softmax(x, axis=-1):
    return jax.nn.softmax(x, axis=axis)

def _gelu(x):
    return jax.nn.gelu(x, approximate=True)

def _silu(x):
    return jax.nn.silu(x)

def _sigmoid(x):
    return jax.nn.sigmoid(x)

def _layernorm(x, axis=-1, eps=1e-05):
    m = jnp.mean(x, axis=axis, keepdims=True)
    v = jnp.var(x, axis=axis, keepdims=True)
    return (x - m) / jnp.sqrt(v + eps)

def _scatter_add(tgt, idx, src, axis=0):
    return tgt.at[idx].add(src)

def _segment_sum(src, seg, n):
    return jax.ops.segment_sum(src, seg, n)
kernel_name = 'mk_decoder_postln_d1_seqx_r4_d24b9d'

def setup_inputs(seed: int=0):
    np.random.seed(seed)
    _w = jnp.asarray

    def _rec_inputs():
        import jax
        import jax.numpy as jnp
        _rk = jax.random.key(seed)
        x = 7.22e-05 + 1 * jax.random.normal(jax.random.fold_in(_rk, 1), (4, 1024, 256), jnp.float32)
        _lenS = 1024 - jax.random.randint(jax.random.fold_in(_rk, 7), (4,), 0, max(1, 1024 // 4) + 1, jnp.int32)
        _lenS2 = 77 - jax.random.randint(jax.random.fold_in(_rk, 8), (4,), 0, max(1, 77 // 4) + 1, jnp.int32)
        _ctx_768P = jax.random.normal(jax.random.fold_in(_rk, 11), (4, 16, 192), jnp.float32)
        _ctx_768c = jax.random.dirichlet(jax.random.fold_in(_rk, 511), 0.3 * jnp.ones((16,), jnp.float32), (4, 77))
        _ctx_768t = jnp.einsum('bsk,bkd->bsd', _ctx_768c, _ctx_768P)
        _ctx_768t = _ctx_768t * jax.lax.rsqrt(jnp.mean(jnp.square(_ctx_768t)) + 1e-12) * 0.953939
        ctx_768 = -0.000191848 + 0.999787 * (_ctx_768t + 0.3 * jax.random.normal(jax.random.fold_in(_rk, 611), (4, 77, 192), jnp.float32))
        return (x, ctx_768)
    x, ctx_768 = _rec_inputs()

    def _L0_attn_setup():
        import jax, jax.numpy as jnp
        import numpy as np
        DIM = 256
        HEADS = 16
        DIM_HEAD = 64
        SEG = 128
        PMEM = 16
        RMS_EPS = 1.1920929e-07

        def _rope(t):
            n, d = (t.shape[-2], t.shape[-1])
            inv_freq = 1.0 / 10000.0 ** (jnp.arange(0, d, 2, dtype=jnp.float32) / d)
            freqs = jnp.arange(n, dtype=jnp.float32)[:, None] * inv_freq[None, :]
            freqs = jnp.repeat(freqs, 2, axis=-1)
            cos, sin = (jnp.cos(freqs), jnp.sin(freqs))
            x = t.reshape(t.shape[:-1] + (d // 2, 2))
            rot = jnp.stack((-x[..., 1], x[..., 0]), axis=-1).reshape(t.shape)
            return t * cos + rot * sin
        key = jax.random.key(seed)
        k0, k1, k2, k3 = jax.random.split(key, 4)
        seq = jax.random.normal(k0, (2, 1024, DIM), jnp.float32)
        g = jnp.ones((DIM,), jnp.float32)
        w_qkv = jax.random.normal(k1, (3 * HEADS * DIM_HEAD, DIM), jnp.float32) * 0.02
        w_out = jax.random.normal(k2, (DIM, HEADS * DIM_HEAD), jnp.float32) * 0.02
        pm = jax.random.normal(k3, (2, HEADS, PMEM, DIM_HEAD), jnp.float32) * 0.02
        return {'seq': seq, 'g': g, 'w_qkv': w_qkv, 'w_out': w_out, 'pm': pm}
    _L0_attn_all = _L0_attn_setup()
    _L0_attn_in = {k: v for k, v in _L0_attn_all.items() if k in ('g', 'w_qkv', 'w_out', 'pm')}
    del _L0_attn_all

    def _L0_xattn_setup():
        import jax, jax.numpy as jnp
        import numpy as np
        NUM_HEADS = 16
        CLAMP = 10000.0
        key = jax.random.key(seed)
        ks = jax.random.split(key, 8)
        B, Nq, Nkv, Cq, Ckv = (4, 512, 512, 256, 192)
        s_q = 1.0 / np.sqrt(Cq)
        s_kv = 1.0 / np.sqrt(Ckv)
        return {'query': jax.random.normal(ks[0], (B, Nq, Cq), jnp.float32), 'key_value': jax.random.normal(ks[1], (B, Nkv, Ckv), jnp.float32), 'Wq': jax.random.normal(ks[2], (Cq, Cq), jnp.float32) * s_q, 'bq': jnp.zeros((Cq,), jnp.float32), 'Wk': jax.random.normal(ks[3], (Ckv, Cq), jnp.float32) * s_kv, 'bk': jnp.zeros((Cq,), jnp.float32), 'Wv': jax.random.normal(ks[4], (Ckv, Cq), jnp.float32) * s_kv, 'bv': jnp.zeros((Cq,), jnp.float32), 'Wo': jax.random.normal(ks[5], (Cq, Cq), jnp.float32) * s_q, 'bo': jnp.zeros((Cq,), jnp.float32)}
    _L0_xattn_all = _L0_xattn_setup()
    _L0_xattn_in = {k: v for k, v in _L0_xattn_all.items() if k in ('Wq', 'bq', 'Wk', 'bk', 'Wv', 'bv', 'Wo', 'bo')}
    del _L0_xattn_all

    def _L0_ffn_setup():
        import jax, jax.numpy as jnp
        import numpy as np
        B, S, H = (2, 1024, 256)
        E, K, I = (8, 2, 352)
        key = jax.random.key(seed)
        ks = jax.random.split(key, 9)
        sc = 0.02
        return {'hidden_states': jax.random.normal(ks[0], (B, S, H), jnp.float32), 'gate_w': jax.random.normal(ks[1], (E, H), jnp.float32) * sc, 'w_gate': jax.random.normal(ks[2], (E, H, I), jnp.float32) * sc, 'w_up': jax.random.normal(ks[3], (E, H, I), jnp.float32) * sc, 'w_down': jax.random.normal(ks[4], (E, I, H), jnp.float32) * sc, 'sw_gate': jax.random.normal(ks[5], (H, I), jnp.float32) * sc, 'sw_up': jax.random.normal(ks[6], (H, I), jnp.float32) * sc, 'sw_down': jax.random.normal(ks[7], (I, H), jnp.float32) * sc, 'shared_gate_w': jax.random.normal(ks[8], (1, H), jnp.float32) * sc}
    _L0_ffn_all = _L0_ffn_setup()
    _L0_ffn_in = {k: v for k, v in _L0_ffn_all.items() if k in ('gate_w', 'w_gate', 'w_up', 'w_down', 'sw_gate', 'sw_up', 'sw_down', 'shared_gate_w')}
    del _L0_ffn_all
    return {'x': x, 'ctx_768': ctx_768, 'L0_attn_g': _L0_attn_in['g'], 'L0_attn_w_qkv': _L0_attn_in['w_qkv'], 'L0_attn_w_out': _L0_attn_in['w_out'], 'L0_attn_pm': _L0_attn_in['pm'], 'L0_xattn_Wq': _L0_xattn_in['Wq'], 'L0_xattn_bq': _L0_xattn_in['bq'], 'L0_xattn_Wk': _L0_xattn_in['Wk'], 'L0_xattn_bk': _L0_xattn_in['bk'], 'L0_xattn_Wv': _L0_xattn_in['Wv'], 'L0_xattn_bv': _L0_xattn_in['bv'], 'L0_xattn_Wo': _L0_xattn_in['Wo'], 'L0_xattn_bo': _L0_xattn_in['bo'], 'L0_ffn_gate_w': _L0_ffn_in['gate_w'], 'L0_ffn_w_gate': _L0_ffn_in['w_gate'], 'L0_ffn_w_up': _L0_ffn_in['w_up'], 'L0_ffn_w_down': _L0_ffn_in['w_down'], 'L0_ffn_sw_gate': _L0_ffn_in['sw_gate'], 'L0_ffn_sw_up': _L0_ffn_in['sw_up'], 'L0_ffn_sw_down': _L0_ffn_in['sw_down'], 'L0_ffn_shared_gate_w': _L0_ffn_in['shared_gate_w']}

def reference(x, ctx_768, L0_attn_g, L0_attn_w_qkv, L0_attn_w_out, L0_attn_pm, L0_xattn_Wq, L0_xattn_bq, L0_xattn_Wk, L0_xattn_bk, L0_xattn_Wv, L0_xattn_bv, L0_xattn_Wo, L0_xattn_bo, L0_ffn_gate_w, L0_ffn_w_gate, L0_ffn_w_up, L0_ffn_w_down, L0_ffn_sw_gate, L0_ffn_sw_up, L0_ffn_sw_down, L0_ffn_shared_gate_w):
    import jax
    import jax.numpy as jnp

    def _L0_attn_ref(seq, g, w_qkv, w_out, pm):
        import jax, jax.numpy as jnp
        import numpy as np
        DIM = 256
        HEADS = 16
        DIM_HEAD = 64
        SEG = 128
        PMEM = 16
        RMS_EPS = 1.1920929e-07

        def _rope(t):
            n, d = (t.shape[-2], t.shape[-1])
            inv_freq = 1.0 / 10000.0 ** (jnp.arange(0, d, 2, dtype=jnp.float32) / d)
            freqs = jnp.arange(n, dtype=jnp.float32)[:, None] * inv_freq[None, :]
            freqs = jnp.repeat(freqs, 2, axis=-1)
            cos, sin = (jnp.cos(freqs), jnp.sin(freqs))
            x = t.reshape(t.shape[:-1] + (d // 2, 2))
            rot = jnp.stack((-x[..., 1], x[..., 0]), axis=-1).reshape(t.shape)
            return t * cos + rot * sin
        b, n, dim = seq.shape
        x = seq * jax.lax.rsqrt(jnp.mean(seq * seq, axis=-1, keepdims=True) + RMS_EPS) * g
        qkv = x @ w_qkv.T
        q, k, v = jnp.split(qkv, 3, axis=-1)

        def heads(t):
            return t.reshape(b, n, HEADS, DIM_HEAD).transpose(0, 2, 1, 3)
        q, k, v = map(heads, (q, k, v))
        q, k = (_rope(q), _rope(k))
        w = n // SEG

        def seg(t):
            return t.reshape(b, HEADS, w, SEG, DIM_HEAD).transpose(0, 2, 1, 3, 4).reshape(b * w, HEADS, SEG, DIM_HEAD)
        q, k, v = map(seg, (q, k, v))
        pmk = jnp.broadcast_to(pm[0], (b * w,) + pm[0].shape)
        pmv = jnp.broadcast_to(pm[1], (b * w,) + pm[1].shape)
        k = jnp.concatenate([pmk, k], axis=2)
        v = jnp.concatenate([pmv, v], axis=2)
        scale = DIM_HEAD ** (-0.5)
        scores = jnp.einsum('bhid,bhjd->bhij', q, k) * scale
        i = jnp.arange(SEG)[:, None]
        j = jnp.arange(SEG + PMEM)[None, :]
        mask = j - PMEM <= i
        scores = jnp.where(mask, scores, -1e+30)
        attn = jax.nn.softmax(scores, axis=-1)
        out = jnp.einsum('bhij,bhjd->bhid', attn, v)
        out = out.transpose(0, 2, 1, 3).reshape(b * w, SEG, HEADS * DIM_HEAD)
        out = out @ w_out.T
        return out.reshape(b, n, dim)

    def _L0_xattn_ref(query, key_value, Wq, bq, Wk, bk, Wv, bv, Wo, bo):
        import jax, jax.numpy as jnp
        import numpy as np
        NUM_HEADS = 16
        CLAMP = 10000.0
        B, Nq, Cq = query.shape
        Nkv = key_value.shape[1]
        H = NUM_HEADS
        D = Cq // H
        scale = D ** (-0.5)
        q = (query @ Wq + bq).reshape(B, Nq, H, D).transpose(0, 2, 1, 3)
        k = (key_value @ Wk + bk).reshape(B, Nkv, H, D).transpose(0, 2, 1, 3)
        v = (key_value @ Wv + bv).reshape(B, Nkv, H, D).transpose(0, 2, 1, 3)
        attn = jnp.einsum('bhqd,bhkd->bhqk', q, k) * scale
        attn = jnp.clip(attn, -CLAMP, CLAMP)
        attn = jax.nn.softmax(attn, axis=-1)
        attn = jnp.where(jnp.any(jnp.isnan(attn)), jnp.asarray(1.0 / Nkv, attn.dtype), attn)
        x = jnp.einsum('bhqk,bhkd->bqhd', attn, v).reshape(B, Nq, Cq)
        return x @ Wo + bo

    def _L0_ffn_ref(hidden_states, gate_w, w_gate, w_up, w_down, sw_gate, sw_up, sw_down, shared_gate_w):
        import jax, jax.numpy as jnp
        import numpy as np
        B, S, H = (2, 1024, 256)
        E, K, I = (8, 2, 352)
        b, s, h = hidden_states.shape
        x = hidden_states.reshape(-1, h)
        logits = jnp.einsum('th,eh->te', x, gate_w)
        probs = jax.nn.softmax(logits.astype(jnp.float32), axis=-1)
        topk_w, topk_i = jax.lax.top_k(probs, K)
        topk_w = topk_w / jnp.sum(topk_w, axis=-1, keepdims=True)
        combine = jnp.sum(jax.nn.one_hot(topk_i, E, dtype=topk_w.dtype) * topk_w[..., None], axis=1)
        combine = combine.astype(x.dtype)
        g = jnp.einsum('th,ehi->eti', x, w_gate)
        u = jnp.einsum('th,ehi->eti', x, w_up)
        eo = jnp.einsum('eti,eih->eth', jax.nn.silu(g) * u, w_down)
        out = jnp.einsum('te,eth->th', combine, eo)
        sg = jax.nn.sigmoid(jnp.einsum('th,oh->to', x, shared_gate_w))
        so = jax.nn.silu(x @ sw_gate) * (x @ sw_up) @ sw_down
        out = out + sg * so
        return out.reshape(b, s, h)
    x = _layernorm(x + _L0_attn_ref(x, L0_attn_g, L0_attn_w_qkv, L0_attn_w_out, L0_attn_pm), axis=-1)
    x = _layernorm(x + _L0_xattn_ref(x, ctx_768, L0_xattn_Wq, L0_xattn_bq, L0_xattn_Wk, L0_xattn_bk, L0_xattn_Wv, L0_xattn_bv, L0_xattn_Wo, L0_xattn_bo), axis=-1)
    x = _layernorm(x + _L0_ffn_ref(x, L0_ffn_gate_w, L0_ffn_w_gate, L0_ffn_w_up, L0_ffn_w_down, L0_ffn_sw_gate, L0_ffn_sw_up, L0_ffn_sw_down, L0_ffn_shared_gate_w), axis=-1)
    return x

_drawn_inputs = setup_inputs


def setup_inputs(seed=0):
    import zlib

    import numpy as np

    out = dict(_drawn_inputs(seed))
    spreads = {'L0_attn_g': (1.0, 0.6),
     'L0_xattn_bq': (0.0, 0.342),
     'L0_xattn_bk': (0.0, 0.8),
     'L0_xattn_bv': (0.0, 0.1),
     'L0_xattn_bo': (0.0, 0.1)}
    factors = {'L0_attn_w_qkv': 2.849,
     'L0_attn_w_out': 2.762,
     'L0_attn_pm': 8.0,
     'L0_ffn_gate_w': 4.603,
     'L0_ffn_w_gate': 4.049,
     'L0_ffn_w_up': 4.007,
     'L0_ffn_w_down': 4.004,
     'L0_ffn_sw_gate': 5.852,
     'L0_ffn_sw_up': 5.752,
     'L0_ffn_sw_down': 5.762,
     'L0_ffn_shared_gate_w': 8.0}
    for name, (base, spread) in spreads.items():
        noise = np.random.default_rng([zlib.crc32(name.encode()), seed]).standard_normal(out[name].shape)
        drawn = base * np.exp(spread * noise) if base else spread * noise
        out[name] = jnp.asarray(drawn.astype(out[name].dtype))
    for name, factor in factors.items():
        out[name] = (out[name] * factor).astype(out[name].dtype)
    return out
```

```python
from contextlib import ExitStack

import concourse.bass as bass
from concourse import mybir

F32 = mybir.dt.float32
BF16 = mybir.dt.bfloat16
I32 = mybir.dt.int32
ALU = mybir.AluOpType
ACT = mybir.ActivationFunctionType
AX = mybir.AxisListType

P = 128
D = 256
KD = D // P
H, DH = 16, 64
SEG, MEM = 128, 16
NK = SEG + MEM
HX, DX = 16, 16
NCTX, CCTX = 77, 192
E, I = 9, 352
NE = 8
IT = [(0, 128), (128, 128), (256, 96)]
ROPE_HALF = DH // 2
SCALE = DH ** -0.5
XSCALE = DX ** -0.5
CLAMP = 10000.0
RMS_EPS = 1.1920929e-07
LN_EPS = 1e-5
TT = 512
NB = TT // P
FLAT = (HX // 2) * NCTX
NCH = -(-FLAT // P)
OG = (HX // 2) * (DX + 1)
FIRST_UP = [0] + [8 * e - 2 for e in range(1, E)]
FIRST_DOWN = [8 * e + 12 for e in range(E - 1)] + [8 * E - 2]
CHUNKS = [0, 2, 1, 3, 4, 5]
MAGIC = float(0x5F3759DF)


class Ring:

    def __init__(self, sem, name, slots, per):
        assert per % slots == 0
        self.slots, self.turns = slots, per // slots
        self.filled = [sem(f"{name}_filled{s}") for s in range(slots)]
        self.drained = [sem(f"{name}_drained{s}") for s in range(slots)]

    def full(self, i, k):
        return self.filled[k % self.slots], i * self.turns + (k // self.slots + 1)

    def free(self, i, k):
        return self.drained[k % self.slots], i * self.turns + (k // self.slots + 1)

    def done(self, i, k):
        return self.drained[k % self.slots], i * self.turns + (k // self.slots + 2)

    def credit(self, eng):
        for s in self.drained:
            eng.sem_inc(s, 1)


class Chain:

    def __init__(self, sem, eng):
        self.sem, self.eng, self.at, self.base = sem, eng, 0, 0

    def start(self, base):
        self.base, self.at = base, 0

    def then(self, ins):
        self.at += 1
        ins.then_inc(self.sem, 1)
        self.eng.wait_ge(self.sem, self.base + self.at)


RSQRT_STEPS = 12


def rsqrt_steps(dve, chain, out, var, eps, tmp_a, tmp_b):
    chain.then(dve.tensor_scalar(tmp_a, var, eps, None, ALU.add))
    chain.then(dve.tensor_scalar(tmp_b.bitcast(I32), tmp_a.bitcast(I32), 1, None, ALU.logical_shift_right))
    chain.then(dve.tensor_scalar(out.bitcast(I32), tmp_b.bitcast(I32), -1.0, MAGIC, ALU.mult, ALU.add))
    for _ in range(3):
        chain.then(dve.tensor_tensor(tmp_b, out, out, ALU.mult))
        chain.then(dve.scalar_tensor_tensor(out=tmp_b, in0=tmp_b, scalar=-0.5, in1=tmp_a, op0=ALU.mult, op1=ALU.mult))
        chain.then(dve.scalar_tensor_tensor(out=out, in0=tmp_b, scalar=1.5, in1=out, op0=ALU.add, op1=ALU.mult))


def bcast(ap, axis, n):
    shape = list(ap.shape)
    return ap.unsqueeze(axis).broadcast_to(shape[:axis] + [n] + shape[axis:])


def self_attention(nc, dram, keep, y_dram):
    x_d, rope_d = dram["x"], dram["rope"]
    segs = x_d.shape[0] // SEG
    ident = keep["ident"]
    with ExitStack() as ctx:
        def sb(name, shape, dt=F32):
            return ctx.enter_context(nc.sbuf_tensor(name, shape, dt))

        def sem(name):
            return ctx.enter_context(nc.semaphore(name))

        wqkv = sb("w_qkv", [P, KD, 3 * H * DH])
        wo = sb("w_out", [P, H * DH // P, D])
        g = sb("rms_gain", [P, KD])
        identb = sb("identity_bf16", [P, P], BF16)
        cmask = sb("causal_mask", [P, 2, NK], BF16)
        x = sb("x_seg", [P, 2, D])
        rope = sb("rope_seg", [P, 2, 3, ROPE_HALF])
        rope_r = sb("rope_scaled", [P, 2, 3, ROPE_HALF])
        sq = sb("x_squared", [P, D])
        ms = sb("mean_square", [P, 2])
        rstd = sb("rms_reciprocal", [P, 2])
        tmp_a = sb("rms_tmp_a", [P, 2])
        tmp_b = sb("rms_tmp_b", [P, 2])
        xT = sb("x_transposed", [P, KD, SEG])
        rot_a = sb("rot_cos", [P, 2, 512])
        rot_b = sb("rot_sin", [P, 2, 512])
        roped = sb("roped", [P, 4, 8, DH])
        qT = sb("q_transposed", [P, H // 2, SEG])
        kz = sb("k_transposed", [P, H // 2, 2, NK])
        v = sb("v_and_one", [P, H, DH + 1])
        vm = sb("mem_v_blocks", [P, 2, 8, DH + 1])
        prob = sb("probs", [P, H, NK])
        pm = sb("mem_probs", [P, H, MEM])
        mx = sb("score_max", [P, H])
        nm = sb("score_bias", [P, H])
        pT = sb("probs_transposed", [P, H, SEG])
        pmT = sb("mem_probs_transposed", [P, 2, SEG])
        rc = sb("sum_reciprocal", [P, H])
        o = sb("heads_out", [P, H, DH])
        oT = sb("heads_out_transposed", [P, 8, SEG])
        y = sb("y_seg", [P, 2, D])

        ps_q = ctx.enter_context(nc.psum_tensor("ps_q", [P, 2, 512], F32))
        ps_t = ctx.enter_context(nc.psum_tensor("ps_t", [P, 2, 512], F32))
        ps_s = ctx.enter_context(nc.psum_tensor("ps_s", [P, 2, 512], F32))
        ps_o = ctx.enter_context(nc.psum_tensor("ps_o", [P, 2, 512], F32))

        T_X, T_QK, T_O = 0, 2, 12
        T_PG, T_MH = [6, 7, 9, 10], [8, 11]
        rt = Ring(sem, "transpose", 2, 28)
        rq = Ring(sem, "project", 2, 16)
        rs = Ring(sem, "score", 2, 16)
        ro = Ring(sem, "attend", 2, 8)
        x_in = [sem("x_in0"), sem("x_in1")]
        s_static = sem("static_ready")
        s_small = sem("small_weights_loaded")
        s_wq = [sem(f"w_qkv_loaded{n}") for n in range(6)]
        s_w = sem("w_qkv_scaled")
        s_rms = sem("rms_chain")
        s_roped = sem("roped_ready")
        s_step = sem("mem_probs_waited")
        s_pm = sem("mem_probs_ready")
        s_max = sem("max_ready")
        s_bias = sem("bias_ready")
        s_recip = sem("recip_ready")
        s_store = [sem("y_stored0"), sem("y_stored1")]

        block = ctx.enter_context(nc.Block())

        @block.sync
        def _(sp):
            for ring in (rt, rq, rs, ro):
                ring.credit(sp)
            for s in (s_roped, s_store[0], s_store[1]):
                sp.sem_inc(s, 1)
            small = [(g[:, :], dram["attn_g"]), (ident[:, :], dram["ident"]), (identb[:, :], dram["identb"]),
                     (cmask[:, :, :], dram["causal"]), (kz[:, :, :, SEG:NK], dram["mem_k"]),
                     (vm[:, 0, :, :], dram["mem_v"][0]), (vm[:, 1, :, :], dram["mem_v"][1]),
                     (wo[:, :, :], dram["w_out"].rearrange("(j p) n -> p j n", p=P))]
            for dst, src in small[:2]:
                sp.dma_start(dst, src).then_inc(s_small, 16)
            for n, c in enumerate(CHUNKS):
                sp.dma_start(wqkv[:, :, c * 512:(c + 1) * 512],
                             dram["w_qkv"].rearrange("(k p) n -> p k n", p=P)[:, :, c * 512:(c + 1) * 512]
                             ).then_inc(s_wq[n], 16)
            for dst, src in small[2:]:
                sp.dma_start(dst, src).then_inc(s_small, 16)
            with sp.Fori(0, segs // 2) as i:
                for r in range(2):
                    sp.wait_ge(s_store[r], i * 16 + 1)
                    sp.dma_start(x[:, r, :], x_d[bass.ds(i * (2 * SEG) + r * SEG, SEG), :]).then_inc(x_in[r], 16)
                    sp.dma_start(rope[:, r, :, :], rope_d[bass.ds(i * (2 * SEG) + r * SEG, SEG), :, :]).then_inc(x_in[r], 16)

        @block.gpsimd
        def _(pool):
            pool.memset(kz[:, :, :, 0:SEG], 0.0).then_inc(s_static, 1)
            pool.memset(v[:, :, DH:DH + 1], 1.0).then_inc(s_static, 1)
            for e in range(E):
                load = keep["ffn_loaded"][e]
                for dst, name in ((keep["w_gate"], "w_gate"), (keep["w_up"], "w_up")):
                    pool.dma_start(dst[:, :, e, :], dram[name][e].rearrange("(k p) m -> p k m", p=P)).then_inc(load, 16)
                pool.dma_start(keep["w_down"][:, e, 0:2, :], dram["w_down"][e, 0:2 * P, :].rearrange("(n p) d -> p n d", p=P)).then_inc(load, 16)
                pool.dma_start(keep["w_down"][0:I - 2 * P, e, 2, :], dram["w_down"][e, 2 * P:I, :]).then_inc(load, 16)
            with pool.Fori(0, segs // 2) as i:
                for r in range(2):
                    for c in range(4):
                        pool.wait_ge(*rq.done(i, 8 * r + c))
                        pool.tensor_tensor(
                            roped[:, c, :, :].rearrange("p h (s j) -> p s h j", s=2),
                            rot_a[:, c % 2, :].rearrange("p (s h j) -> p s h j", s=2, h=8),
                            rot_b[:, c % 2, :].rearrange("p (s h j) -> p s h j", s=2, h=8),
                            ALU.add).then_inc(s_roped, 1)
                    for half in range(2):
                        for p in range(4 * half, 4 * half + 4):
                            pool.wait_ge(*rs.done(i, 8 * r + p))
                        pool.sem_inc(s_step, 1)
                        pool.tensor_copy(pm[:, 8 * half:8 * half + 8, :], prob[:, 8 * half:8 * half + 8, SEG:NK]
                                         ).then_inc(s_pm, 1)

        @block.tensor
        def _(pe):
            pe.wait_ge(s_static, 2)
            pe.wait_ge(s_small, 16 * 8)
            with pe.Fori(0, segs // 2) as i:
                for r in range(2):
                    def score(p):
                        if p % 4 == 0:
                            pe.wait_ge(*rt.done(i, 14 * r + T_QK + p // 2))
                            pe.wait_ge(*rt.done(i, 14 * r + T_QK + p // 2 + 1))
                        pe.wait_ge(*rs.free(i, 8 * r + p))
                        pe.matmul(ps_s[:, p % 2, 0:2 * NK], qT[:, p, :], kz[:, p, :, :], start=True, stop=False)
                        pe.matmul(ps_s[:, p % 2, 0:2 * NK], identb[:, :], cmask[:, :, :], start=False,
                                  stop=True).then_inc(rs.filled[p % 2], 1)

                    def turn_probs(g, use):
                        pe.wait_ge(*rs.done(i, 8 * r + 2 * g))
                        pe.wait_ge(*rs.done(i, 8 * r + 2 * g + 1))
                        pe.wait_ge(*rt.free(i, 14 * r + use))
                        for h in range(4):
                            ins = pe.transpose(ps_t[:, use % 2, h * P:(h + 1) * P], prob[:, 4 * g + h, 0:SEG], ident[:, :])
                        ins.then_inc(rt.filled[use % 2], 1)

                    def turn_mem(half, use):
                        pe.wait_ge(*rt.free(i, 14 * r + use))
                        pe.wait_ge(s_pm, i * 4 + (2 * r + half + 1))
                        pe.transpose(ps_t[:, use % 2, 0:P], pm[:, 8 * half:8 * half + 8, :],
                                     ident[:, :]).then_inc(rt.filled[use % 2], 1)

                    def attend(g):
                        pe.wait_ge(*rt.done(i, 14 * r + T_PG[g]))
                        if g % 2 == 0:
                            pe.wait_ge(*rt.done(i, 14 * r + T_MH[g // 2]))
                            pe.wait_ge(*rq.done(i, 8 * r + 4 + g // 2))
                        pe.wait_ge(*ro.free(i, 4 * r + g))
                        out = ps_o[:, g % 2, 0:4 * (DH + 1)]
                        pe.matmul(out, pmT[:, g // 2, :], vm[:, g // 2, 4 * (g % 2):4 * (g % 2) + 4, :],
                                  start=True, stop=False)
                        for h in range(4):
                            ins = pe.matmul(out[:, h * (DH + 1):(h + 1) * (DH + 1)], pT[:, 4 * g + h, :],
                                            v[:, 4 * g + h, :], start=False, stop=(h == 3))
                        ins.then_inc(ro.filled[g % 2], 1)

                    pe.wait_ge(x_in[r], i * 32 + 32)
                    for k in range(KD):
                        pe.wait_ge(*rt.free(i, 14 * r + T_X + k))
                        pe.transpose(ps_t[:, k, 0:P], x[:, r, k * P:(k + 1) * P], ident[:, :]).then_inc(rt.filled[k], 1)
                    for k in range(KD):
                        pe.wait_ge(*rt.done(i, 14 * r + T_X + k))
                    for n, c in enumerate(CHUNKS):
                        if r == 0:
                            pe.wait_ge(s_w, KD * (n + 1))
                        pe.wait_ge(*rq.free(i, 8 * r + n))
                        for k in range(KD):
                            ins = pe.matmul(ps_q[:, n % 2, :], xT[:, k, :], wqkv[:, k, c * 512:(c + 1) * 512],
                                            start=(k == 0), stop=(k == KD - 1))
                        ins.then_inc(rq.filled[n % 2], 1)
                    for c in range(4):
                        pe.wait_ge(s_roped, i * 8 + (r * 4 + c + 2))
                        pe.wait_ge(*rt.free(i, 14 * r + T_QK + c))
                        for p in range(4):
                            ins = pe.transpose(ps_t[:, c % 2, p * P:(p + 1) * P], roped[:, c, 2 * p:2 * p + 2, :], ident[:, :])
                        ins.then_inc(rt.filled[c % 2], 1)
                    score(0), score(1), score(2), score(3)
                    turn_probs(0, T_PG[0])
                    score(4)
                    turn_probs(1, T_PG[1])
                    turn_mem(0, T_MH[0])
                    score(5)
                    score(6)
                    attend(0)
                    turn_probs(2, T_PG[2])
                    score(7)
                    attend(1)
                    turn_probs(3, T_PG[3])
                    turn_mem(1, T_MH[1])
                    attend(2)
                    attend(3)
                    for half in range(2):
                        pe.wait_ge(*ro.done(i, 4 * r + 2 * half))
                        pe.wait_ge(*ro.done(i, 4 * r + 2 * half + 1))
                        pe.wait_ge(*rt.free(i, 14 * r + T_O + half))
                        for j in range(4):
                            ins = pe.transpose(ps_t[:, half, j * P:(j + 1) * P],
                                               o[:, 8 * half + 2 * j:8 * half + 2 * j + 2, :], ident[:, :])
                        ins.then_inc(rt.filled[half], 1)
                    for half in range(2):
                        pe.wait_ge(*rt.done(i, 14 * r + T_O + half))
                        pe.wait_ge(*rq.free(i, 8 * r + 6 + half))
                        for j in range(4):
                            ins = pe.matmul(ps_q[:, half, 0:D], oT[:, 4 * half + j, :], wo[:, 4 * half + j, :],
                                            start=(j == 0), stop=(j == 3))
                        ins.then_inc(rq.filled[half], 1)

        @block.vector
        def _(dve):
            chain = Chain(s_rms, dve)
            dve.wait_ge(s_static, 2)
            dve.wait_ge(s_small, 16 * 8)
            for n, c in enumerate(CHUNKS):
                dve.wait_ge(s_wq[n], 16)
                for k in range(KD):
                    w = wqkv[:, k, c * 512:(c + 1) * 512]
                    dve.tensor_scalar(w, w, g[:, k:k + 1], None, ALU.mult).then_inc(s_w, 1)
            with dve.Fori(0, segs // 2) as i:
                chain.start(i * (RSQRT_STEPS + 4))
                for r in range(2):
                    dve.wait_ge(x_in[r], i * 32 + 32)
                    chain.then(dve.tensor_tensor_reduce(sq[:, :], x[:, r, :], x[:, r, :], 1.0 / D, 0.0,
                                                        ALU.mult, ALU.add, ms[:, r:r + 1]))
                rsqrt_steps(dve, chain, rstd[:, :], ms[:, :], RMS_EPS, tmp_a[:, :], tmp_b[:, :])
                for r in range(2):
                    chain.then(dve.tensor_scalar(rope_r[:, r, :, :], rope[:, r, :, :], rstd[:, r:r + 1], None, ALU.mult))

                for r in range(2):
                    def rotate(n):
                        dve.wait_ge(*rq.full(i, 8 * r + n))
                        dve.wait_ge(s_roped, i * 8 + (max(r * 4 + n - 1, 0) + 1))
                        t = ps_q[:, n % 2, :].rearrange("p (s h j) -> p s h j", s=2, h=8)
                        b = rot_b[:, n % 2, :].rearrange("p (s h j) -> p s h j", s=2, h=8)
                        cos, sin, neg = (rope_r[:, r, m, :] for m in range(3))
                        dve.tensor_tensor(rot_a[:, n % 2, :].rearrange("p (q j) -> p q j", q=16),
                                          ps_q[:, n % 2, :].rearrange("p (q j) -> p q j", q=16),
                                          bcast(cos, 1, 16), ALU.mult)
                        dve.tensor_tensor(b[:, 0], t[:, 1], bcast(neg, 1, 8), ALU.mult)
                        dve.tensor_tensor(b[:, 1], t[:, 0], bcast(sin, 1, 8), ALU.mult).then_inc(rq.drained[n % 2], 1)

                    for n in range(4):
                        rotate(n)
                    for c in (1, 3):
                        dve.wait_ge(*rt.full(i, 14 * r + T_QK + c))
                        for z in range(2):
                            rows = slice(64 * z, 64 * z + 64)
                            ins = dve.tensor_copy(
                                kz[rows, 2 * (c - 1):2 * (c - 1) + 4, z, 0:SEG],
                                ps_t[rows, c % 2, :].rearrange("p (j t) -> p j t", j=4))
                        ins.then_inc(rt.drained[c % 2], 1)

                    def maxima(p):
                        dve.wait_ge(*rs.full(i, 8 * r + p))
                        dve.tensor_reduce(mx[:, 2 * p:2 * p + 2],
                                          ps_s[:, p % 2, 0:2 * NK].rearrange("p (h k) -> p h k", h=2),
                                          AX.X, ALU.max).then_inc(s_max, 1)
                        dve.wait_ge(s_max, i * 16 + (r * 8 + p + 1))
                        dve.tensor_scalar(nm[:, 2 * p:2 * p + 2], mx[:, 2 * p:2 * p + 2], -SCALE, None,
                                          ALU.mult).then_inc(s_bias, 1)

                    def take_probs(g):
                        use = T_PG[g]
                        dve.wait_ge(*rt.full(i, 14 * r + use))
                        dve.tensor_copy(pT[:, 4 * g:4 * g + 4, :], ps_t[:, use % 2, :].rearrange("p (h t) -> p h t", h=4)
                                        ).then_inc(rt.drained[use % 2], 1)

                    def take_mem(half):
                        use = T_MH[half]
                        dve.wait_ge(*rt.full(i, 14 * r + use))
                        dve.tensor_copy(pmT[:, half, :], ps_t[:, use % 2, 0:P]).then_inc(rt.drained[use % 2], 1)

                    def normalize(g):
                        dve.wait_ge(*ro.full(i, 4 * r + g))
                        out = ps_o[:, g % 2, 0:4 * (DH + 1)].rearrange("p (h d) -> p h d", h=4)
                        dve.reciprocal(rc[:, 4 * g:4 * g + 4], out[:, :, DH]).then_inc(s_recip, 1)
                        dve.wait_ge(s_recip, i * 8 + (r * 4 + g + 1))
                        dve.tensor_tensor(o[:, 4 * g:4 * g + 4, :], out[:, :, 0:DH],
                                          bcast(rc[:, 4 * g:4 * g + 4], 2, DH), ALU.mult).then_inc(ro.drained[g % 2], 1)

                    maxima(0), maxima(1), maxima(2), maxima(3)
                    take_probs(0)
                    maxima(4)
                    take_probs(1)
                    take_mem(0)
                    maxima(5)
                    maxima(6)
                    normalize(0)
                    take_probs(2)
                    maxima(7)
                    normalize(1)
                    take_probs(3)
                    take_mem(1)
                    normalize(2)
                    normalize(3)
                    dve.wait_ge(s_store[r], i * 16 + 1)
                    dve.wait_ge(*rq.full(i, 8 * r + 6))
                    dve.tensor_tensor(y[:, r, :], x[:, r, :], ps_q[:, 0, 0:D], ALU.add).then_inc(rq.drained[0], 1)
                    dve.wait_ge(*rq.done(i, 8 * r + 6))
                    dve.wait_ge(*rq.full(i, 8 * r + 7))
                    dve.tensor_tensor(y[:, r, :], y[:, r, :], ps_q[:, 1, 0:D], ALU.add).then_inc(rq.drained[1], 1)

        @block.scalar
        def _(act):
            with act.Fori(0, segs // 2) as i:
                for r in range(2):
                    for k in range(KD):
                        act.wait_ge(*rt.full(i, 14 * r + T_X + k))
                        act.copy(xT[:, k, :], ps_t[:, k, 0:P]).then_inc(rt.drained[k], 1)
                    for n in (4, 5):
                        act.wait_ge(*rq.full(i, 8 * r + n))
                        if r == 0:
                            act.wait_ge(s_rms, i * (RSQRT_STEPS + 4) + RSQRT_STEPS + 2)
                        act.activation(v[:, 8 * (n - 4):8 * (n - 4) + 8, 0:DH],
                                       ps_q[:, n % 2, :].rearrange("p (h d) -> p h d", h=8), ACT.Copy,
                                       scale=rstd[:, r:r + 1]).then_inc(rq.drained[n % 2], 1)
                    for c in (0, 2):
                        act.wait_ge(*rt.full(i, 14 * r + T_QK + c))
                        act.copy(qT[:, 2 * c:2 * c + 4, :], ps_t[:, c % 2, :].rearrange("p (j t) -> p j t", j=4)
                                 ).then_inc(rt.drained[c % 2], 1)
                    for p in range(8):
                        act.wait_ge(s_bias, i * 16 + (r * 8 + p + 1))
                        for h in (2 * p, 2 * p + 1):
                            ins = act.activation(prob[:, h, :], ps_s[:, p % 2, (h % 2) * NK:(h % 2 + 1) * NK], ACT.Exp,
                                                 bias=nm[:, h:h + 1], scale=SCALE)
                        ins.then_inc(rs.drained[p % 2], 1)
                    for half in range(2):
                        act.wait_ge(*rt.full(i, 14 * r + T_O + half))
                        act.copy(oT[:, 4 * half:4 * half + 4, :], ps_t[:, half, :].rearrange("p (j t) -> p j t", j=4)
                                 ).then_inc(rt.drained[half], 1)
                    act.wait_ge(*rq.done(i, 8 * r + 7))
                    act.dma_start(y_dram[bass.ds(i * (2 * SEG) + r * SEG, SEG), :], y[:, r, :]).then_inc(s_store[r], 16)
            for r in range(2):
                act.wait_ge(s_store[r], 16 * (segs // 2) + 1)


def cross_attention_and_experts(nc, dram, keep, y_dram, out):
    batches = dram["ctx_t"].shape[0]
    tiles = dram["x"].shape[0] // TT // batches
    ident, wg, wu, wd, s_ffn = keep["ident"], keep["w_gate"], keep["w_up"], keep["w_down"], keep["ffn_loaded"]
    with ExitStack() as ctx:
        def sb(name, shape, dt=F32):
            return ctx.enter_context(nc.sbuf_tensor(name, shape, dt))

        def sem(name):
            return ctx.enter_context(nc.semaphore(name))

        wq = sb("xw_q", [P, KD, D])
        wk = sb("xw_k", [P, 2, D])
        wv = sb("xw_v", [P, 2, D])
        wo = sb("xw_o", [P, KD, D])
        bq = sb("x_bias_q", [P, KD])
        bk = sb("x_bias_k", [P, KD])
        bv = sb("x_bias_v", [NCTX, D])
        bo = sb("x_bias_o", [P, D])
        spread = sb("key_of_flat", [NCTX, NCH * P])
        maskv = sb("head_of_flat", [P, NCH, HX // 2])
        maskk = sb("head_of_dim", [P, HX // 2])
        rev = sb("pick_order", [P, NE])
        gw = sb("router_w", [P, KD, E])
        ctxT = sb("ctx_transposed", [P, 2, NCTX])
        kT = sb("ctx_k", [P, KD, NCTX])
        kbd = sb("ctx_k_blocks", [P, KD, HX // 2, NCTX])
        va = sb("ctx_v_and_one", [NCTX, HX, DX + 1])
        vbd = sb("ctx_v_blocks", [P, KD, NCH, OG])
        y1 = sb("y1", [P, 2, NB, D])
        x1 = sb("x1", [P, NB, D])
        x1b = sb("x1_and_bias", [P, NB, D])
        st = sb("ln_stats", [P, NB, 6])
        ag = sb("ln_mean_var", [P, NB, 2])
        rstd = sb("ln_rstd", [P, NB])
        ta = sb("ln_tmp_a", [P, NB])
        tb = sb("ln_tmp_b", [P, NB])
        x1T = sb("x1_transposed", [P, KD, TT])
        qT = sb("xq_transposed", [P, KD, TT])
        sc = sb("x_scores", [P, 2, HX, NCTX])
        mx = sb("x_max", [P, 2, HX])
        pr = sb("x_probs", [P, 2, KD, NCH * P])
        pT = sb("x_probs_transposed", [P, 2, KD * NCH, P])
        rc = sb("x_recip", [P, HX])
        ox = sb("x_heads", [P, NB, D])
        oxT = sb("x_heads_transposed", [P, KD, TT])
        y2 = sb("y2", [P, NB, D])
        x2 = sb("x2", [P, NB, D])
        x2T = sb("x2_transposed", [P, KD, TT])
        lg = sb("logits", [P, NB, E])
        top = sb("top", [P, 4, NB])
        ex = sb("expert_exp", [P, NB, NE])
        r8 = sb("router_tmp", [P, 4, NB, NE])
        cmb = sb("combine", [P, NB, E])
        sil = sb("silu_gate", [P, 2, TT])
        hT = sb("hidden", [P, 2, len(IT), TT])
        acc = sb("acc", [P, NB, D])
        fin = sb("out_tile", [P, 2, NB, D])

        ps_t = ctx.enter_context(nc.psum_tensor("ps2_t", [P, 2, 512], F32))
        ps_q = ctx.enter_context(nc.psum_tensor("ps2_q", [P, 2, 512], F32))
        ps_m = ctx.enter_context(nc.psum_tensor("ps2_m", [P, 4, 512], F32))

        T_X1, T_P, T_OX, T_X2, T_N = 0, 2, 14, 16, 18
        Q_K, Q_V, Q_VB, Q_PREP = 0, 1, 2, 6
        Q_Q, Q_PV, Q_O, Q_R, Q_N = 0, 2, 6, 8, 9
        M_S, M_E, M_N = 0, 16, 16 + 8 * E
        rt = Ring(sem, "x_transpose", 2, T_N * tiles)
        rq = Ring(sem, "x_project", 2, Q_PREP + Q_N * tiles)
        rm = Ring(sem, "x_matrix", 4, M_N * tiles)
        s_w = sem("x_weights_loaded")
        s_ctx = sem("ctx_loaded")
        s_static = sem("x_static_ready")
        s_y1 = [sem("y1_loaded0"), sem("y1_loaded1")]
        s_kbd = sem("ctx_k_blocks_ready")
        s_chain = sem("dve_chain")
        s_step = sem("stats_waited")
        s_x1 = sem("x1_ready")
        s_x1b = sem("x1_and_bias_ready")
        s_max = sem("x_max_ready")
        s_sub = sem("x_shifted")
        s_exp = sem("x_exp_ready")
        s_recip = sem("x_recip_ready")
        s_x2 = sem("x2_ready")
        s_ex = sem("router_exp_ready")
        s_fin = sem("out_ready")
        s_out = [sem("out_stored0"), sem("out_stored1")]
        LN_STEPS = 2 * NB + RSQRT_STEPS
        ROUTER_STEPS = 20
        CHAIN = (3 * LN_STEPS + ROUTER_STEPS) * tiles
        block = ctx.enter_context(nc.Block())

        def tile_rows(i, j):
            return bass.ds(i * (tiles * TT) + j * TT, TT)

        small = [(wq[:, :, :], dram["xWq"].rearrange("(k p) n -> p k n", p=P)),
                 (wk[:, 0, :], dram["xWk"][0:P, :]), (wk[0:CCTX - P, 1, :], dram["xWk"][P:CCTX, :]),
                 (wv[:, 0, :], dram["xWv"][0:P, :]), (wv[0:CCTX - P, 1, :], dram["xWv"][P:CCTX, :]),
                 (wo[:, :, :], dram["xWo"].rearrange("(k p) n -> p k n", p=P)),
                 (bq[:, :], dram["xbq"]), (bk[:, :], dram["xbk"]),
                 (bv[:, :], dram["xbv"].partition_broadcast(NCTX)), (bo[:, :], dram["xbo"].partition_broadcast(P)),
                 (spread[:, :], dram["spread"]), (maskv[:, :, :], dram["maskv"]), (maskk[:, :], dram["maskk"]),
                 (rev[:, :], dram["rev"]), (gw[:, :, :], dram["router"].rearrange("(k p) e -> p k e", p=P))]

        @block.sync
        def _(sp):
            for ring in (rt, rq, rm):
                ring.credit(sp)
            for s in (s_x1, s_exp, s_out[0], s_out[1]):
                sp.sem_inc(s, 1)
            for dst, src in small:
                sp.dma_start(dst, src).then_inc(s_w, 16)
            with sp.Fori(0, batches) as i:
                sp.wait_ge(s_x1, i * (tiles * NB) + 1)
                sp.dma_start(ctxT[:, 0, :], dram["ctx_t"][bass.ds(i, 1), 0:P, :].rearrange("b c k -> (b c) k")).then_inc(s_ctx, 16)
                sp.dma_start(ctxT[0:CCTX - P, 1, :], dram["ctx_t"][bass.ds(i, 1), P:CCTX, :].rearrange("b c k -> (b c) k")).then_inc(s_ctx, 16)
                for j in range(tiles):
                    sp.dma_start(y1[:, j, :, :], y_dram[tile_rows(i, j), :].rearrange("(t p) d -> p t d", p=P)).then_inc(s_y1[j], 16)

        @block.gpsimd
        def _(pool):
            pool.memset(va[:, :, DX:DX + 1], 1.0).then_inc(s_static, 1)
            pool.memset(pr[:, :, :, FLAT:NCH * P], 0.0).then_inc(s_static, 1)
            pool.wait_ge(s_w, 16 * len(small))
            with pool.Fori(0, batches) as i:
                for j in range(tiles):
                    for t in range(NB):
                        n = j * NB + t
                        pool.wait_ge(s_x1, i * (tiles * NB) + (n + 2))
                        pool.tensor_tensor(x1b[:, t, :], x1[:, t, :], bo[:, :], ALU.add).then_inc(s_x1b, 1)
                    for t in range(NB):
                        n = j * NB + t
                        pool.wait_ge(s_max, i * (tiles * NB) + (n + 1))
                        pool.tensor_tensor(sc[:, t % 2, :, :], sc[:, t % 2, :, :], bcast(mx[:, t % 2, :], 2, NCTX),
                                           ALU.subtract).then_inc(s_sub, 1)

        @block.tensor
        def _(pe):
            pe.wait_ge(s_w, 16 * len(small))
            pe.wait_ge(s_static, 2)
            with pe.Fori(0, batches) as i:
                pe.wait_ge(s_ctx, i * 32 + 32)
                rows = [P, CCTX - P]
                pe.wait_ge(*rq.free(i, Q_K))
                for g in range(KD):
                    for k in range(2):
                        ins = pe.matmul(ps_q[:, 0, g * NCTX:(g + 1) * NCTX], wk[0:rows[k], k, g * P:(g + 1) * P],
                                        ctxT[0:rows[k], k, :], start=(k == 0), stop=(k == 1))
                ins.then_inc(rq.filled[0], 1)
                pe.wait_ge(*rq.free(i, Q_V))
                for k in range(2):
                    ins = pe.matmul(ps_q[0:NCTX, 1, 0:D], ctxT[0:rows[k], k, :], wv[0:rows[k], k, :],
                                    start=(k == 0), stop=(k == 1))
                ins.then_inc(rq.filled[1], 1)
                pe.wait_ge(*rq.done(i, Q_V))
                for u in range(4):
                    pe.wait_ge(*rq.free(i, Q_VB + u))
                    for n in range(3 * u, min(3 * u + 3, KD * NCH)):
                        g, c = n // NCH, n % NCH
                        ins = pe.matmul(ps_q[:, u % 2, (n % 3) * OG:(n % 3 + 1) * OG], spread[:, c * P:(c + 1) * P],
                                        va[:, g * 8:g * 8 + 8, :], start=True, stop=True)
                    ins.then_inc(rq.filled[u % 2], 1)
                for j in range(tiles):
                    tT, tQ, tM = T_N * j, Q_PREP + Q_N * j, M_N * j

                    def turn(src, use, ready):
                        for k in range(KD):
                            pe.wait_ge(*rt.free(i, tT + use + k))
                            for t in range(NB):
                                if k == 0:
                                    pe.wait_ge(*ready(t))
                                ins = pe.transpose(ps_t[:, (use + k) % 2, t * P:(t + 1) * P],
                                                   src[:, t, k * P:(k + 1) * P], ident[:, :])
                            ins.then_inc(rt.filled[(use + k) % 2], 1)
                        for k in range(KD):
                            pe.wait_ge(*rt.done(i, tT + use + k))

                    turn(x1, T_X1, lambda t: (s_x1, i * (tiles * NB) + (j * NB + t + 2)))
                    for g in range(KD):
                        pe.wait_ge(*rq.free(i, tQ + Q_Q + g))
                        for k in range(KD):
                            ins = pe.matmul(ps_q[:, (tQ + Q_Q + g) % 2, :], wq[:, k, g * P:(g + 1) * P], x1T[:, k, :],
                                            start=(k == 0), stop=(k == KD - 1))
                        ins.then_inc(rq.filled[(tQ + Q_Q + g) % 2], 1)
                    for g in range(KD):
                        pe.wait_ge(*rq.done(i, tQ + Q_Q + g))
                    pe.wait_ge(s_kbd, i * KD + KD)

                    def scores(t):
                        for u in range(4):
                            m = tM + M_S + 4 * t + u
                            pe.wait_ge(*rm.free(i, m))
                            pe.matmul(ps_m[:, u, 0:4 * NCTX], qT[:, u // 2, t * P:(t + 1) * P],
                                      kbd[:, u // 2, 4 * (u % 2):4 * (u % 2) + 4, :], start=True,
                                      stop=True).then_inc(rm.filled[u], 1)

                    def attend(t):
                        pe.wait_ge(s_exp, i * (tiles * NB) + (j * NB + t + 2))
                        for u in range(3):
                            use = tT + T_P + 3 * t + u
                            pe.wait_ge(*rt.free(i, use))
                            for n in range(4 * u, min(4 * u + 4, KD * NCH)):
                                g, c = n // NCH, n % NCH
                                ins = pe.transpose(ps_t[:, use % 2, (n % 4) * P:(n % 4 + 1) * P],
                                                   pr[:, t % 2, g, c * P:(c + 1) * P], ident[:, :])
                            ins.then_inc(rt.filled[use % 2], 1)

                    def weigh(t):
                        for u in range(3):
                            pe.wait_ge(*rt.done(i, tT + T_P + 3 * t + u))
                        use = tQ + Q_PV + t
                        pe.wait_ge(*rq.free(i, use))
                        for g in range(KD):
                            for c in range(NCH):
                                ins = pe.matmul(ps_q[:, use % 2, g * OG:(g + 1) * OG], pT[:, t % 2, g * NCH + c, :],
                                                vbd[:, g, c, :], start=(c == 0), stop=(c == NCH - 1))
                        ins.then_inc(rq.filled[use % 2], 1)

                    if j == 0:
                        for u in range(4):
                            pe.wait_ge(*rq.done(i, Q_VB + u))
                    scores(0)
                    scores(1)
                    attend(0)
                    scores(2)
                    weigh(0)
                    attend(1)
                    scores(3)
                    weigh(1)
                    attend(2)
                    weigh(2)
                    attend(3)
                    weigh(3)
                    turn(ox, T_OX, lambda t: rq.done(i, tQ + Q_PV + t))
                    for u in range(2):
                        use = tQ + Q_O + u
                        pe.wait_ge(*rq.free(i, use))
                        for t in (2 * u, 2 * u + 1):
                            for k in range(KD):
                                ins = pe.matmul(ps_q[:, use % 2, (t % 2) * D:(t % 2 + 1) * D],
                                                oxT[:, k, t * P:(t + 1) * P], wo[:, k, :], start=(k == 0), stop=(k == KD - 1))
                        ins.then_inc(rq.filled[use % 2], 1)
                    turn(x2, T_X2, lambda t: (s_x2, i * (tiles * NB) + (j * NB + t + 1)))
                    use = tQ + Q_R
                    pe.wait_ge(*rq.free(i, use))
                    for t in range(NB):
                        for k in range(KD):
                            ins = pe.matmul(ps_q[:, use % 2, t * E:(t + 1) * E], x2T[:, k, t * P:(t + 1) * P],
                                            gw[:, k, :], start=(k == 0), stop=(k == KD - 1))
                    ins.then_inc(rq.filled[use % 2], 1)

                    def up(e):
                        if j == 0:
                            pe.wait_ge(s_ffn[e], 16 * 4)
                        for n, (m0, m) in enumerate(IT):
                            for w, (mat, place) in enumerate(((wg, 0), (wu, 1))):
                                use = tM + M_E + FIRST_UP[e] + 2 * n + w
                                pe.wait_ge(*rm.free(i, use))
                                for k in range(KD):
                                    ins = pe.matmul(ps_m[0:m, use % 4, :], mat[:, k, e, m0:m0 + m], x2T[:, k, :],
                                                    start=(k == 0), stop=(k == KD - 1))
                                ins.then_inc(rm.filled[use % 4], 1)

                    def down(e):
                        for n in range(len(IT)):
                            pe.wait_ge(*rm.done(i, tM + M_E + FIRST_UP[e] + 2 * n + 1))
                        for u in range(2):
                            use = tM + M_E + FIRST_DOWN[e] + u
                            pe.wait_ge(*rm.free(i, use))
                            for t in (2 * u, 2 * u + 1):
                                for n, (m0, m) in enumerate(IT):
                                    ins = pe.matmul(ps_m[:, use % 4, (t % 2) * D:(t % 2 + 1) * D],
                                                    hT[0:m, e % 2, n, t * P:(t + 1) * P], wd[0:m, e, n, :],
                                                    start=(n == 0), stop=(n == len(IT) - 1))
                            ins.then_inc(rm.filled[use % 4], 1)

                    for e in range(E + 1):
                        if e < E:
                            up(e)
                        if e > 0:
                            down(e - 1)

        @block.vector
        def _(dve):
            chain = Chain(s_chain, dve)

            def layer_norm(src, dst, signal):
                for t in range(NB):
                    chain.at += 1
                    dve.bn_stats(st[:, t, :], src[:, t, :]).then_inc(s_chain, 1)
                dve.wait_ge(s_chain, chain.base + chain.at)
                dve.sem_inc(s_step, 1)
                for t in range(NB):
                    chain.at += 1
                    dve.bn_aggr(ag[:, t, :], st[:, t, :]).then_inc(s_chain, 1)
                dve.wait_ge(s_chain, chain.base + chain.at)
                rsqrt_steps(dve, chain, rstd[:, :], ag[:, :, 1], LN_EPS, ta[:, :], tb[:, :])
                for t in range(NB):
                    dve.tensor_scalar(dst[:, t, :], src[:, t, :], ag[:, t, 0:1], rstd[:, t:t + 1], ALU.subtract,
                                      ALU.mult).then_inc(signal, 1)

            dve.wait_ge(s_w, 16 * len(small))
            dve.wait_ge(s_static, 2)
            with dve.Fori(0, batches) as i:
                dve.wait_ge(*rq.full(i, Q_V))
                dve.tensor_tensor(va[:, :, 0:DX], ps_q[0:NCTX, 1, 0:D].rearrange("p (h d) -> p h d", h=HX),
                                  bv[:, :].rearrange("p (h d) -> p h d", h=HX), ALU.add).then_inc(rq.drained[1], 1)
                for g in range(KD):
                    dve.wait_ge(*rq.done(i, Q_K))
                    dve.tensor_tensor(kbd[:, g, :, :], bcast(kT[:, g, :], 1, HX // 2), bcast(maskk[:, :], 2, NCTX),
                                      ALU.mult).then_inc(s_kbd, 1)
                for u in range(4):
                    dve.wait_ge(*rq.full(i, Q_VB + u))
                    for n in range(3 * u, min(3 * u + 3, KD * NCH)):
                        g, c = n // NCH, n % NCH
                        ins = dve.tensor_tensor(vbd[:, g, c, :].rearrange("p (h d) -> p h d", h=HX // 2),
                                                ps_q[:, u % 2, (n % 3) * OG:(n % 3 + 1) * OG].rearrange("p (h d) -> p h d", h=HX // 2),
                                                bcast(maskv[:, c, :], 2, DX + 1), ALU.mult)
                    ins.then_inc(rq.drained[u % 2], 1)
                for j in range(tiles):
                    tQ, tM, blocks = Q_PREP + Q_N * j, M_N * j, j * NB
                    chain.start(i * CHAIN + j * (CHAIN // tiles))
                    dve.wait_ge(s_y1[j], i * 16 + 16)
                    layer_norm(y1[:, j], x1, s_x1)

                    def maxima(t):
                        if t >= 2:
                            dve.wait_ge(s_exp, i * (tiles * NB) + (blocks + t))
                        else:
                            dve.wait_ge(s_exp, i * (tiles * NB) + (blocks + 1))
                        for u in range(4):
                            dve.wait_ge(*rm.full(i, tM + M_S + 4 * t + u))
                            dve.tensor_scalar(sc[:, t % 2, 4 * u:4 * u + 4, :],
                                              ps_m[:, u, 0:4 * NCTX].rearrange("p (h k) -> p h k", h=4),
                                              CLAMP / XSCALE, -CLAMP / XSCALE, ALU.min, ALU.max).then_inc(rm.drained[u], 1)
                        for u in range(4):
                            dve.wait_ge(*rm.done(i, tM + M_S + 4 * t + u))
                        dve.tensor_reduce(mx[:, t % 2, :], sc[:, t % 2, :, :], AX.X, ALU.max).then_inc(s_max, 1)

                    def normalize(t):
                        use = tQ + Q_PV + t
                        dve.wait_ge(*rq.full(i, use))
                        o = ps_q[:, use % 2, 0:KD * OG].rearrange("p (h d) -> p h d", h=HX)
                        dve.reciprocal(rc[:, :], o[:, :, DX]).then_inc(s_recip, 1)
                        dve.wait_ge(s_recip, i * (tiles * NB) + (blocks + t + 1))
                        dve.tensor_tensor(ox[:, t, :].rearrange("p (h d) -> p h d", h=HX), o[:, :, 0:DX],
                                          bcast(rc[:, :], 2, DX), ALU.mult).then_inc(rq.drained[use % 2], 1)

                    def take(u, t):
                        use = T_N * j + T_P + 3 * t + u
                        n = min(4, KD * NCH - 4 * u)
                        dve.wait_ge(*rt.full(i, use))
                        dve.tensor_copy(pT[:, t % 2, 4 * u:4 * u + n, :],
                                        ps_t[:, use % 2, 0:n * P].rearrange("p (n t) -> p n t", n=n)
                                        ).then_inc(rt.drained[use % 2], 1)

                    maxima(0)
                    maxima(1)
                    take(1, 0)
                    maxima(2)
                    normalize(0)
                    take(1, 1)
                    maxima(3)
                    normalize(1)
                    take(1, 2)
                    normalize(2)
                    take(1, 3)
                    normalize(3)
                    for u in range(2):
                        use = tQ + Q_O + u
                        dve.wait_ge(*rq.full(i, use))
                        dve.wait_ge(s_x1b, i * (tiles * NB) + (blocks + 2 * u + 2))
                        dve.tensor_tensor(y2[:, 2 * u:2 * u + 2, :], x1b[:, 2 * u:2 * u + 2, :],
                                          ps_q[:, use % 2, :].rearrange("p (t d) -> p t d", t=2), ALU.add
                                          ).then_inc(rq.drained[use % 2], 1)
                        dve.wait_ge(*rq.done(i, use))
                    layer_norm(y2, x2, s_x2)

                    use = tQ + Q_R
                    l8 = lg[:, :, 0:NE]
                    m1, m2, pick, tmp = (top[:, n, :] for n in range(4))
                    k1, k2, eq, e2 = (r8[:, n, :, :] for n in range(4))

                    def first_of(k, vals, m):
                        chain.then(dve.tensor_reduce(m, vals, AX.X, ALU.max))
                        chain.then(dve.tensor_tensor(eq, vals, bcast(m, 2, NE), ALU.is_equal))
                        chain.then(dve.tensor_tensor(eq, eq, bcast(rev[:, :], 1, NB), ALU.mult))
                        chain.then(dve.tensor_reduce(pick, eq, AX.X, ALU.max))
                        chain.then(dve.tensor_tensor(k, eq, bcast(pick, 2, NE), ALU.is_equal))

                    dve.wait_ge(*rq.full(i, use))
                    dve.tensor_copy(lg[:, :, :], ps_q[:, use % 2, 0:NB * E].rearrange("p (t e) -> p t e", t=NB)
                                    ).then_inc(rq.drained[use % 2], 1)
                    dve.wait_ge(*rq.done(i, use))
                    chain.then(dve.tensor_reduce(tmp, l8, AX.X, ALU.max))
                    chain.then(dve.tensor_tensor(e2, l8, bcast(tmp, 2, NE), ALU.subtract))
                    dve.wait_ge(s_ex, i * (tiles * 2) + (2 * j + 2))
                    first_of(k1, ex[:, :, :], m1)
                    chain.then(dve.scalar_tensor_tensor(out=e2, in0=k1, scalar=-2.0, in1=ex[:, :, :], op0=ALU.mult, op1=ALU.add))
                    first_of(k2, e2, m2)
                    chain.then(dve.tensor_tensor(k1, k1, k2, ALU.add))
                    chain.then(dve.tensor_tensor(k1, k1, ex[:, :, :], ALU.mult))
                    chain.then(dve.tensor_tensor(m1, m1, m2, ALU.add))
                    chain.then(dve.reciprocal(m1, m1))
                    chain.then(dve.tensor_tensor(cmb[:, :, 0:NE], k1, bcast(m1, 2, NE), ALU.mult))
                    chain.then(dve.tensor_scalar(cmb[:, :, NE], cmb[:, :, NE], 1.0, None, ALU.add))
                    chain.then(dve.reciprocal(cmb[:, :, NE], cmb[:, :, NE]))
                    assert chain.at == 2 * LN_STEPS + ROUTER_STEPS, chain.at

                    def hidden(e):
                        for n, (m0, m) in enumerate(IT):
                            use = tM + M_E + FIRST_UP[e] + 2 * n + 1
                            dve.wait_ge(*rm.done(i, use - 1))
                            dve.wait_ge(*rm.full(i, use))
                            dve.tensor_tensor(hT[0:m, e % 2, n, :], sil[0:m, (3 * e + n) % 2, :], ps_m[0:m, use % 4, :],
                                              ALU.mult).then_inc(rm.drained[use % 4], 1)

                    def add(e):
                        for u in range(2):
                            use = tM + M_E + FIRST_DOWN[e] + u
                            dve.wait_ge(*rm.full(i, use))
                            if e > 0:
                                dve.wait_ge(*rm.done(i, tM + M_E + FIRST_DOWN[e - 1] + u))
                            for t in (2 * u, 2 * u + 1):
                                src = x2 if e == 0 else acc
                                ins = dve.scalar_tensor_tensor(out=acc[:, t, :], in0=ps_m[:, use % 4, (t % 2) * D:(t % 2 + 1) * D],
                                                               scalar=cmb[:, t, e:e + 1], in1=src[:, t, :], op0=ALU.mult, op1=ALU.add)
                            ins.then_inc(rm.drained[use % 4], 1)
                            if e == E - 1:
                                dve.wait_ge(*rm.done(i, use))

                    for e in range(E + 1):
                        if e < E:
                            hidden(e)
                        if e > 0:
                            add(e - 1)
                    dve.wait_ge(s_out[j], i * 16 + 1)
                    layer_norm(acc, fin[:, j], s_fin)

        @block.scalar
        def _(act):
            act.wait_ge(s_w, 16 * len(small))
            act.wait_ge(s_static, 2)
            with act.Fori(0, batches) as i:
                act.wait_ge(*rq.full(i, Q_K))
                for g in range(KD):
                    ins = act.activation(kT[:, g, :], ps_q[:, 0, g * NCTX:(g + 1) * NCTX], ACT.Identity, bias=bk[:, g:g + 1])
                ins.then_inc(rq.drained[0], 1)
                for j in range(tiles):
                    tT, tQ, tM, blocks = T_N * j, Q_PREP + Q_N * j, M_N * j, j * NB

                    def take_tile(dst, use):
                        for k in range(KD):
                            act.wait_ge(*rt.full(i, tT + use + k))
                            act.copy(dst[:, k, :], ps_t[:, (use + k) % 2, :]).then_inc(rt.drained[(use + k) % 2], 1)

                    def take(u, t):
                        use = tT + T_P + 3 * t + u
                        n = min(4, KD * NCH - 4 * u)
                        act.wait_ge(*rt.full(i, use))
                        act.copy(pT[:, t % 2, 4 * u:4 * u + n, :],
                                 ps_t[:, use % 2, 0:n * P].rearrange("p (n t) -> p n t", n=n)).then_inc(rt.drained[use % 2], 1)

                    take_tile(x1T, T_X1)
                    for g in range(KD):
                        use = tQ + Q_Q + g
                        act.wait_ge(*rq.full(i, use))
                        act.activation(qT[:, g, :], ps_q[:, use % 2, :], ACT.Identity, bias=bq[:, g:g + 1]
                                       ).then_inc(rq.drained[use % 2], 1)

                    def exponential(t):
                        act.wait_ge(s_sub, i * (tiles * NB) + (blocks + t + 1))
                        act.activation(pr[:, t % 2, :, 0:FLAT],
                                       sc[:, t % 2, :, :].rearrange("p (g h) k -> p g (h k)", g=KD), ACT.Exp,
                                       scale=XSCALE).then_inc(s_exp, 1)

                    exponential(0)
                    exponential(1)
                    take(0, 0), take(2, 0)
                    exponential(2)
                    take(0, 1), take(2, 1)
                    exponential(3)
                    take(0, 2), take(2, 2)
                    take(0, 3), take(2, 3)
                    take_tile(oxT, T_OX)
                    take_tile(x2T, T_X2)
                    act.wait_ge(s_chain, i * CHAIN + (j * (CHAIN // tiles) + 2 * LN_STEPS + 2))
                    act.activation(ex[:, :, :], r8[:, 3, :, :], ACT.Exp).then_inc(s_ex, 1)
                    act.activation(cmb[:, :, NE], lg[:, :, NE], ACT.Exp, scale=-1.0).then_inc(s_ex, 1)
                    for e in range(E):
                        for n, (m0, m) in enumerate(IT):
                            use = tM + M_E + FIRST_UP[e] + 2 * n
                            act.wait_ge(*rm.full(i, use))
                            k = 3 * e + n
                            if k >= 2:
                                act.wait_ge(*rm.done(i, tM + M_E + FIRST_UP[(k - 2) // 3] + 2 * ((k - 2) % 3) + 1))
                            act.activation(sil[0:m, k % 2, :], ps_m[0:m, use % 4, :], ACT.Silu).then_inc(rm.drained[use % 4], 1)
                    act.wait_ge(s_fin, i * (tiles * NB) + (j + 1) * NB)
                    act.dma_start(out[tile_rows(i, j), :].rearrange("(t p) d -> p t d", p=P), fin[:, j, :, :]).then_inc(s_out[j], 16)
            for j in range(tiles):
                act.wait_ge(s_out[j], 16 * batches + 1)



def decoder_layer(nc, dram, out):
    y_dram = nc.dram_tensor("x_and_attention", [dram["x"].shape[0], D], F32, kind="Internal").ap()
    with ExitStack() as ctx:
        keep = {"ident": ctx.enter_context(nc.sbuf_tensor("identity", [P, P], F32)),
                "w_gate": ctx.enter_context(nc.sbuf_tensor("w_gate", [P, KD, E, I], F32)),
                "w_up": ctx.enter_context(nc.sbuf_tensor("w_up", [P, KD, E, I], F32)),
                "w_down": ctx.enter_context(nc.sbuf_tensor("w_down", [P, E, len(IT), D], F32)),
                "ffn_loaded": [ctx.enter_context(nc.semaphore(f"expert_loaded{e}")) for e in range(E)]}
        self_attention(nc, dram, keep, y_dram)
        cross_attention_and_experts(nc, dram, keep, y_dram, out)


def constants(np, n):
    inv = (1.0 / np.float32(10000.0) ** (np.arange(0, DH, 2, dtype=np.float32) / np.float32(DH))).astype(np.float32)
    angle = (np.arange(n, dtype=np.float32)[:, None] * inv[None, :]).astype(np.float32)
    cos, sin = np.cos(angle), np.sin(angle)
    key, query = np.arange(NK)[None, :], np.arange(SEG)[:, None]
    bf16 = mybir.dt.np(BF16)
    causal = np.where((key >= SEG) | (key <= query), 0.0, -1e30).astype(bf16)
    flat = np.arange(NCH * P)
    real = flat < FLAT
    head = flat.reshape(NCH, P).T[:, :, None] // NCTX
    return {
        "rope": np.stack([cos, sin, -sin], axis=1).astype(np.float32),
        "ident": np.eye(P, dtype=np.float32),
        "identb": np.eye(P, dtype=np.float32).astype(bf16),
        "causal": np.ascontiguousarray(np.broadcast_to(causal[:, None, :], (SEG, 2, NK))),
        "spread": ((flat[None, :] % NCTX == np.arange(NCTX)[:, None]) & real).astype(np.float32),
        "maskv": (head == np.arange(HX // 2)).astype(np.float32),
        "maskk": (np.arange(P)[:, None] // DX == np.arange(HX // 2)).astype(np.float32),
        "rev": np.ascontiguousarray(np.broadcast_to(np.arange(NE, 0, -1, dtype=np.float32), (P, NE))),
    }


def laid_out(np, a):
    x = a["x"]
    qkv = a["L0_attn_w_qkv"].reshape(3, 2, 8, DH // 2, 2, D)
    qk = qkv[:2].transpose(5, 0, 1, 4, 2, 3).reshape(D, 2 * H * DH)
    v = qkv[2].reshape(H * DH, D).T
    mk = a["L0_attn_pm"][0].reshape(H // 2, 2, MEM, DH // 2, 2)
    mem_k = np.zeros((2, DH, H // 2, 2, MEM), np.float32)
    for z in range(2):
        mem_k[z, :, :, z, :] = mk[:, z].transpose(3, 2, 0, 1).reshape(DH, H // 2, MEM)
    mv = a["L0_attn_pm"][1].reshape(2, 8, MEM, DH)
    mem_v = np.zeros((2, 8, MEM, 8, DH + 1), np.float32)
    for h in range(8):
        mem_v[:, h, :, h, :DH] = mv[:, h]
        mem_v[:, h, :, h, DH] = 1.0
    pos = constants(np, x.shape[1])
    rope = np.concatenate([pos.pop("rope")] * x.shape[0])
    join = lambda routed, shared: np.concatenate([routed, shared[None]])
    return {
        "x": x.reshape(-1, D), "rope": rope, **pos,
        "attn_g": a["L0_attn_g"].reshape(KD, P).T, "w_qkv": np.concatenate([qk, v], axis=1),
        "w_out": a["L0_attn_w_out"].T, "mem_k": mem_k.reshape(P, H // 2, 2, MEM), "mem_v": mem_v.reshape(2, P, 8, DH + 1),
        "ctx_t": a["ctx_768"].transpose(0, 2, 1),
        "xWq": a["L0_xattn_Wq"], "xWk": a["L0_xattn_Wk"], "xWv": a["L0_xattn_Wv"], "xWo": a["L0_xattn_Wo"],
        "xbq": a["L0_xattn_bq"].reshape(KD, P).T, "xbk": a["L0_xattn_bk"].reshape(KD, P).T,
        "xbv": a["L0_xattn_bv"], "xbo": a["L0_xattn_bo"],
        "router": np.concatenate([a["L0_ffn_gate_w"], a["L0_ffn_shared_gate_w"]]).T,
        "w_gate": join(a["L0_ffn_w_gate"], a["L0_ffn_sw_gate"]), "w_up": join(a["L0_ffn_w_up"], a["L0_ffn_sw_up"]),
        "w_down": join(a["L0_ffn_w_down"], a["L0_ffn_sw_down"]),
    }


def kernel(**inputs):
    import numpy as np
    import concourse.bacc as bacc
    from concourse.bass_utils import run_bass_kernel_spmd

    given = {k: np.asarray(v) for k, v in inputs.items()}
    arrays = {f"in_{k}": np.ascontiguousarray(v) for k, v in laid_out(np, given).items()}
    nc = bacc.Bacc("TRN2", target_bir_lowering=False, num_devices=1)
    dram = {k[3:]: nc.dram_tensor(k, v.shape, mybir.dt.from_np(v.dtype), kind="ExternalInput").ap() for k, v in arrays.items()}
    out = nc.dram_tensor("out", arrays["in_x"].shape, F32, kind="ExternalOutput").ap()
    decoder_layer(nc, dram, out)
    r = run_bass_kernel_spmd(nc, [arrays], core_ids=[0])
    return r.results[0]["out"].reshape(given["x"].shape)
```

```python
from contextlib import ExitStack

import concourse.bass as bass
from concourse import mybir

F32 = mybir.dt.float32
BF16 = mybir.dt.bfloat16
I32 = mybir.dt.int32
ALU = mybir.AluOpType
ACT = mybir.ActivationFunctionType
AX = mybir.AxisListType

P = 128
D = 256
KD = D // P
H, DH = 16, 64
SEG, MEM = 128, 16
NK = SEG + MEM
HX, DX = 16, 16
NCTX, CCTX = 77, 192
E, I = 9, 352
NE = 8
IT = [(0, 128), (128, 128), (256, 96)]
ROPE_HALF = DH // 2
SCALE = DH ** -0.5
XSCALE = DX ** -0.5
CLAMP = 10000.0
RMS_EPS = 1.1920929e-07
LN_EPS = 1e-5
TT = 512
NB = TT // P
FLAT = (HX // 2) * NCTX
NCH = -(-FLAT // P)
OG = (HX // 2) * (DX + 1)
CONTEXT = "ck . cv . cb .".split()
LAYER = ("n1s . n1r . n1n . tx . q . s0 . . s1 . e0 . a0 . w0 s2 . e1 . a1 . w1 s3 . . e2 . a2 . w2 . e3 . a3 . w3 . to . o . "
         "n2s . n2r . n2n . t2 . r . r1 . re . r2 . r3 . r4").split()
LEAD = 3
Q_COST = {"q": 2, "s": 4, "w": 1, "o": 2, "r": 1}
FIRST_UP = [0] + [8 * e - 2 for e in range(1, E)]
FIRST_DOWN = [8 * e + 12 for e in range(E - 1)] + [8 * E - 2]
CHUNKS = [0, 2, 1, 3, 4, 5]
MAGIC = float(0x5F3759DF)


class Ring:

    def __init__(self, sem, name, slots):
        self.slots = slots
        self.filled = [sem(f"{name}_filled{s}") for s in range(slots)]
        self.drained = [sem(f"{name}_drained{s}") for s in range(slots)]

    def full(self, base, k):
        return self.filled[k % self.slots], base + (k // self.slots + 1)

    def free(self, base, k):
        return self.drained[k % self.slots], base + (k // self.slots + 1)

    def done(self, base, k):
        return self.drained[k % self.slots], base + (k // self.slots + 2)

    def credit(self, eng):
        for s in self.drained:
            eng.sem_inc(s, 1)


class Chain:

    def __init__(self, sem, eng):
        self.sem, self.eng, self.at, self.base = sem, eng, 0, 0

    def start(self, base):
        self.base, self.at = base, 0

    def then(self, ins):
        self.at += 1
        ins.then_inc(self.sem, 1)
        self.eng.wait_ge(self.sem, self.base + self.at)


RSQRT_STEPS = 12


def rsqrt_steps(dve, chain, out, var, eps, tmp_a, tmp_b):
    chain.then(dve.tensor_scalar(tmp_a, var, eps, None, ALU.add))
    chain.then(dve.tensor_scalar(tmp_b.bitcast(I32), tmp_a.bitcast(I32), 1, None, ALU.logical_shift_right))
    chain.then(dve.tensor_scalar(out.bitcast(I32), tmp_b.bitcast(I32), -1.0, MAGIC, ALU.mult, ALU.add))
    for _ in range(3):
        chain.then(dve.tensor_tensor(tmp_b, out, out, ALU.mult))
        chain.then(dve.scalar_tensor_tensor(out=tmp_b, in0=tmp_b, scalar=-0.5, in1=tmp_a, op0=ALU.mult, op1=ALU.mult))
        chain.then(dve.scalar_tensor_tensor(out=out, in0=tmp_b, scalar=1.5, in1=out, op0=ALU.add, op1=ALU.mult))


def bcast(ap, axis, n):
    shape = list(ap.shape)
    return ap.unsqueeze(axis).broadcast_to(shape[:axis] + [n] + shape[axis:])


ORDER = [("x", 0), ("x", 1), ("s", 0), ("s", 1), ("p", 0), ("s", 2), ("s", 3), ("p", 1), ("t", 0), ("s", 4), ("t", 1), ("m", 0),
         ("s", 5), ("p", 2), ("a", 0), ("a", 1), ("r", 0), ("s", 6), ("t", 2), ("s", 7), ("p", 3), ("t", 3), ("m", 1),
         ("a", 2), ("r", 1), ("o", 0), ("p", 4), ("a", 3), ("r", 2), ("r", 3), ("y", 0), ("p", 5), ("o", 1), ("y", 1)]
PROJECT, ATTEND = "xpr", "stmaoy"
T_DVE = (0, 2)


def steps(kinds):
    return [s for s in ORDER if s[0] in kinds]


def uses(kinds, of):
    return {s: n for n, s in enumerate(s for s in steps(kinds) if s[0] in of)}


def self_attention(nc, dram, keep, y_dram):
    x_d, rope_d = dram["x"], dram["rope"]
    segs = x_d.shape[0] // SEG
    ident = keep["ident"]
    with ExitStack() as ctx:
        def sb(name, shape, dt=F32):
            return ctx.enter_context(nc.sbuf_tensor(name, shape, dt))

        def sem(name):
            return ctx.enter_context(nc.semaphore(name))

        wqkv = sb("w_qkv", [P, KD, 3 * H * DH])
        wo = sb("w_out", [P, H * DH // P, D])
        g = sb("rms_gain", [P, KD])
        identb = sb("identity_bf16", [P, P], BF16)
        cmask = sb("causal_mask", [P, 2, NK], BF16)
        STAT = 4
        xs = sb("x_for_stats", [P, 2, segs // STAT, D])
        ms = sb("mean_square", [P, segs])
        rstd = sb("rms_reciprocal", [P, segs])
        tmp_a = sb("rms_tmp_a", [P, segs])
        tmp_b = sb("rms_tmp_b", [P, segs])
        x = sb("x_seg", [P, 2, D])
        xr = sb("x_residual", [P, 2, D])
        rope = sb("rope_seg", [P, 2, 3, ROPE_HALF])
        rope_r = sb("rope_scaled", [P, 2, 3, ROPE_HALF])
        rms_seg = sb("rms_of_seg", [P, 2])
        xT = sb("x_transposed", [P, KD, SEG])
        rot_a = sb("rot_cos", [P, 2, 512])
        rot_b = sb("rot_sin", [P, 2, 512])
        roped = sb("roped", [P, 4, 8, DH])
        qT = sb("q_transposed", [P, 2, H // 2, SEG])
        kz = sb("k_transposed", [P, 2, H // 2, 2, NK])
        v = sb("v_and_one", [P, 2, H, DH + 1])
        vm = sb("mem_v_blocks", [P, 2, 8, DH + 1])
        prob = sb("probs", [P, H, NK])
        pm = sb("mem_probs", [P, H, MEM])
        mx = sb("score_max", [P, H])
        nm = sb("score_bias", [P, H])
        pT = sb("probs_transposed", [P, H, SEG])
        pmT = sb("mem_probs_transposed", [P, 2, SEG])
        rc = sb("sum_reciprocal", [P, H])
        o = sb("heads_out", [P, H, DH])
        oT = sb("heads_out_transposed", [P, 8, SEG])
        y = sb("y_seg", [P, 2, D])

        ps_q = ctx.enter_context(nc.psum_tensor("ps_q", [P, 2, 512], F32))
        ps_t = ctx.enter_context(nc.psum_tensor("ps_t", [P, 2, 512], F32))
        ps_s = ctx.enter_context(nc.psum_tensor("ps_s", [P, 2, 512], F32))
        ps_o = ctx.enter_context(nc.psum_tensor("ps_o", [P, 2, 512], F32))

        rt = Ring(sem, "transpose", 2)
        rq = Ring(sem, "project", 2)
        rs = Ring(sem, "score", 2)
        ro = Ring(sem, "attend", 2)
        x_in = [sem("x_in0"), sem("x_in1")]
        xr_in = [sem("x_residual_in0"), sem("x_residual_in1")]
        s_static = sem("static_ready")
        s_small = sem("small_weights_loaded")
        s_wq = [sem(f"w_qkv_loaded{n}") for n in range(6)]
        s_w = sem("w_qkv_scaled")
        s_xs = [sem("stats_x_loaded0"), sem("stats_x_loaded1")]
        s_sq = [sem("stats_even"), sem("stats_odd")]
        s_rms = sem("rms_chain")
        s_rope = sem("rope_scaled_ready")
        s_roped = sem("roped_ready")
        s_step = sem("mem_probs_waited")
        s_pace = sem("reload_waited")
        s_pm = sem("mem_probs_ready")
        s_max = sem("max_ready")
        s_bias = sem("bias_ready")
        s_recip = sem("recip_ready")
        s_store = [sem("y_stored0"), sem("y_stored1")]

        T_PER, Q_PER, S_PER, O_PER = (len(uses(PROJECT + ATTEND, of)) // 2 for of in ("xrtmo", "py", "s", "a"))
        T_FIRST, Q_FIRST = len(uses(PROJECT, "xr")) // 2, len(uses(PROJECT, "p")) // 2

        class Segment:

            def __init__(self, s, cur, turn, nturn, kinds=PROJECT + ATTEND):
                self.s, self.n, self.cur, self.nxt, self.turn, self.nturn = s, s + 1, cur, 1 - cur, turn, nturn
                self.steps, self.first = steps(kinds), False
                self.t, self.q, self.sc, self.o = s * T_PER + T_FIRST, s * Q_PER + Q_FIRST, s * S_PER, s * O_PER
                self.tu, self.qu = uses(kinds, "xrtmo"), uses(kinds, "py")

            @classmethod
            def before(cls):
                it = cls(0, 1, 0, 0, PROJECT)
                it.n, it.t, it.q, it.first = 0, 0, 0, True
                return it

        def each_segment(eng, program):
            program(Segment.before())
            with eng.Fori(0, segs // 2 - 1) as i:
                program(Segment(i * 2, 0, i, i))
                program(Segment(i * 2 + 1, 1, i, i + 1))
            last = segs // 2 - 1
            program(Segment(segs - 2, 0, last, last))
            program(Segment(segs - 1, 1, last, last, ATTEND))

        block = ctx.enter_context(nc.Block())

        @block.sync
        def _(sp):
            for ring in (rt, rq, rs, ro):
                ring.credit(sp)
            for s in (s_roped, s_store[0], s_store[1]):
                sp.sem_inc(s, 1)
            for n in range(2):
                sp.dma_start(xs[:, n, :, :], x_d[n * segs // STAT * P:(n + 1) * segs // STAT * P, :].rearrange("(t p) d -> p t d", p=P)
                             ).then_inc(s_xs[n], 16)
            small = [(g[:, :], dram["attn_g"]), (ident[:, :], dram["ident"]), (identb[:, :], dram["identb"]),
                     (cmask[:, :, :], dram["causal"]), (vm[:, 0, :, :], dram["mem_v"][0]), (vm[:, 1, :, :], dram["mem_v"][1]),
                     (kz[:, 0, :, :, SEG:NK], dram["mem_k"]), (kz[:, 1, :, :, SEG:NK], dram["mem_k"]),
                     (wo[:, :, :], dram["w_out"].rearrange("(j p) n -> p j n", p=P))]
            for dst, src in small:
                sp.dma_start(dst, src).then_inc(s_small, 16)

            def load(r, at):
                sp.dma_start(x[:, r, :], x_d[bass.ds(at, SEG), :]).then_inc(x_in[r], 16)
                sp.dma_start(rope[:, r, :, :], rope_d[bass.ds(at, SEG), :, :]).then_inc(x_in[r], 16)

            def reload(sg):
                sp.wait_ge(*rt.done(sg.t, sg.tu["x", 1]))
                sp.sem_inc(s_pace, 1)
                sp.wait_ge(s_rope, sg.n + 1)
                sp.sem_inc(s_pace, 1)
                load(sg.nxt, sg.n * SEG + 2 * SEG)

            def reload_residual(sg):
                sp.wait_ge(s_store[sg.cur], sg.turn * 16 + 17)
                sp.sem_inc(s_pace, 1)
                sp.dma_start(xr[:, sg.cur, :], x_d[bass.ds(sg.s * SEG + 2 * SEG, SEG), :]).then_inc(xr_in[sg.cur], 16)

            for r in range(2):
                load(r, r * SEG)
                sp.dma_start(xr[:, r, :], x_d[r * SEG:(r + 1) * SEG, :]).then_inc(xr_in[r], 16)
            reload(Segment.before())
            with sp.Fori(0, segs // 2 - 2) as i:
                for r in range(2):
                    sg = Segment(i * 2 + r, r, i, i + r)
                    reload(sg)
                    reload_residual(sg)
            last = segs // 2 - 2
            reload(Segment(segs - 4, 0, last, last))
            reload_residual(Segment(segs - 4, 0, last, last))
            reload_residual(Segment(segs - 3, 1, last, last + 1))

        @block.gpsimd
        def _(pool):
            pool.memset(kz[:, :, :, :, 0:SEG], 0.0).then_inc(s_static, 1)
            pool.memset(v[:, :, :, DH:DH + 1], 1.0).then_inc(s_static, 1)

            def program(sg):
                for kind, k in sg.steps:
                    if kind == "p" and k < 4:
                        pool.wait_ge(*rq.done(sg.q, sg.qu["p", k]))
                        pool.tensor_tensor(
                            roped[:, k, :, :].rearrange("p h (s j) -> p s h j", s=2),
                            rot_a[:, k % 2, :].rearrange("p (s h j) -> p s h j", s=2, h=8),
                            rot_b[:, k % 2, :].rearrange("p (s h j) -> p s h j", s=2, h=8),
                            ALU.add).then_inc(s_roped, 1)
                    if kind == "s" and k % 4 == 3:
                        for p in range(k - 3, k + 1):
                            pool.wait_ge(*rs.done(sg.sc, p))
                        pool.sem_inc(s_step, 1)
                        pool.tensor_copy(pm[:, 2 * k - 6:2 * k + 2, :], prob[:, 2 * k - 6:2 * k + 2, SEG:NK]).then_inc(s_pm, 1)

            each_segment(pool, program)

        @block.tensor
        def _(pe):
            pe.wait_ge(s_static, 2)
            pe.wait_ge(s_small, 16 * 9)

            def program(sg):
                cur, nxt, n = sg.cur, sg.nxt, sg.n
                for kind, k in sg.steps:
                    use = sg.tu.get((kind, k))
                    if kind == "x":
                        if k == 0:
                            pe.wait_ge(x_in[nxt], sg.nturn * 32 + 32)
                        pe.wait_ge(*rt.free(sg.t, use))
                        pe.transpose(ps_t[:, use % 2, 0:P], x[:, nxt, k * P:(k + 1) * P], ident[:, :]).then_inc(rt.filled[use % 2], 1)
                    if kind == "p":
                        if k == 0:
                            for h in range(KD):
                                pe.wait_ge(*rt.done(sg.t, sg.tu["x", h]))
                        if sg.first:
                            pe.wait_ge(s_w, KD * (k + 1))
                        c, slot = CHUNKS[k], sg.qu[kind, k] % 2
                        pe.wait_ge(*rq.free(sg.q, sg.qu[kind, k]))
                        for h in range(KD):
                            ins = pe.matmul(ps_q[:, slot, :], xT[:, h, :], wqkv[:, h, c * 512:(c + 1) * 512],
                                            start=(h == 0), stop=(h == KD - 1))
                        ins.then_inc(rq.filled[slot], 1)
                    if kind == "r":
                        pe.wait_ge(s_roped, n * 4 + (k + 2))
                        pe.wait_ge(*rt.free(sg.t, use))
                        for p in range(4):
                            ins = pe.transpose(ps_t[:, use % 2, p * P:(p + 1) * P], roped[:, k, 2 * p:2 * p + 2, :], ident[:, :])
                        ins.then_inc(rt.filled[use % 2], 1)
                    if kind == "s":
                        if k == 0:
                            pe.wait_ge(*rt.free(sg.t, 0))
                            pe.wait_ge(*rt.free(sg.t, 1))
                        pe.wait_ge(*rs.free(sg.sc, k))
                        pe.matmul(ps_s[:, k % 2, 0:2 * NK], qT[:, cur, k, :], kz[:, cur, k, :, :], start=True, stop=False)
                        pe.matmul(ps_s[:, k % 2, 0:2 * NK], identb[:, :], cmask[:, :, :], start=False,
                                  stop=True).then_inc(rs.filled[k % 2], 1)
                    if kind == "t":
                        pe.wait_ge(*rs.done(sg.sc, 2 * k))
                        pe.wait_ge(*rs.done(sg.sc, 2 * k + 1))
                        pe.wait_ge(*rt.free(sg.t, use))
                        for h in range(4):
                            ins = pe.transpose(ps_t[:, use % 2, h * P:(h + 1) * P], prob[:, 4 * k + h, 0:SEG], ident[:, :])
                        ins.then_inc(rt.filled[use % 2], 1)
                    if kind == "m":
                        pe.wait_ge(*rt.free(sg.t, use))
                        pe.wait_ge(s_pm, sg.s * 2 + (k + 1))
                        pe.transpose(ps_t[:, use % 2, 0:P], pm[:, 8 * k:8 * k + 8, :], ident[:, :]).then_inc(rt.filled[use % 2], 1)
                    if kind == "a":
                        pe.wait_ge(*rt.done(sg.t, sg.tu["t", k]))
                        if k % 2 == 0:
                            pe.wait_ge(*rt.done(sg.t, sg.tu["m", k // 2]))
                        if k == 0:
                            pe.wait_ge(*rq.free(sg.q, 0))
                            pe.wait_ge(*rq.free(sg.q, 1))
                        pe.wait_ge(*ro.free(sg.o, k))
                        out = ps_o[:, k % 2, 0:4 * (DH + 1)]
                        pe.matmul(out, pmT[:, k // 2, :], vm[:, k // 2, 4 * (k % 2):4 * (k % 2) + 4, :], start=True, stop=False)
                        for h in range(4):
                            ins = pe.matmul(out[:, h * (DH + 1):(h + 1) * (DH + 1)], pT[:, 4 * k + h, :],
                                            v[:, cur, 4 * k + h, :], start=False, stop=(h == 3))
                        ins.then_inc(ro.filled[k % 2], 1)
                    if kind == "o":
                        pe.wait_ge(*ro.done(sg.o, 2 * k))
                        pe.wait_ge(*ro.done(sg.o, 2 * k + 1))
                        pe.wait_ge(*rt.free(sg.t, use))
                        for j in range(4):
                            ins = pe.transpose(ps_t[:, use % 2, j * P:(j + 1) * P], o[:, 8 * k + 2 * j:8 * k + 2 * j + 2, :], ident[:, :])
                        ins.then_inc(rt.filled[use % 2], 1)
                    if kind == "y":
                        slot = sg.qu[kind, k] % 2
                        pe.wait_ge(*rt.done(sg.t, sg.tu["o", k]))
                        pe.wait_ge(*rq.free(sg.q, sg.qu[kind, k]))
                        for j in range(4):
                            ins = pe.matmul(ps_q[:, slot, 0:D], oT[:, 4 * k + j, :], wo[:, 4 * k + j, :], start=(j == 0), stop=(j == 3))
                        ins.then_inc(rq.filled[slot], 1)

            each_segment(pe, program)

        @block.vector
        def _(dve):
            dve.wait_ge(s_static, 2)
            dve.wait_ge(s_small, 16 * 9)
            chain = Chain(s_rms, dve)
            for t in range(STAT):
                dve.wait_ge(s_xs[t % 2], 16 * (t // 2 + 1))
                for n in range(0, segs // STAT, 2):
                    at = t * segs // STAT + n
                    dve.tensor_tensor_reduce(xs[:, t % 2, n, :], xs[:, t % 2, n, :], xs[:, t % 2, n, :], 1.0 / D, 0.0,
                                             ALU.mult, ALU.add, ms[:, at:at + 1]).then_inc(s_sq[0], 1)
            dve.wait_ge(s_sq[0], segs // 2)
            dve.wait_ge(s_sq[1], segs // 2)
            rsqrt_steps(dve, chain, rstd[:, :], ms[:, :], RMS_EPS, tmp_a[:, :], tmp_b[:, :])
            for n, c in enumerate(CHUNKS):
                dve.wait_ge(s_wq[n], 16)
                for k in range(KD):
                    w = wqkv[:, k, c * 512:(c + 1) * 512]
                    dve.tensor_scalar(w, w, g[:, k:k + 1], None, ALU.mult).then_inc(s_w, 1)

            def program(sg):
                cur, nxt, n = sg.cur, sg.nxt, sg.n
                for kind, k in sg.steps:
                    use = sg.tu.get((kind, k))
                    if kind == "x" and k == 0:
                        dve.wait_ge(x_in[nxt], sg.nturn * 32 + 32)
                        dve.tensor_copy(rms_seg[:, nxt:nxt + 1], rstd[:, bass.ds(n, 1)])
                        dve.tensor_scalar(rope_r[:, nxt, :, :], rope[:, nxt, :, :], rstd[:, bass.ds(n, 1)], None, ALU.mult).then_inc(s_rope, 1)
                    if kind == "p" and k < 4:
                        slot = sg.qu[kind, k] % 2
                        if k == 0:
                            dve.wait_ge(s_rope, n + 1)
                        dve.wait_ge(*rq.full(sg.q, sg.qu[kind, k]))
                        dve.wait_ge(s_roped, n * 4 + max(k, 1))
                        t = ps_q[:, slot, :].rearrange("p (s h j) -> p s h j", s=2, h=8)
                        b = rot_b[:, k % 2, :].rearrange("p (s h j) -> p s h j", s=2, h=8)
                        cos, sin, neg = (rope_r[:, nxt, m, :] for m in range(3))
                        dve.tensor_tensor(rot_a[:, k % 2, :].rearrange("p (q j) -> p q j", q=16),
                                          ps_q[:, slot, :].rearrange("p (q j) -> p q j", q=16),
                                          bcast(cos, 1, 16), ALU.mult)
                        dve.tensor_tensor(b[:, 0], t[:, 1], bcast(neg, 1, 8), ALU.mult)
                        dve.tensor_tensor(b[:, 1], t[:, 0], bcast(sin, 1, 8), ALU.mult).then_inc(rq.drained[slot], 1)
                    if kind == "r" and k % 2 == 1:
                        dve.wait_ge(*rt.full(sg.t, use))
                        for z in range(2):
                            rows = slice(64 * z, 64 * z + 64)
                            ins = dve.tensor_copy(kz[rows, nxt, 2 * (k - 1):2 * (k - 1) + 4, z, 0:SEG],
                                                  ps_t[rows, use % 2, :].rearrange("p (j t) -> p j t", j=4))
                        ins.then_inc(rt.drained[use % 2], 1)
                    if kind == "s":
                        dve.wait_ge(*rs.full(sg.sc, k))
                        dve.tensor_reduce(mx[:, 2 * k:2 * k + 2], ps_s[:, k % 2, 0:2 * NK].rearrange("p (h k) -> p h k", h=2),
                                          AX.X, ALU.max).then_inc(s_max, 1)
                        dve.wait_ge(s_max, sg.s * 8 + (k + 1))
                        dve.tensor_scalar(nm[:, 2 * k:2 * k + 2], mx[:, 2 * k:2 * k + 2], -SCALE, None, ALU.mult).then_inc(s_bias, 1)
                    if kind == "t" and k in T_DVE:
                        dve.wait_ge(*rt.full(sg.t, use))
                        dve.tensor_copy(pT[:, 4 * k:4 * k + 4, :], ps_t[:, use % 2, :].rearrange("p (h t) -> p h t", h=4)
                                        ).then_inc(rt.drained[use % 2], 1)
                    if kind == "m":
                        dve.wait_ge(*rt.full(sg.t, use))
                        dve.tensor_copy(pmT[:, k, :], ps_t[:, use % 2, 0:P]).then_inc(rt.drained[use % 2], 1)
                    if kind == "a":
                        dve.wait_ge(*ro.full(sg.o, k))
                        out = ps_o[:, k % 2, 0:4 * (DH + 1)].rearrange("p (h d) -> p h d", h=4)
                        dve.reciprocal(rc[:, 4 * k:4 * k + 4], out[:, :, DH]).then_inc(s_recip, 1)
                        dve.wait_ge(s_recip, sg.s * 4 + (k + 1))
                        dve.tensor_tensor(o[:, 4 * k:4 * k + 4, :], out[:, :, 0:DH],
                                          bcast(rc[:, 4 * k:4 * k + 4], 2, DH), ALU.mult).then_inc(ro.drained[k % 2], 1)
                    if kind == "y":
                        slot = sg.qu[kind, k] % 2
                        if k == 0:
                            dve.wait_ge(s_store[cur], sg.turn * 16 + 1)
                            dve.wait_ge(xr_in[cur], sg.turn * 16 + 16)
                        else:
                            dve.wait_ge(*rq.done(sg.q, sg.qu[kind, 0]))
                        dve.wait_ge(*rq.full(sg.q, sg.qu[kind, k]))
                        dve.tensor_tensor(y[:, cur, :], xr[:, cur, :] if k == 0 else y[:, cur, :], ps_q[:, slot, 0:D],
                                          ALU.add).then_inc(rq.drained[slot], 1)

            each_segment(dve, program)

        @block.scalar
        def _(act):
            for n, c in enumerate(CHUNKS):
                act.dma_start(wqkv[:, :, c * 512:(c + 1) * 512],
                              dram["w_qkv"].rearrange("(k p) n -> p k n", p=P)[:, :, c * 512:(c + 1) * 512]).then_inc(s_wq[n], 16)
            for t in range(STAT):
                act.wait_ge(s_xs[t % 2], 16 * (t // 2 + 1))
                for n in range(1, segs // STAT, 2):
                    at = t * segs // STAT + n
                    act.activation(xs[:, t % 2, n, :], xs[:, t % 2, n, :], ACT.Square, scale=float(D) ** -0.5,
                                   accum_out=ms[:, at:at + 1]).then_inc(s_sq[1], 1)
                if t + 2 < STAT:
                    act.wait_ge(s_sq[0], (t + 1) * segs // STAT // 2)
                    act.wait_ge(s_sq[1], (t + 1) * segs // STAT // 2)
                    at = (t + 2) * segs // STAT * P
                    act.dma_start(xs[:, t % 2, :, :], x_d[at:at + segs // STAT * P, :].rearrange("(t p) d -> p t d", p=P)
                                  ).then_inc(s_xs[t % 2], 16)
            act.wait_ge(s_rms, RSQRT_STEPS)

            def program(sg):
                cur, nxt, n = sg.cur, sg.nxt, sg.n
                for kind, k in sg.steps:
                    use = sg.tu.get((kind, k))
                    if kind == "x":
                        act.wait_ge(*rt.full(sg.t, use))
                        act.copy(xT[:, k, :], ps_t[:, use % 2, 0:P]).then_inc(rt.drained[use % 2], 1)
                    if kind == "p" and k >= 4:
                        slot = sg.qu[kind, k] % 2
                        act.wait_ge(*rq.full(sg.q, sg.qu[kind, k]))
                        act.wait_ge(s_rope, n + 1)
                        act.activation(v[:, nxt, 8 * (k - 4):8 * (k - 4) + 8, 0:DH],
                                       ps_q[:, slot, :].rearrange("p (h d) -> p h d", h=8), ACT.Copy,
                                       scale=rms_seg[:, nxt:nxt + 1]).then_inc(rq.drained[slot], 1)
                    if kind == "r" and k % 2 == 0:
                        act.wait_ge(*rt.full(sg.t, use))
                        act.copy(qT[:, nxt, 2 * k:2 * k + 4, :], ps_t[:, use % 2, :].rearrange("p (j t) -> p j t", j=4)
                                 ).then_inc(rt.drained[use % 2], 1)
                    if kind == "s":
                        act.wait_ge(s_bias, sg.s * 8 + (k + 1))
                        for h in (2 * k, 2 * k + 1):
                            ins = act.activation(prob[:, h, :], ps_s[:, k % 2, (h % 2) * NK:(h % 2 + 1) * NK], ACT.Exp,
                                                 bias=nm[:, h:h + 1], scale=SCALE)
                        ins.then_inc(rs.drained[k % 2], 1)
                    if kind == "t" and k not in T_DVE:
                        act.wait_ge(*rt.full(sg.t, use))
                        act.copy(pT[:, 4 * k:4 * k + 4, :], ps_t[:, use % 2, :].rearrange("p (h t) -> p h t", h=4)
                                 ).then_inc(rt.drained[use % 2], 1)
                    if kind == "o":
                        act.wait_ge(*rt.full(sg.t, use))
                        act.copy(oT[:, 4 * k:4 * k + 4, :], ps_t[:, use % 2, :].rearrange("p (j t) -> p j t", j=4)
                                 ).then_inc(rt.drained[use % 2], 1)
                    if kind == "y" and k == 1:
                        act.wait_ge(*rq.done(sg.q, sg.qu[kind, k]))
                        act.dma_start(y_dram[bass.ds(sg.s * SEG, SEG), :], y[:, cur, :]).then_inc(s_store[cur], 16)

            each_segment(act, program)
            for r in range(2):
                act.wait_ge(s_store[r], 16 * (segs // 2) + 1)


def cross_attention_and_experts(nc, dram, keep, y_dram, out):
    batches = dram["ctx_t"].shape[0]
    tiles = dram["x"].shape[0] // TT // batches
    ident = keep["ident"]
    with ExitStack() as ctx:
        def sb(name, shape, dt=F32):
            return ctx.enter_context(nc.sbuf_tensor(name, shape, dt))

        def sem(name):
            return ctx.enter_context(nc.semaphore(name))

        wg = sb("w_gate", [P, KD, E, I])
        wu = sb("w_up", [P, KD, E, I])
        wd = sb("w_down", [P, E, len(IT), D])
        wq = sb("xw_q", [P, KD, D])
        wk = sb("xw_k", [P, 2, D])
        wv = sb("xw_v", [P, 2, D])
        wo = sb("xw_o", [P, KD, D])
        bq = sb("x_bias_q", [P, KD])
        bk = sb("x_bias_k", [P, KD])
        bv = sb("x_bias_v", [NCTX, D])
        bo = sb("x_bias_o", [P, D])
        spread = sb("key_of_flat", [NCTX, NCH * P])
        maskv = sb("head_of_flat", [P, NCH, HX // 2])
        maskk = sb("head_of_dim", [P, HX // 2])
        rev = sb("pick_order", [P, NE])
        gw = sb("router_w", [P, KD, E])
        ctxT = sb("ctx_transposed", [P, 2, NCTX])
        kT = sb("ctx_k", [P, KD, NCTX])
        kbd = sb("ctx_k_blocks", [P, KD, HX // 2, NCTX])
        va = sb("ctx_v_and_one", [NCTX, HX, DX + 1])
        vbd = sb("ctx_v_blocks", [P, KD, NCH, OG])
        y1 = sb("y1", [P, 2, NB, D])
        x1 = sb("x1", [P, NB, D])
        x1b = sb("x1_and_bias", [P, NB, D])
        def norm_buffers(name):
            return [sb(f"{name}_{part}", shape) for part, shape in (
                ("stats", [P, NB, 6]), ("mean_var", [P, NB, 2]), ("rstd", [P, NB]), ("tmp_a", [P, NB]), ("tmp_b", [P, NB]))]

        ln_attend, ln_final = norm_buffers("ln"), norm_buffers("ln_final")
        x1T = sb("x1_transposed", [P, KD, TT])
        qT = sb("xq_transposed", [P, KD, TT])
        sc = sb("x_scores", [P, 2, HX, NCTX])
        mx = sb("x_max", [P, 2, HX])
        pr = sb("x_probs", [P, 2, KD, NCH * P])
        pT = sb("x_probs_transposed", [P, 2, KD * NCH, P])
        rc = sb("x_recip", [P, HX])
        ox = sb("x_heads", [P, NB, D])
        oxT = sb("x_heads_transposed", [P, KD, TT])
        x2 = sb("x2", [P, NB, D])
        x2T = sb("x2_transposed", [P, 2, KD, TT])
        lg = sb("logits", [P, NB, E])
        top = sb("top", [P, 4, NB])
        ex = sb("expert_exp", [P, NB, NE])
        r8 = sb("router_tmp", [P, 4, NB, NE])
        cmb = sb("combine", [P, 2, NB, E])
        sil = sb("silu_gate", [P, 2, TT])
        hT = sb("hidden", [P, 2, len(IT), TT])
        acc = sb("acc", [P, NB, D])
        fin = sb("out_tile", [P, 2, NB, D])

        ps_t = ctx.enter_context(nc.psum_tensor("ps2_t", [P, 2, 512], F32))
        ps_q = ctx.enter_context(nc.psum_tensor("ps2_q", [P, 2, 512], F32))
        ps_m = ctx.enter_context(nc.psum_tensor("ps2_m", [P, 4, 512], F32))

        T_FIRST = {"tx": 0, "a0": 2, "a1": 5, "a2": 8, "a3": 11, "to": 14, "t2": 16}
        T_N = 18
        Q_K, Q_V, Q_VB, Q_PREP = 0, 1, 2, 6
        Q_FIRST, Q_N = {}, 0
        for step in LAYER:
            if step in ("q", "o", "r") or step[0] in "sw":
                Q_FIRST[step] = Q_N
                Q_N += Q_COST[step[0]]
        M_N = 8 * E
        rt = Ring(sem, "x_transpose", 2)
        rq = Ring(sem, "x_project", 2)
        rm = Ring(sem, "x_matrix", 4)
        T_TURNS, Q_TURNS, M_TURNS = T_N * tiles // 2, (Q_PREP + Q_N * tiles) // 2, M_N * tiles // 4
        s_w = sem("x_weights_loaded")
        s_ffn = [sem(f"expert_loaded{e}") for e in range(E)]
        s_ctx = sem("ctx_loaded")
        s_static = sem("x_static_ready")
        s_y1 = [sem("y1_loaded0"), sem("y1_loaded1")]
        s_kbd = sem("ctx_k_blocks_ready")
        s_chain = sem("attention_chain")
        s_final = sem("final_norm_chain")
        s_step = sem("stats_waited")
        s_x1 = sem("x1_ready")
        s_x1b = sem("x1_and_bias_ready")
        s_max = sem("x_max_ready")
        s_sub = sem("x_shifted")
        s_exp = sem("x_exp_ready")
        s_recip = sem("x_recip_ready")
        s_x2 = sem("x2_ready")
        s_ex = sem("router_exp_ready")
        s_fin = sem("out_ready")
        s_out = [sem("out_stored0"), sem("out_stored1")]
        LN_STEPS = 2 * NB + RSQRT_STEPS
        ROUTER_STEPS = 20
        CHAIN = 2 * LN_STEPS + ROUTER_STEPS
        block = ctx.enter_context(nc.Block())

        class Tile:

            def __init__(self, i, off, j):
                self.i, self.off, self.j = i, off, j
                self.blocks, self.n = self.before(NB), self.before(1)

            def batches(self, per):
                return self.i * per + self.off * per

            def before(self, per):
                return self.i * (per * tiles) + (self.off * tiles + self.j) * per

            def rows(self):
                return bass.ds(self.before(TT), TT)

        class Stage:

            def __init__(self, attend, experts, following):
                self.attend, self.experts, self.following = attend, experts, following

            def steps(self):
                work = (CONTEXT if self.attend.j == 0 else []) + LAYER if self.attend else []
                pieces = []
                if self.experts:
                    for e in range(E + 1):
                        pieces += [("up", e, n) for n in range(len(IT)) if e < E]
                        pieces += [("down", e - 1, u) for u in range(2) if e > 0]
                    pieces, work = pieces[LEAD:], pieces[:LEAD] + work
                for step in work:
                    if step != ".":
                        yield step
                    elif pieces:
                        yield pieces.pop(0)
                yield from pieces
                if self.experts:
                    yield from ("fs", "fr", "fn")

        def each_stage(eng, program):
            program(Stage(Tile(0, 0, 0), None, Tile(0, 0, 1)))
            with eng.Fori(0, batches - 1) as i:
                program(Stage(Tile(i, 0, 1), Tile(i, 0, 0), Tile(i, 1, 0)))
                program(Stage(Tile(i, 1, 0), Tile(i, 0, 1), Tile(i, 1, 1)))
            last = batches - 1
            program(Stage(Tile(last, 0, 1), Tile(last, 0, 0), None))
            program(Stage(None, Tile(last, 0, 1), None))

        small = [(wq[:, :, :], dram["xWq"].rearrange("(k p) n -> p k n", p=P)),
                 (wk[:, 0, :], dram["xWk"][0:P, :]), (wk[0:CCTX - P, 1, :], dram["xWk"][P:CCTX, :]),
                 (wv[:, 0, :], dram["xWv"][0:P, :]), (wv[0:CCTX - P, 1, :], dram["xWv"][P:CCTX, :]),
                 (wo[:, :, :], dram["xWo"].rearrange("(k p) n -> p k n", p=P)),
                 (bq[:, :], dram["xbq"]), (bk[:, :], dram["xbk"]),
                 (bv[:, :], dram["xbv"].partition_broadcast(NCTX)), (bo[:, :], dram["xbo"].partition_broadcast(P)),
                 (spread[:, :], dram["spread"]), (maskv[:, :, :], dram["maskv"]), (maskk[:, :], dram["maskk"]),
                 (rev[:, :], dram["rev"]), (gw[:, :, :], dram["router"].rearrange("(k p) e -> p k e", p=P))]

        @block.sync
        def _(sp):
            for ring in (rt, rq, rm):
                ring.credit(sp)
            for s in (s_x1, s_x2, s_exp, s_out[0], s_out[1]):
                sp.sem_inc(s, 1)

            def load(a):
                if a.j == 0:
                    ctx_t = dram["ctx_t"][bass.ds(a.batches(1), 1), :, :].rearrange("b c k -> (b c) k")
                    sp.dma_start(ctxT[:, 0, :], ctx_t[0:P, :]).then_inc(s_ctx, 16)
                    sp.dma_start(ctxT[0:CCTX - P, 1, :], ctx_t[P:CCTX, :]).then_inc(s_ctx, 16)
                sp.dma_start(y1[:, a.j, :, :], y_dram[a.rows(), :].rearrange("(t p) d -> p t d", p=P)).then_inc(s_y1[a.j], 16)

            for dst, src in small[:4]:
                sp.dma_start(dst, src).then_inc(s_w, 16)
            load(Tile(0, 0, 0))
            for dst, src in small[4:]:
                sp.dma_start(dst, src).then_inc(s_w, 16)

            def program(stage):
                a, f = stage.attend, stage.experts
                if stage.following:
                    sp.wait_ge(s_x2, a.blocks + 1)
                    load(stage.following)
                if f:
                    sp.wait_ge(s_fin, f.blocks + NB)
                    sp.dma_start(out[f.rows(), :].rearrange("(t p) d -> p t d", p=P), fin[:, f.j, :, :]).then_inc(s_out[f.j], 16)

            each_stage(sp, program)
            for j in range(tiles):
                sp.wait_ge(s_out[j], 16 * batches + 1)

        @block.gpsimd
        def _(pool):
            pool.memset(va[:, :, DX:DX + 1], 1.0).then_inc(s_static, 1)
            pool.memset(pr[:, :, :, FLAT:NCH * P], 0.0).then_inc(s_static, 1)
            for e in range(E):
                for dst, name in ((wg, "w_gate"), (wu, "w_up")):
                    pool.dma_start(dst[:, :, e, :], dram[name][e].rearrange("(k p) m -> p k m", p=P)).then_inc(s_ffn[e], 16)
                pool.dma_start(wd[:, e, 0:2, :], dram["w_down"][e, 0:2 * P, :].rearrange("(n p) d -> p n d", p=P)).then_inc(s_ffn[e], 16)
                pool.dma_start(wd[0:I - 2 * P, e, 2, :], dram["w_down"][e, 2 * P:I, :]).then_inc(s_ffn[e], 16)
            pool.wait_ge(s_w, 16 * len(small))

            def program(stage):
                a = stage.attend
                for step in stage.steps():
                    if step == "n1n":
                        for t in range(NB):
                            pool.wait_ge(s_x1, a.blocks + (t + 2))
                            pool.tensor_tensor(x1b[:, t, :], x1[:, t, :], bo[:, :], ALU.add).then_inc(s_x1b, 1)
                    elif step[0] == "s":
                        t = int(step[1])
                        pool.wait_ge(s_max, a.blocks + (t + 1))
                        pool.tensor_tensor(sc[:, t % 2, :, :], sc[:, t % 2, :, :], bcast(mx[:, t % 2, :], 2, NCTX),
                                           ALU.subtract).then_inc(s_sub, 1)

            each_stage(pool, program)

        @block.tensor
        def _(pe):
            pe.wait_ge(s_w, 16 * len(small))
            pe.wait_ge(s_static, 2)
            rows = [P, CCTX - P]

            def program(stage):
                a, f = stage.attend, stage.experts
                if a:
                    ip, it = a.batches(Q_TURNS), a.before(T_N // 2)
                    tQ = Q_PREP + Q_N * a.j
                if f:
                    im = f.before(M_N // 4)

                def turn(src, use, ready):
                    for k in range(KD):
                        pe.wait_ge(*rt.free(it, use + k))
                        for t in range(NB):
                            if k == 0:
                                pe.wait_ge(*ready(t))
                            ins = pe.transpose(ps_t[:, (use + k) % 2, t * P:(t + 1) * P],
                                               src[:, t, k * P:(k + 1) * P], ident[:, :])
                        ins.then_inc(rt.filled[(use + k) % 2], 1)

                def turned(use):
                    for k in range(KD):
                        pe.wait_ge(*rt.done(it, use + k))

                def context_keys():
                    pe.wait_ge(s_ctx, a.batches(32) + 32)
                    pe.wait_ge(*rq.free(ip, Q_K))
                    for g in range(KD):
                        for k in range(2):
                            ins = pe.matmul(ps_q[:, 0, g * NCTX:(g + 1) * NCTX], wk[0:rows[k], k, g * P:(g + 1) * P],
                                            ctxT[0:rows[k], k, :], start=(k == 0), stop=(k == 1))
                    ins.then_inc(rq.filled[0], 1)

                def context_values():
                    pe.wait_ge(*rq.free(ip, Q_V))
                    for k in range(2):
                        ins = pe.matmul(ps_q[0:NCTX, 1, 0:D], ctxT[0:rows[k], k, :], wv[0:rows[k], k, :],
                                        start=(k == 0), stop=(k == 1))
                    ins.then_inc(rq.filled[1], 1)

                def value_blocks():
                    pe.wait_ge(*rq.done(ip, Q_V))
                    for u in range(4):
                        pe.wait_ge(*rq.free(ip, Q_VB + u))
                        for n in range(3 * u, min(3 * u + 3, KD * NCH)):
                            g, c = n // NCH, n % NCH
                            ins = pe.matmul(ps_q[:, u % 2, (n % 3) * OG:(n % 3 + 1) * OG], spread[:, c * P:(c + 1) * P],
                                            va[:, g * 8:g * 8 + 8, :], start=True, stop=True)
                        ins.then_inc(rq.filled[u % 2], 1)

                def queries():
                    turned(T_FIRST["tx"])
                    for g in range(KD):
                        use = tQ + Q_FIRST["q"] + g
                        pe.wait_ge(*rq.free(ip, use))
                        for k in range(KD):
                            ins = pe.matmul(ps_q[:, use % 2, :], wq[:, k, g * P:(g + 1) * P], x1T[:, k, :],
                                            start=(k == 0), stop=(k == KD - 1))
                        ins.then_inc(rq.filled[use % 2], 1)

                def scores(t):
                    if t == 0:
                        for g in range(KD):
                            pe.wait_ge(*rq.done(ip, tQ + Q_FIRST["q"] + g))
                        pe.wait_ge(s_kbd, a.batches(KD) + KD)
                    for u in range(4):
                        use = tQ + Q_FIRST[f"s{t}"] + u
                        pe.wait_ge(*rq.free(ip, use))
                        pe.matmul(ps_q[:, use % 2, 0:4 * NCTX], qT[:, u // 2, t * P:(t + 1) * P],
                                  kbd[:, u // 2, 4 * (u % 2):4 * (u % 2) + 4, :], start=True,
                                  stop=True).then_inc(rq.filled[use % 2], 1)

                def probs_transposed(t):
                    pe.wait_ge(s_exp, a.blocks + (t + 2))
                    for u in range(3):
                        use = T_FIRST[f"a{t}"] + u
                        pe.wait_ge(*rt.free(it, use))
                        for n in range(4 * u, min(4 * u + 4, KD * NCH)):
                            g, c = n // NCH, n % NCH
                            ins = pe.transpose(ps_t[:, use % 2, (n % 4) * P:(n % 4 + 1) * P],
                                               pr[:, t % 2, g, c * P:(c + 1) * P], ident[:, :])
                        ins.then_inc(rt.filled[use % 2], 1)

                def weigh(t):
                    if t == 0 and a.j == 0:
                        for u in range(4):
                            pe.wait_ge(*rq.done(ip, Q_VB + u))
                    for u in range(3):
                        pe.wait_ge(*rt.done(it, T_FIRST[f"a{t}"] + u))
                    use = tQ + Q_FIRST[f"w{t}"]
                    pe.wait_ge(*rq.free(ip, use))
                    for g in range(KD):
                        for c in range(NCH):
                            ins = pe.matmul(ps_q[:, use % 2, g * OG:(g + 1) * OG], pT[:, t % 2, g * NCH + c, :],
                                            vbd[:, g, c, :], start=(c == 0), stop=(c == NCH - 1))
                    ins.then_inc(rq.filled[use % 2], 1)

                def output_projection():
                    turned(T_FIRST["to"])
                    for u in range(2):
                        use = tQ + Q_FIRST["o"] + u
                        pe.wait_ge(*rq.free(ip, use))
                        for t in (2 * u, 2 * u + 1):
                            for k in range(KD):
                                ins = pe.matmul(ps_q[:, use % 2, (t % 2) * D:(t % 2 + 1) * D],
                                                oxT[:, k, t * P:(t + 1) * P], wo[:, k, :], start=(k == 0), stop=(k == KD - 1))
                        ins.then_inc(rq.filled[use % 2], 1)

                def router():
                    turned(T_FIRST["t2"])
                    use = tQ + Q_FIRST["r"]
                    pe.wait_ge(*rq.free(ip, use))
                    for t in range(NB):
                        for k in range(KD):
                            ins = pe.matmul(ps_q[:, use % 2, t * E:(t + 1) * E], x2T[:, a.j, k, t * P:(t + 1) * P],
                                            gw[:, k, :], start=(k == 0), stop=(k == KD - 1))
                    ins.then_inc(rq.filled[use % 2], 1)

                def up(e, n):
                    if f.j == 0 and n == 0:
                        pe.wait_ge(s_ffn[e], 16 * 4)
                    m0, m = IT[n]
                    for w, mat in enumerate((wg, wu)):
                        use = FIRST_UP[e] + 2 * n + w
                        pe.wait_ge(*rm.free(im, use))
                        for k in range(KD):
                            ins = pe.matmul(ps_m[0:m, use % 4, :], mat[:, k, e, m0:m0 + m], x2T[:, f.j, k, :],
                                            start=(k == 0), stop=(k == KD - 1))
                        ins.then_inc(rm.filled[use % 4], 1)

                def down(e, u):
                    if u == 0:
                        for n in range(len(IT)):
                            pe.wait_ge(*rm.done(im, FIRST_UP[e] + 2 * n + 1))
                    use = FIRST_DOWN[e] + u
                    pe.wait_ge(*rm.free(im, use))
                    for t in (2 * u, 2 * u + 1):
                        for n, (m0, m) in enumerate(IT):
                            ins = pe.matmul(ps_m[:, use % 4, (t % 2) * D:(t % 2 + 1) * D],
                                            hT[0:m, e % 2, n, t * P:(t + 1) * P], wd[0:m, e, n, :],
                                            start=(n == 0), stop=(n == len(IT) - 1))
                    ins.then_inc(rm.filled[use % 4], 1)

                for step in stage.steps():
                    if step == "ck":
                        context_keys()
                    elif step == "cv":
                        context_values()
                    elif step == "cb":
                        value_blocks()
                    elif step == "tx":
                        turn(x1, T_FIRST["tx"], lambda t: (s_x1, a.blocks + (t + 2)))
                    elif step == "q":
                        queries()
                    elif step[0] == "s":
                        scores(int(step[1]))
                    elif step[0] == "a":
                        probs_transposed(int(step[1]))
                    elif step[0] == "w":
                        weigh(int(step[1]))
                    elif step == "to":
                        turn(ox, T_FIRST["to"], lambda t: rq.done(ip, tQ + Q_FIRST[f"w{t}"]))
                    elif step == "o":
                        output_projection()
                    elif step == "t2":
                        turn(x2, T_FIRST["t2"], lambda t: (s_x2, a.blocks + (t + 2)))
                    elif step == "r":
                        router()
                    elif step[0] == "up":
                        up(*step[1:])
                    elif step[0] == "down":
                        down(*step[1:])

            each_stage(pe, program)

        @block.vector
        def _(dve):
            def norm_stats(buffers, chain, src):
                st, ag = buffers[:2]
                for t in range(NB):
                    chain.at += 1
                    dve.bn_stats(st[:, t, :], src[:, t, :]).then_inc(chain.sem, 1)
                dve.wait_ge(chain.sem, chain.base + chain.at)
                dve.sem_inc(s_step, 1)
                for t in range(NB):
                    chain.at += 1
                    dve.bn_aggr(ag[:, t, :], st[:, t, :]).then_inc(chain.sem, 1)

            def norm_root(buffers, chain):
                _, ag, rstd, ta, tb = buffers
                dve.wait_ge(chain.sem, chain.base + chain.at)
                rsqrt_steps(dve, chain, rstd[:, :], ag[:, :, 1], LN_EPS, ta[:, :], tb[:, :])

            def norm_scale(buffers, src, dst, signal):
                _, ag, rstd, _, _ = buffers
                for t in range(NB):
                    dve.tensor_scalar(dst[:, t, :], src[:, t, :], ag[:, t, 0:1], rstd[:, t:t + 1], ALU.subtract,
                                      ALU.mult).then_inc(signal, 1)

            dve.wait_ge(s_w, 16 * len(small))
            dve.wait_ge(s_static, 2)

            def program(stage):
                a, f = stage.attend, stage.experts
                chain, final = Chain(s_chain, dve), Chain(s_final, dve)
                if a:
                    ip, it = a.batches(Q_TURNS), a.before(T_N // 2)
                    tQ = Q_PREP + Q_N * a.j
                    chain.start(a.before(CHAIN))
                if f:
                    im = f.before(M_N // 4)
                    final.start(f.before(LN_STEPS))

                def context_values():
                    dve.wait_ge(*rq.full(ip, Q_V))
                    dve.tensor_tensor(va[:, :, 0:DX], ps_q[0:NCTX, 1, 0:D].rearrange("p (h d) -> p h d", h=HX),
                                      bv[:, :].rearrange("p (h d) -> p h d", h=HX), ALU.add).then_inc(rq.drained[1], 1)
                    for g in range(KD):
                        dve.wait_ge(*rq.done(ip, Q_K))
                        dve.tensor_tensor(kbd[:, g, :, :], bcast(kT[:, g, :], 1, HX // 2), bcast(maskk[:, :], 2, NCTX),
                                          ALU.mult).then_inc(s_kbd, 1)

                def value_blocks():
                    for u in range(4):
                        dve.wait_ge(*rq.full(ip, Q_VB + u))
                        for n in range(3 * u, min(3 * u + 3, KD * NCH)):
                            g, c = n // NCH, n % NCH
                            ins = dve.tensor_tensor(vbd[:, g, c, :].rearrange("p (h d) -> p h d", h=HX // 2),
                                                    ps_q[:, u % 2, (n % 3) * OG:(n % 3 + 1) * OG].rearrange("p (h d) -> p h d", h=HX // 2),
                                                    bcast(maskv[:, c, :], 2, DX + 1), ALU.mult)
                        ins.then_inc(rq.drained[u % 2], 1)

                def maxima(t):
                    dve.wait_ge(s_exp, a.blocks + (t if t >= 2 else 1))
                    for u in range(4):
                        use = tQ + Q_FIRST[f"s{t}"] + u
                        dve.wait_ge(*rq.full(ip, use))
                        dve.tensor_scalar(sc[:, t % 2, 4 * u:4 * u + 4, :],
                                          ps_q[:, use % 2, 0:4 * NCTX].rearrange("p (h k) -> p h k", h=4),
                                          CLAMP / XSCALE, -CLAMP / XSCALE, ALU.min, ALU.max).then_inc(rq.drained[use % 2], 1)
                    for u in (2, 3):
                        dve.wait_ge(*rq.done(ip, tQ + Q_FIRST[f"s{t}"] + u))
                    dve.tensor_reduce(mx[:, t % 2, :], sc[:, t % 2, :, :], AX.X, ALU.max).then_inc(s_max, 1)

                def normalize(t):
                    use = tQ + Q_FIRST[f"w{t}"]
                    dve.wait_ge(*rq.full(ip, use))
                    o = ps_q[:, use % 2, 0:KD * OG].rearrange("p (h d) -> p h d", h=HX)
                    dve.reciprocal(rc[:, :], o[:, :, DX]).then_inc(s_recip, 1)
                    dve.wait_ge(s_recip, a.blocks + (t + 1))
                    dve.tensor_tensor(ox[:, t, :].rearrange("p (h d) -> p h d", h=HX), o[:, :, 0:DX],
                                      bcast(rc[:, :], 2, DX), ALU.mult).then_inc(rq.drained[use % 2], 1)

                def take(u, t):
                    use = T_FIRST[f"a{t}"] + u
                    n = min(4, KD * NCH - 4 * u)
                    dve.wait_ge(*rt.full(it, use))
                    dve.tensor_copy(pT[:, t % 2, 4 * u:4 * u + n, :],
                                    ps_t[:, use % 2, 0:n * P].rearrange("p (n t) -> p n t", n=n)
                                    ).then_inc(rt.drained[use % 2], 1)

                def residual():
                    for u in range(2):
                        use = tQ + Q_FIRST["o"] + u
                        dve.wait_ge(*rq.full(ip, use))
                        dve.wait_ge(s_x1b, a.blocks + (2 * u + 2))
                        dve.tensor_tensor(y1[:, a.j, 2 * u:2 * u + 2, :], x1b[:, 2 * u:2 * u + 2, :],
                                          ps_q[:, use % 2, :].rearrange("p (t d) -> p t d", t=2), ALU.add
                                          ).then_inc(rq.drained[use % 2], 1)

                l8 = lg[:, :, 0:NE]
                m1, m2, pick, tmp = (top[:, n, :] for n in range(4))
                k1, k2, eq, e2 = (r8[:, n, :, :] for n in range(4))

                def first_of(k, vals, m):
                    chain.then(dve.tensor_reduce(m, vals, AX.X, ALU.max))
                    chain.then(dve.tensor_tensor(eq, vals, bcast(m, 2, NE), ALU.is_equal))
                    chain.then(dve.tensor_tensor(eq, eq, bcast(rev[:, :], 1, NB), ALU.mult))
                    chain.then(dve.tensor_reduce(pick, eq, AX.X, ALU.max))
                    chain.then(dve.tensor_tensor(k, eq, bcast(pick, 2, NE), ALU.is_equal))

                def router_shift():
                    use = tQ + Q_FIRST["r"]
                    dve.wait_ge(*rq.full(ip, use))
                    dve.tensor_copy(lg[:, :, :], ps_q[:, use % 2, 0:NB * E].rearrange("p (t e) -> p t e", t=NB)
                                    ).then_inc(rq.drained[use % 2], 1)
                    dve.wait_ge(*rq.done(ip, use))
                    chain.then(dve.tensor_reduce(tmp, l8, AX.X, ALU.max))
                    chain.then(dve.tensor_tensor(e2, l8, bcast(tmp, 2, NE), ALU.subtract))

                def router_second():
                    chain.then(dve.scalar_tensor_tensor(out=e2, in0=k1, scalar=-2.0, in1=ex[:, :, :], op0=ALU.mult, op1=ALU.add))
                    first_of(k2, e2, m2)

                def router_weights():
                    c = cmb[:, a.j]
                    chain.then(dve.tensor_tensor(k1, k1, k2, ALU.add))
                    chain.then(dve.tensor_tensor(k1, k1, ex[:, :, :], ALU.mult))
                    chain.then(dve.tensor_tensor(m1, m1, m2, ALU.add))
                    chain.then(dve.reciprocal(m1, m1))
                    chain.then(dve.tensor_tensor(c[:, :, 0:NE], k1, bcast(m1, 2, NE), ALU.mult))
                    chain.then(dve.tensor_scalar(c[:, :, NE], c[:, :, NE], 1.0, None, ALU.add))
                    chain.then(dve.reciprocal(c[:, :, NE], c[:, :, NE]))
                    assert chain.at == CHAIN, chain.at

                def hidden(e, n):
                    m = IT[n][1]
                    use = FIRST_UP[e] + 2 * n + 1
                    dve.wait_ge(*rm.done(im, use - 1))
                    dve.wait_ge(*rm.full(im, use))
                    dve.tensor_tensor(hT[0:m, e % 2, n, :], sil[0:m, (3 * e + n) % 2, :], ps_m[0:m, use % 4, :],
                                      ALU.mult).then_inc(rm.drained[use % 4], 1)

                def add(e, u):
                    use = FIRST_DOWN[e] + u
                    dve.wait_ge(*rm.full(im, use))
                    if e > 0:
                        dve.wait_ge(*rm.done(im, FIRST_DOWN[e - 1] + u))
                    for t in (2 * u, 2 * u + 1):
                        src = x2 if e == 0 else acc
                        ins = dve.scalar_tensor_tensor(out=acc[:, t, :], in0=ps_m[:, use % 4, (t % 2) * D:(t % 2 + 1) * D],
                                                       scalar=cmb[:, f.j, t, e:e + 1], in1=src[:, t, :], op0=ALU.mult, op1=ALU.add)
                    ins.then_inc(rm.drained[use % 4], 1)

                for step in stage.steps():
                    if step == "cv":
                        context_values()
                    elif step == "cb":
                        value_blocks()
                    elif step == "n1s":
                        dve.wait_ge(s_y1[a.j], a.batches(16) + 16)
                        norm_stats(ln_attend, chain, y1[:, a.j])
                    elif step == "n1r" or step == "n2r":
                        norm_root(ln_attend, chain)
                    elif step == "n1n":
                        norm_scale(ln_attend, y1[:, a.j], x1, s_x1)
                    elif step[0] == "s":
                        maxima(int(step[1]))
                    elif step[0] == "a":
                        take(1, int(step[1]))
                    elif step[0] == "w":
                        normalize(int(step[1]))
                    elif step == "o":
                        residual()
                    elif step == "n2s":
                        for u in range(2):
                            dve.wait_ge(*rq.done(ip, tQ + Q_FIRST["o"] + u))
                        norm_stats(ln_attend, chain, y1[:, a.j])
                    elif step == "n2n":
                        norm_scale(ln_attend, y1[:, a.j], x2, s_x2)
                    elif step == "r1":
                        router_shift()
                    elif step == "r2":
                        dve.wait_ge(s_ex, a.before(2) + 2)
                        first_of(k1, ex[:, :, :], m1)
                    elif step == "r3":
                        router_second()
                    elif step == "r4":
                        router_weights()
                    elif step[0] == "up":
                        hidden(*step[1:])
                    elif step[0] == "down":
                        add(*step[1:])
                    elif step == "fs":
                        for u in range(2):
                            dve.wait_ge(*rm.done(im, FIRST_DOWN[E - 1] + u))
                        norm_stats(ln_final, final, acc)
                    elif step == "fr":
                        norm_root(ln_final, final)
                    elif step == "fn":
                        dve.wait_ge(s_out[f.j], f.batches(16) + 1)
                        norm_scale(ln_final, acc, fin[:, f.j], s_fin)

            each_stage(dve, program)

        @block.scalar
        def _(act):
            act.wait_ge(s_w, 16 * len(small))
            act.wait_ge(s_static, 2)

            def program(stage):
                a, f = stage.attend, stage.experts
                if a:
                    ip, it = a.batches(Q_TURNS), a.before(T_N // 2)
                    tQ = Q_PREP + Q_N * a.j
                if f:
                    im = f.before(M_N // 4)

                def context_keys():
                    act.wait_ge(*rq.full(ip, Q_K))
                    for g in range(KD):
                        ins = act.activation(kT[:, g, :], ps_q[:, 0, g * NCTX:(g + 1) * NCTX], ACT.Identity, bias=bk[:, g:g + 1])
                    ins.then_inc(rq.drained[0], 1)

                def take_tile(dst, use):
                    for k in range(KD):
                        act.wait_ge(*rt.full(it, use + k))
                        act.copy(dst[:, k, :], ps_t[:, (use + k) % 2, :]).then_inc(rt.drained[(use + k) % 2], 1)

                def queries():
                    for g in range(KD):
                        use = tQ + Q_FIRST["q"] + g
                        act.wait_ge(*rq.full(ip, use))
                        act.activation(qT[:, g, :], ps_q[:, use % 2, :], ACT.Identity, bias=bq[:, g:g + 1]
                                       ).then_inc(rq.drained[use % 2], 1)

                def take(u, t):
                    use = T_FIRST[f"a{t}"] + u
                    n = min(4, KD * NCH - 4 * u)
                    act.wait_ge(*rt.full(it, use))
                    act.copy(pT[:, t % 2, 4 * u:4 * u + n, :],
                             ps_t[:, use % 2, 0:n * P].rearrange("p (n t) -> p n t", n=n)).then_inc(rt.drained[use % 2], 1)

                def exponential(t):
                    act.wait_ge(s_sub, a.blocks + (t + 1))
                    act.activation(pr[:, t % 2, :, 0:FLAT],
                                   sc[:, t % 2, :, :].rearrange("p (g h) k -> p g (h k)", g=KD), ACT.Exp,
                                   scale=XSCALE).then_inc(s_exp, 1)

                def router_exponentials():
                    act.wait_ge(s_chain, a.before(CHAIN) + (2 * LN_STEPS + 2))
                    act.activation(ex[:, :, :], r8[:, 3, :, :], ACT.Exp).then_inc(s_ex, 1)
                    act.activation(cmb[:, a.j, :, NE], lg[:, :, NE], ACT.Exp, scale=-1.0).then_inc(s_ex, 1)

                def silu(e, n):
                    m = IT[n][1]
                    use = FIRST_UP[e] + 2 * n
                    act.wait_ge(*rm.full(im, use))
                    k = 3 * e + n
                    if k >= 2:
                        act.wait_ge(*rm.done(im, FIRST_UP[(k - 2) // 3] + 2 * ((k - 2) % 3) + 1))
                    act.activation(sil[0:m, k % 2, :], ps_m[0:m, use % 4, :], ACT.Silu).then_inc(rm.drained[use % 4], 1)

                for step in stage.steps():
                    if step == "ck":
                        context_keys()
                    elif step == "tx":
                        take_tile(x1T, T_FIRST["tx"])
                    elif step == "q":
                        queries()
                    elif step[0] == "e":
                        exponential(int(step[1]))
                    elif step[0] == "a":
                        take(0, int(step[1])), take(2, int(step[1]))
                    elif step == "to":
                        take_tile(oxT, T_FIRST["to"])
                    elif step == "t2":
                        take_tile(x2T[:, a.j], T_FIRST["t2"])
                    elif step == "re":
                        router_exponentials()
                    elif step[0] == "up":
                        silu(*step[1:])

            each_stage(act, program)


def decoder_layer(nc, dram, out):
    y_dram = nc.dram_tensor("x_and_attention", [dram["x"].shape[0], D], F32, kind="Internal").ap()
    with ExitStack() as ctx:
        keep = {"ident": ctx.enter_context(nc.sbuf_tensor("identity", [P, P], F32))}
        self_attention(nc, dram, keep, y_dram)
        cross_attention_and_experts(nc, dram, keep, y_dram, out)


def constants(np, n):
    inv = (1.0 / np.float32(10000.0) ** (np.arange(0, DH, 2, dtype=np.float32) / np.float32(DH))).astype(np.float32)
    angle = (np.arange(n, dtype=np.float32)[:, None] * inv[None, :]).astype(np.float32)
    cos, sin = np.cos(angle), np.sin(angle)
    key, query = np.arange(NK)[None, :], np.arange(SEG)[:, None]
    bf16 = mybir.dt.np(BF16)
    causal = np.where((key >= SEG) | (key <= query), 0.0, -1e30).astype(bf16)
    flat = np.arange(NCH * P)
    real = flat < FLAT
    head = flat.reshape(NCH, P).T[:, :, None] // NCTX
    return {
        "rope": np.stack([cos, sin, -sin], axis=1).astype(np.float32),
        "ident": np.eye(P, dtype=np.float32),
        "identb": np.eye(P, dtype=np.float32).astype(bf16),
        "causal": np.ascontiguousarray(np.broadcast_to(causal[:, None, :], (SEG, 2, NK))),
        "spread": ((flat[None, :] % NCTX == np.arange(NCTX)[:, None]) & real).astype(np.float32),
        "maskv": (head == np.arange(HX // 2)).astype(np.float32),
        "maskk": (np.arange(P)[:, None] // DX == np.arange(HX // 2)).astype(np.float32),
        "rev": np.ascontiguousarray(np.broadcast_to(np.arange(NE, 0, -1, dtype=np.float32), (P, NE))),
    }


def laid_out(np, a):
    x = a["x"]
    qkv = a["L0_attn_w_qkv"].reshape(3, 2, 8, DH // 2, 2, D)
    qk = qkv[:2].transpose(5, 0, 1, 4, 2, 3).reshape(D, 2 * H * DH)
    v = qkv[2].reshape(H * DH, D).T
    mk = a["L0_attn_pm"][0].reshape(H // 2, 2, MEM, DH // 2, 2)
    mem_k = np.zeros((2, DH, H // 2, 2, MEM), np.float32)
    for z in range(2):
        mem_k[z, :, :, z, :] = mk[:, z].transpose(3, 2, 0, 1).reshape(DH, H // 2, MEM)
    mv = a["L0_attn_pm"][1].reshape(2, 8, MEM, DH)
    mem_v = np.zeros((2, 8, MEM, 8, DH + 1), np.float32)
    for h in range(8):
        mem_v[:, h, :, h, :DH] = mv[:, h]
        mem_v[:, h, :, h, DH] = 1.0
    pos = constants(np, x.shape[1])
    rope = np.concatenate([pos.pop("rope")] * x.shape[0])
    join = lambda routed, shared: np.concatenate([routed, shared[None]])
    return {
        "x": x.reshape(-1, D), "rope": rope, **pos,
        "attn_g": a["L0_attn_g"].reshape(KD, P).T, "w_qkv": np.concatenate([qk, v], axis=1),
        "w_out": a["L0_attn_w_out"].T, "mem_k": mem_k.reshape(P, H // 2, 2, MEM), "mem_v": mem_v.reshape(2, P, 8, DH + 1),
        "ctx_t": a["ctx_768"].transpose(0, 2, 1),
        "xWq": a["L0_xattn_Wq"], "xWk": a["L0_xattn_Wk"], "xWv": a["L0_xattn_Wv"], "xWo": a["L0_xattn_Wo"],
        "xbq": a["L0_xattn_bq"].reshape(KD, P).T, "xbk": a["L0_xattn_bk"].reshape(KD, P).T,
        "xbv": a["L0_xattn_bv"], "xbo": a["L0_xattn_bo"],
        "router": np.concatenate([a["L0_ffn_gate_w"], a["L0_ffn_shared_gate_w"]]).T,
        "w_gate": join(a["L0_ffn_w_gate"], a["L0_ffn_sw_gate"]), "w_up": join(a["L0_ffn_w_up"], a["L0_ffn_sw_up"]),
        "w_down": join(a["L0_ffn_w_down"], a["L0_ffn_sw_down"]),
    }


def kernel(**inputs):
    import numpy as np
    import concourse.bacc as bacc
    from concourse.bass_utils import run_bass_kernel_spmd

    given = {k: np.asarray(v) for k, v in inputs.items()}
    arrays = {f"in_{k}": np.ascontiguousarray(v) for k, v in laid_out(np, given).items()}
    nc = bacc.Bacc("TRN2", target_bir_lowering=False, num_devices=1)
    dram = {k[3:]: nc.dram_tensor(k, v.shape, mybir.dt.from_np(v.dtype), kind="ExternalInput").ap() for k, v in arrays.items()}
    out = nc.dram_tensor("out", arrays["in_x"].shape, F32, kind="ExternalOutput").ap()
    decoder_layer(nc, dram, out)
    r = run_bass_kernel_spmd(nc, [arrays], core_ids=[0])
    return r.results[0]["out"].reshape(given["x"].shape)
```

```python
from contextlib import ExitStack

import concourse.bass as bass
from concourse import mybir

F32 = mybir.dt.float32
BF16 = mybir.dt.bfloat16
F16 = mybir.dt.float16
I32 = mybir.dt.int32
ALU = mybir.AluOpType
ACT = mybir.ActivationFunctionType
AX = mybir.AxisListType

P = 128
D = 256
KD = D // P
H, DH = 16, 64
SEG, MEM = 128, 16
NK = SEG + MEM
HX, DX = 16, 16
NCTX, CCTX = 77, 192
E, I = 9, 352
NE = 8
IT = [(0, 128), (128, 128), (256, 96)]
ROPE_HALF = DH // 2
SCALE = DH ** -0.5
XSCALE = DX ** -0.5
CLAMP = 10000.0
RMS_EPS = 1.1920929e-07
LN_EPS = 1e-5
TT = 512
NB = TT // P
FLAT = (HX // 2) * NCTX
NCH = -(-FLAT // P)
OG = (HX // 2) * (DX + 1)
IP = 384
BB = 8
NQ = 2 * BB + NE - 1

CONTEXT = "ck . cv . cb .".split()
LAYER = ("n1s . n1r . n1n . tx . q . s0 . . s1 . e0 . a0 . w0 s2 . e1 . a1 . w1 s3 . . e2 . a2 . w2 . e3 . a3 . w3 . to . o . "
         "n2s . n2r . n2n .").split()
SECOND = ("n1s . n1r . n1n . tx . <r1 . q . <re s0 . <r2 . s1 . <r3 e0 . <r4 a0 . w0 s2 . e1 . a1 . w1 s3 . . e2 . a2 . w2 . e3 . a3 . w3 . "
          "to . o . n2s . n2r . n2n .").split()
LAST_ROUTER = ("t2 + r + c c r1 + c c re + r2 r3 r4 k0 + kp k1 scatter c c c + + c c c c + + c c c + + +").split()
LATER = 7
CUT_LATER = 6
GATHERS = 4
Q_COST = {"q": 2, "s": 4, "w": 1, "o": 2, "r": 1}


def shared_steps():
    pieces = []
    for j in range(2):
        pieces += [[("up", j, 1), ("hi", j, 0)], [("up", j, 2), ("hi", j, 1)], [("hi", j, 2)]]
        pieces += ([[("up", 1, 0)]] if j == 0 else []) + [[("down", j, 0)], [("down", j, 1)]]
    return [[("up", 0, 0)]] + pieces


def routed_steps():
    pieces = [[("load", 0), ("load", 1)], [("load", 2), ("turn", 0)]]
    for q in range(NQ + 2):
        if q < NQ:
            pieces += [([("turn", q + 1)] if q + 1 < NQ else []) + [("both", q)]]
        pieces += [([("load", q + 3)] if q + 3 < NQ else []) + ([("flip", q - 1)] if 0 < q <= NQ else [])
                   + ([("back", q - 2)] if q >= 2 else [])]
    pieces[-1] += [("gather", t) for t in range(GATHERS)]
    return pieces


def combine_steps():
    pieces = []
    for t in range(BB):
        pieces += [[("add", t)] + ([("gather", t + GATHERS)] if t + GATHERS < BB else [])]
        if t % NB == NB - 1:
            pieces += [[("fs", t // NB)], [("fr", t // NB)], [("fn", t // NB)]]
    return pieces


M_USE, M_N = {}, 0
_shared = shared_steps()
_order = [step for mark in LAST_ROUTER for step in ([("rank",)] if mark == "kp" else _shared.pop(0) if mark == "+" else [])]
for _step in _order + sum(routed_steps(), []):
    if _step[0] in ("up", "down", "rank", "turn", "both", "flip", "back"):
        M_USE[_step] = M_N
        M_N += 2 if _step[0] in ("up", "both") else 1
CHUNKS = [0, 2, 1, 3, 4, 5]
MAGIC = float(0x5F3759DF)
PASSES = [(0, 0), (0, 1), (1, 0)]
W_SCALE, X_SCALE, H_SCALE = 64.0, 64.0, 32.0


class Ring:

    def __init__(self, sem, name, slots):
        self.slots = slots
        self.filled = [sem(f"{name}_filled{s}") for s in range(slots)]
        self.drained = [sem(f"{name}_drained{s}") for s in range(slots)]

    def full(self, base, k):
        return self.filled[k % self.slots], base + (k // self.slots + 1)

    def free(self, base, k):
        return self.drained[k % self.slots], base + (k // self.slots + 1)

    def done(self, base, k):
        return self.drained[k % self.slots], base + (k // self.slots + 2)

    def credit(self, eng):
        for s in self.drained:
            eng.sem_inc(s, 1)


class Chain:

    def __init__(self, sem, eng):
        self.sem, self.eng, self.at, self.base = sem, eng, 0, 0

    def start(self, base):
        self.base, self.at = base, 0

    def then(self, ins):
        self.at += 1
        ins.then_inc(self.sem, 1)
        self.eng.wait_ge(self.sem, self.base + self.at)


RSQRT_STEPS = 12


def rsqrt_steps(dve, chain, out, var, eps, tmp_a, tmp_b):
    chain.then(dve.tensor_scalar(tmp_a, var, eps, None, ALU.add))
    chain.then(dve.tensor_scalar(tmp_b.bitcast(I32), tmp_a.bitcast(I32), 1, None, ALU.logical_shift_right))
    chain.then(dve.tensor_scalar(out.bitcast(I32), tmp_b.bitcast(I32), -1.0, MAGIC, ALU.mult, ALU.add))
    for _ in range(3):
        chain.then(dve.tensor_tensor(tmp_b, out, out, ALU.mult))
        chain.then(dve.scalar_tensor_tensor(out=tmp_b, in0=tmp_b, scalar=-0.5, in1=tmp_a, op0=ALU.mult, op1=ALU.mult))
        chain.then(dve.scalar_tensor_tensor(out=out, in0=tmp_b, scalar=1.5, in1=out, op0=ALU.add, op1=ALU.mult))


def bcast(ap, axis, n):
    shape = list(ap.shape)
    return ap.unsqueeze(axis).broadcast_to(shape[:axis] + [n] + shape[axis:])


ORDER = [("x", 0), ("x", 1), ("s", 0), ("s", 1), ("p", 0), ("s", 2), ("s", 3), ("p", 1), ("t", 0), ("s", 4), ("t", 1), ("m", 0),
         ("s", 5), ("p", 2), ("a", 0), ("a", 1), ("r", 0), ("s", 6), ("t", 2), ("s", 7), ("p", 3), ("t", 3), ("m", 1),
         ("a", 2), ("r", 1), ("o", 0), ("p", 4), ("a", 3), ("r", 2), ("r", 3), ("y", 0), ("o", 1), ("p", 5), ("y", 1)]
PROJECT, ATTEND = "xpr", "stmaoy"
QKV_X, QKV_W, OUT_X, OUT_W = 16.0, 64.0, 16.0, 64.0


def steps(kinds):
    return [s for s in ORDER if s[0] in kinds]


def uses(kinds, of):
    return {s: n for n, s in enumerate(s for s in steps(kinds) if s[0] in of)}


def self_attention(nc, dram, keep, y_dram):
    x_d, rope_d = dram["x"], dram["rope"]
    segs = x_d.shape[0] // SEG
    ident = keep["ident"]
    with ExitStack() as ctx:
        def sb(name, shape, dt=F32):
            return ctx.enter_context(nc.sbuf_tensor(name, shape, dt))

        def sem(name):
            return ctx.enter_context(nc.semaphore(name))

        wqkv32 = sb("w_qkv", [P, KD, 3 * H * DH])
        wo32 = sb("w_out", [P, H * DH // P, D])
        wqkv = sb("w_qkv_split", [P, 2, KD, 3 * H * DH], F16)
        wo = sb("w_out_split", [P, 2, H * DH // P, D], F16)
        gs = sb("rms_gain_scaled", [P, KD])
        g = sb("rms_gain", [P, KD])
        identb = sb("identity_bf16", [P, P], BF16)
        cmask = sb("causal_mask", [P, 2, NK], BF16)
        STAT = 4
        xs = sb("x_for_stats", [P, 2, segs // STAT, D])
        ms = sb("mean_square", [P, segs])
        rstd = sb("rms_reciprocal", [P, segs])
        tmp_a = sb("rms_tmp_a", [P, segs])
        tmp_b = sb("rms_tmp_b", [P, segs])
        x = sb("x_seg", [P, 2, D])
        xr = sb("x_residual", [P, 2, D])
        rope = sb("rope_seg", [P, 2, 3, ROPE_HALF])
        rope_r = sb("rope_scaled", [P, 2, 3, ROPE_HALF])
        rms_seg = sb("rms_of_seg", [P, 2])
        xT = sb("x_transposed_split", [P, 2, KD, SEG], F16)
        rot_a = sb("rot_cos", [P, 2, 512])
        rot_b = sb("rot_sin", [P, 2, 512])
        roped = sb("roped", [P, 4, 8, DH])
        qT = sb("q_transposed", [P, 2, H // 2, SEG])
        kz = sb("k_transposed", [P, 2, H // 2, 2, NK])
        v = sb("v_and_one", [P, 2, H, DH + 1])
        vm = sb("mem_v_blocks", [P, 2, 8, DH + 1])
        prob = sb("probs", [P, H, NK])
        pm = sb("mem_probs", [P, H, MEM])
        mx = sb("score_max", [P, H])
        nm = sb("score_bias", [P, H])
        pT = sb("probs_transposed", [P, H, SEG])
        pmT = sb("mem_probs_transposed", [P, 2, SEG])
        rc = sb("sum_reciprocal", [P, H])
        o = sb("heads_out", [P, H, DH])
        oT = sb("heads_out_transposed_split", [P, 2, 8, SEG], F16)
        y = sb("y_seg", [P, 2, D])

        ps_q = ctx.enter_context(nc.psum_tensor("ps_q", [P, 2, 512], F32))
        ps_t = ctx.enter_context(nc.psum_tensor("ps_t", [P, 2, 512], F32))
        ps_s = ctx.enter_context(nc.psum_tensor("ps_s", [P, 2, 512], F32))
        ps_o = ctx.enter_context(nc.psum_tensor("ps_o", [P, 2, 512], F32))

        rt = Ring(sem, "transpose", 2)
        rq = Ring(sem, "project", 2)
        rs = Ring(sem, "score", 2)
        ro = Ring(sem, "attend", 2)
        x_in = [sem("x_in0"), sem("x_in1")]
        xr_in = [sem("x_residual_in0"), sem("x_residual_in1")]
        s_static = sem("static_ready")
        s_g = sem("gain_loaded")
        s_small = sem("small_weights_loaded")
        s_wq = [sem(f"w_qkv_loaded{n}") for n in range(6)]
        s_gs = sem("gain_scaled")
        s_whi = sem("w_hi_ready")
        s_w = sem("w_lo_ready")
        s_xhi = sem("x_hi_ready")
        s_ohi = sem("heads_out_hi_ready")
        s_xs = [sem("stats_x_loaded0"), sem("stats_x_loaded1")]
        s_sq = [sem("stats_even"), sem("stats_odd")]
        s_rms = sem("rms_chain")
        s_rope = sem("rope_scaled_ready")
        s_roped = sem("roped_ready")
        s_step = sem("mem_probs_waited")
        s_pace = sem("reload_waited")
        s_pm = sem("mem_probs_ready")
        s_max = sem("max_ready")
        s_bias = sem("bias_ready")
        s_recip = sem("recip_ready")
        s_store = [sem("y_stored0"), sem("y_stored1")]

        T_PER, Q_PER, S_PER, O_PER = (len(uses(PROJECT + ATTEND, of)) // 2 for of in ("xrtmo", "py", "s", "a"))
        T_FIRST, Q_FIRST = len(uses(PROJECT, "xr")) // 2, len(uses(PROJECT, "p")) // 2

        class Segment:

            def __init__(self, s, cur, turn, nturn, kinds=PROJECT + ATTEND):
                self.s, self.n, self.cur, self.nxt, self.turn, self.nturn = s, s + 1, cur, 1 - cur, turn, nturn
                self.steps, self.first = steps(kinds), False
                self.t, self.q, self.sc, self.o = s * T_PER + T_FIRST, s * Q_PER + Q_FIRST, s * S_PER, s * O_PER
                self.tu, self.qu = uses(kinds, "xrtmo"), uses(kinds, "py")

            @classmethod
            def before(cls):
                it = cls(0, 1, 0, 0, PROJECT)
                it.n, it.t, it.q, it.first = 0, 0, 0, True
                return it

        def each_segment(eng, program, after_first=None):
            program(Segment.before())
            if after_first:
                after_first()
            with eng.Fori(0, segs // 2 - 1) as i:
                program(Segment(i * 2, 0, i, i))
                program(Segment(i * 2 + 1, 1, i, i + 1))
            last = segs // 2 - 1
            program(Segment(segs - 2, 0, last, last))
            program(Segment(segs - 1, 1, last, last, ATTEND))

        block = ctx.enter_context(nc.Block())

        @block.sync
        def _(sp):
            for ring in (rt, rq, rs, ro):
                ring.credit(sp)
            for s in (s_roped, s_store[0], s_store[1]):
                sp.sem_inc(s, 1)
            sp.dma_start(g[:, :], dram["attn_g"]).then_inc(s_g, 16)
            for n in range(2):
                sp.dma_start(xs[:, n, :, :], x_d[n * segs // STAT * P:(n + 1) * segs // STAT * P, :].rearrange("(t p) d -> p t d", p=P)
                             ).then_inc(s_xs[n], 16)
            small = [(ident[:, :], dram["ident"]), (identb[:, :], dram["identb"]),
                     (cmask[:, :, :], dram["causal"]), (vm[:, 0, :, :], dram["mem_v"][0]), (vm[:, 1, :, :], dram["mem_v"][1]),
                     (kz[:, 0, :, :, SEG:NK], dram["mem_k"]), (kz[:, 1, :, :, SEG:NK], dram["mem_k"]),
                     (wo32[:, :, :], dram["w_out"].rearrange("(j p) n -> p j n", p=P))]
            for dst, src in small:
                sp.dma_start(dst, src).then_inc(s_small, 16)

            def load(r, at):
                sp.dma_start(x[:, r, :], x_d[bass.ds(at, SEG), :]).then_inc(x_in[r], 16)
                sp.dma_start(rope[:, r, :, :], rope_d[bass.ds(at, SEG), :, :]).then_inc(x_in[r], 16)

            def reload(sg):
                sp.wait_ge(*rt.done(sg.t, sg.tu["x", 1]))
                sp.sem_inc(s_pace, 1)
                sp.wait_ge(s_rope, sg.n + 1)
                sp.sem_inc(s_pace, 1)
                load(sg.nxt, sg.n * SEG + 2 * SEG)

            def reload_residual(sg):
                sp.wait_ge(s_store[sg.cur], sg.turn * 16 + 17)
                sp.sem_inc(s_pace, 1)
                sp.dma_start(xr[:, sg.cur, :], x_d[bass.ds(sg.s * SEG + 2 * SEG, SEG), :]).then_inc(xr_in[sg.cur], 16)

            for r in range(2):
                load(r, r * SEG)
                sp.dma_start(xr[:, r, :], x_d[r * SEG:(r + 1) * SEG, :]).then_inc(xr_in[r], 16)

            def store(sg):
                sp.wait_ge(*rq.done(sg.q, sg.qu["y", 1]))
                sp.sem_inc(s_pace, 1)
                sp.dma_start(y_dram[bass.ds(sg.s * SEG, SEG), :], y[:, sg.cur, :]).then_inc(s_store[sg.cur], 16)

            for dst, src in keep["small_from"]:
                sp.dma_start(dst, src).then_inc(keep["small_loaded"], 16)
            reload(Segment.before())
            with sp.Fori(0, segs // 2 - 2) as i:
                for r in range(2):
                    sg = Segment(i * 2 + r, r, i, i + r)
                    reload(sg)
                    store(sg)
                    reload_residual(sg)
            last = segs // 2 - 2
            sg = Segment(segs - 4, 0, last, last)
            reload(sg)
            store(sg)
            reload_residual(sg)
            sg = Segment(segs - 3, 1, last, last + 1)
            store(sg)
            reload_residual(sg)
            store(Segment(segs - 2, 0, last + 1, last + 1))
            store(Segment(segs - 1, 1, last + 1, last + 1, ATTEND))
            for r in range(2):
                sp.wait_ge(s_store[r], 16 * (segs // 2) + 1)

        @block.gpsimd
        def _(pool):
            pool.memset(kz[:, :, :, :, 0:SEG], 0.0).then_inc(s_static, 1)
            pool.memset(v[:, :, :, DH:DH + 1], 1.0).then_inc(s_static, 1)

            def program(sg):
                for kind, k in sg.steps:
                    if kind == "p" and k < 4:
                        pool.wait_ge(*rq.done(sg.q, sg.qu["p", k]))
                        pool.tensor_tensor(
                            roped[:, k, :, :].rearrange("p h (s j) -> p s h j", s=2),
                            rot_a[:, k % 2, :].rearrange("p (s h j) -> p s h j", s=2, h=8),
                            rot_b[:, k % 2, :].rearrange("p (s h j) -> p s h j", s=2, h=8),
                            ALU.add).then_inc(s_roped, 1)
                    if kind == "s" and k % 4 == 3:
                        for p in range(k - 3, k + 1):
                            pool.wait_ge(*rs.done(sg.sc, p))
                        pool.sem_inc(s_step, 1)
                        pool.tensor_copy(pm[:, 2 * k - 6:2 * k + 2, :], prob[:, 2 * k - 6:2 * k + 2, SEG:NK]).then_inc(s_pm, 1)

            each_segment(pool, program)

        @block.tensor
        def _(pe):
            pe.wait_ge(s_static, 2)
            pe.wait_ge(s_small, 16 * 8)

            def program(sg):
                cur, nxt, n = sg.cur, sg.nxt, sg.n
                for kind, k in sg.steps:
                    use = sg.tu.get((kind, k))
                    if kind == "x":
                        if k == 0:
                            pe.wait_ge(x_in[nxt], sg.nturn * 32 + 32)
                        pe.wait_ge(*rt.free(sg.t, use))
                        pe.transpose(ps_t[:, use % 2, 0:P], x[:, nxt, k * P:(k + 1) * P], ident[:, :]).then_inc(rt.filled[use % 2], 1)
                    if kind == "p":
                        if k == 0:
                            for h in range(KD):
                                pe.wait_ge(*rt.done(sg.t, sg.tu["x", h]))
                        if sg.first:
                            pe.wait_ge(s_w, k + 1)
                        c, slot = CHUNKS[k], sg.qu[kind, k] % 2
                        pe.wait_ge(*rq.free(sg.q, sg.qu[kind, k]))
                        for h in range(KD):
                            for z, (zx, zw) in enumerate(PASSES):
                                ins = pe.matmul(ps_q[:, slot, :], xT[:, zx, h, :], wqkv[:, zw, h, c * 512:(c + 1) * 512],
                                                start=(h == 0 and z == 0), stop=(h == KD - 1 and z == 2))
                        ins.then_inc(rq.filled[slot], 1)
                    if kind == "r":
                        pe.wait_ge(s_roped, n * 4 + (k + 2))
                        pe.wait_ge(*rt.free(sg.t, use))
                        for p in range(4):
                            ins = pe.transpose(ps_t[:, use % 2, p * P:(p + 1) * P], roped[:, k, 2 * p:2 * p + 2, :], ident[:, :])
                        ins.then_inc(rt.filled[use % 2], 1)
                    if kind == "s":
                        if k == 0:
                            pe.wait_ge(*rt.free(sg.t, 0))
                            pe.wait_ge(*rt.free(sg.t, 1))
                        pe.wait_ge(*rs.free(sg.sc, k))
                        pe.matmul(ps_s[:, k % 2, 0:2 * NK], qT[:, cur, k, :], kz[:, cur, k, :, :], start=True, stop=False)
                        pe.matmul(ps_s[:, k % 2, 0:2 * NK], identb[:, :], cmask[:, :, :], start=False,
                                  stop=True).then_inc(rs.filled[k % 2], 1)
                    if kind == "t":
                        pe.wait_ge(*rs.done(sg.sc, 2 * k))
                        pe.wait_ge(*rs.done(sg.sc, 2 * k + 1))
                        pe.wait_ge(*rt.free(sg.t, use))
                        for h in range(4):
                            ins = pe.transpose(ps_t[:, use % 2, h * P:(h + 1) * P], prob[:, 4 * k + h, 0:SEG], ident[:, :])
                        ins.then_inc(rt.filled[use % 2], 1)
                    if kind == "m":
                        pe.wait_ge(*rt.free(sg.t, use))
                        pe.wait_ge(s_pm, sg.s * 2 + (k + 1))
                        pe.transpose(ps_t[:, use % 2, 0:P], pm[:, 8 * k:8 * k + 8, :], ident[:, :]).then_inc(rt.filled[use % 2], 1)
                    if kind == "a":
                        pe.wait_ge(*rt.done(sg.t, sg.tu["t", k]))
                        if k % 2 == 0:
                            pe.wait_ge(*rt.done(sg.t, sg.tu["m", k // 2]))
                        if k == 0:
                            pe.wait_ge(*rq.free(sg.q, 0))
                            pe.wait_ge(*rq.free(sg.q, 1))
                        pe.wait_ge(*ro.free(sg.o, k))
                        out = ps_o[:, k % 2, 0:4 * (DH + 1)]
                        pe.matmul(out, pmT[:, k // 2, :], vm[:, k // 2, 4 * (k % 2):4 * (k % 2) + 4, :], start=True, stop=False)
                        for h in range(4):
                            ins = pe.matmul(out[:, h * (DH + 1):(h + 1) * (DH + 1)], pT[:, 4 * k + h, :],
                                            v[:, cur, 4 * k + h, :], start=False, stop=(h == 3))
                        ins.then_inc(ro.filled[k % 2], 1)
                    if kind == "o":
                        pe.wait_ge(*ro.done(sg.o, 2 * k))
                        pe.wait_ge(*ro.done(sg.o, 2 * k + 1))
                        pe.wait_ge(*rt.free(sg.t, use))
                        for j in range(4):
                            ins = pe.transpose(ps_t[:, use % 2, j * P:(j + 1) * P], o[:, 8 * k + 2 * j:8 * k + 2 * j + 2, :], ident[:, :])
                        ins.then_inc(rt.filled[use % 2], 1)
                    if kind == "y":
                        slot = sg.qu[kind, k] % 2
                        pe.wait_ge(s_w, 7)
                        pe.wait_ge(*rt.done(sg.t, sg.tu["o", k]))
                        pe.wait_ge(*rq.free(sg.q, sg.qu[kind, k]))
                        for j in range(4):
                            for z, (zo, zw) in enumerate(PASSES):
                                ins = pe.matmul(ps_q[:, slot, 0:D], oT[:, zo, 4 * k + j, :], wo[:, zw, 4 * k + j, :],
                                                start=(j == 0 and z == 0), stop=(j == 3 and z == 2))
                        ins.then_inc(rq.filled[slot], 1)

            each_segment(pe, program)

        @block.vector
        def _(dve):
            chain = Chain(s_rms, dve)
            dve.wait_ge(s_g, 16)
            dve.tensor_scalar(gs[:, :], g[:, :], QKV_W, None, ALU.mult).then_inc(s_gs, 1)
            def squares(t):
                dve.wait_ge(s_xs[t % 2], 16 * (t // 2 + 1))
                for n in range(0, segs // STAT, 2):
                    at = t * segs // STAT + n
                    dve.tensor_tensor_reduce(xs[:, t % 2, n, :], xs[:, t % 2, n, :], xs[:, t % 2, n, :], 1.0 / D, 0.0,
                                             ALU.mult, ALU.add, ms[:, at:at + 1]).then_inc(s_sq[0], 1)

            squares(0)
            squares(1)
            for n, c in enumerate(CHUNKS):
                dve.wait_ge(s_whi, n + 1)
                for k in range(KD):
                    cols = slice(c * 512, (c + 1) * 512)
                    ins = dve.scalar_tensor_tensor(out=wqkv[:, 1, k, cols], in0=wqkv32[:, k, cols], scalar=gs[:, k:k + 1],
                                                   in1=wqkv[:, 0, k, cols], op0=ALU.mult, op1=ALU.subtract)
                ins.then_inc(s_w, 1)
            squares(2)
            squares(3)
            dve.wait_ge(s_sq[0], segs // 2)
            dve.wait_ge(s_sq[1], segs // 2)
            rsqrt_steps(dve, chain, rstd[:, :], ms[:, :], RMS_EPS, tmp_a[:, :], tmp_b[:, :])
            chain.then(dve.tensor_scalar(rstd[:, :], rstd[:, :], 1.0 / (QKV_X * QKV_W), None, ALU.mult))
            dve.wait_ge(s_static, 2)
            dve.wait_ge(s_small, 16 * 8)

            def w_out_lo():
                dve.wait_ge(s_whi, len(CHUNKS) + 1)
                dve.scalar_tensor_tensor(out=wo[:, 1], in0=wo32[:, :, :], scalar=OUT_W, in1=wo[:, 0],
                                         op0=ALU.mult, op1=ALU.subtract).then_inc(s_w, 1)

            def program(sg):
                cur, nxt, n = sg.cur, sg.nxt, sg.n
                for kind, k in sg.steps:
                    use = sg.tu.get((kind, k))
                    if kind == "x" and k == 0:
                        dve.wait_ge(x_in[nxt], sg.nturn * 32 + 32)
                        dve.tensor_copy(rms_seg[:, nxt:nxt + 1], rstd[:, bass.ds(n, 1)])
                        dve.tensor_scalar(rope_r[:, nxt, :, :], rope[:, nxt, :, :], rstd[:, bass.ds(n, 1)], None, ALU.mult).then_inc(s_rope, 1)
                    if kind == "x":
                        dve.wait_ge(s_xhi, n * KD + (k + 1))
                        dve.scalar_tensor_tensor(out=xT[:, 1, k, :], in0=ps_t[:, use % 2, 0:P], scalar=QKV_X, in1=xT[:, 0, k, :],
                                                 op0=ALU.mult, op1=ALU.subtract).then_inc(rt.drained[use % 2], 1)
                    if kind == "o":
                        dve.wait_ge(s_ohi, sg.s * 2 + (k + 1))
                        dve.scalar_tensor_tensor(out=oT[:, 1, 4 * k:4 * k + 4, :], in0=ps_t[:, use % 2, :].rearrange("p (j t) -> p j t", j=4),
                                                 scalar=OUT_X, in1=oT[:, 0, 4 * k:4 * k + 4, :], op0=ALU.mult, op1=ALU.subtract
                                                 ).then_inc(rt.drained[use % 2], 1)
                    if kind == "p" and k < 4:
                        slot = sg.qu[kind, k] % 2
                        if k == 0:
                            dve.wait_ge(s_rope, n + 1)
                        dve.wait_ge(*rq.full(sg.q, sg.qu[kind, k]))
                        dve.wait_ge(s_roped, n * 4 + max(k, 1))
                        t = ps_q[:, slot, :].rearrange("p (s h j) -> p s h j", s=2, h=8)
                        b = rot_b[:, k % 2, :].rearrange("p (s h j) -> p s h j", s=2, h=8)
                        cos, sin, neg = (rope_r[:, nxt, m, :] for m in range(3))
                        dve.tensor_tensor(rot_a[:, k % 2, :].rearrange("p (q j) -> p q j", q=16),
                                          ps_q[:, slot, :].rearrange("p (q j) -> p q j", q=16),
                                          bcast(cos, 1, 16), ALU.mult)
                        dve.tensor_tensor(b[:, 0], t[:, 1], bcast(neg, 1, 8), ALU.mult)
                        dve.tensor_tensor(b[:, 1], t[:, 0], bcast(sin, 1, 8), ALU.mult).then_inc(rq.drained[slot], 1)
                    if kind == "r" and k % 2 == 1:
                        dve.wait_ge(*rt.full(sg.t, use))
                        for z in range(2):
                            rows = slice(64 * z, 64 * z + 64)
                            ins = dve.tensor_copy(kz[rows, nxt, 2 * (k - 1):2 * (k - 1) + 4, z, 0:SEG],
                                                  ps_t[rows, use % 2, :].rearrange("p (j t) -> p j t", j=4))
                        ins.then_inc(rt.drained[use % 2], 1)
                    if kind == "s":
                        dve.wait_ge(*rs.full(sg.sc, k))
                        dve.tensor_reduce(mx[:, 2 * k:2 * k + 2], ps_s[:, k % 2, 0:2 * NK].rearrange("p (h k) -> p h k", h=2),
                                          AX.X, ALU.max).then_inc(s_max, 1)
                        dve.wait_ge(s_max, sg.s * 8 + (k + 1))
                        dve.tensor_scalar(nm[:, 2 * k:2 * k + 2], mx[:, 2 * k:2 * k + 2], -SCALE, None, ALU.mult).then_inc(s_bias, 1)
                    if kind == "a":
                        dve.wait_ge(*ro.full(sg.o, k))
                        out = ps_o[:, k % 2, 0:4 * (DH + 1)].rearrange("p (h d) -> p h d", h=4)
                        dve.reciprocal(rc[:, 4 * k:4 * k + 4], out[:, :, DH]).then_inc(s_recip, 1)
                        dve.wait_ge(s_recip, sg.s * 4 + (k + 1))
                        dve.tensor_tensor(o[:, 4 * k:4 * k + 4, :], out[:, :, 0:DH],
                                          bcast(rc[:, 4 * k:4 * k + 4], 2, DH), ALU.mult).then_inc(ro.drained[k % 2], 1)
                    if kind == "y":
                        slot = sg.qu[kind, k] % 2
                        if k == 0:
                            dve.wait_ge(s_store[cur], sg.turn * 16 + 1)
                            dve.wait_ge(xr_in[cur], sg.turn * 16 + 16)
                        else:
                            dve.wait_ge(*rq.done(sg.q, sg.qu[kind, 0]))
                        dve.wait_ge(*rq.full(sg.q, sg.qu[kind, k]))
                        dve.scalar_tensor_tensor(out=y[:, cur, :], in0=ps_q[:, slot, 0:D], scalar=1.0 / (OUT_X * OUT_W),
                                                 in1=xr[:, cur, :] if k == 0 else y[:, cur, :], op0=ALU.mult, op1=ALU.add
                                                 ).then_inc(rq.drained[slot], 1)

            each_segment(dve, program, w_out_lo)

        @block.scalar
        def _(act):
            for n, c in enumerate(CHUNKS):
                act.dma_start(wqkv32[:, :, c * 512:(c + 1) * 512],
                              dram["w_qkv"].rearrange("(k p) n -> p k n", p=P)[:, :, c * 512:(c + 1) * 512]).then_inc(s_wq[n], 16)
            def squares(t):
                act.wait_ge(s_xs[t % 2], 16 * (t // 2 + 1))
                for n in range(1, segs // STAT, 2):
                    at = t * segs // STAT + n
                    act.activation(xs[:, t % 2, n, :], xs[:, t % 2, n, :], ACT.Square, scale=float(D) ** -0.5,
                                   accum_out=ms[:, at:at + 1]).then_inc(s_sq[1], 1)

            def next_part(t):
                act.wait_ge(s_sq[0], (t + 1) * segs // STAT // 2)
                act.wait_ge(s_sq[1], (t + 1) * segs // STAT // 2)
                at = (t + 2) * segs // STAT * P
                act.dma_start(xs[:, t % 2, :, :], x_d[at:at + segs // STAT * P, :].rearrange("(t p) d -> p t d", p=P)
                              ).then_inc(s_xs[t % 2], 16)

            squares(0)
            next_part(0)
            squares(1)
            next_part(1)
            act.wait_ge(s_gs, 1)
            for n, c in enumerate(CHUNKS):
                act.wait_ge(s_wq[n], 16)
                for k in range(KD):
                    cols = slice(c * 512, (c + 1) * 512)
                    ins = act.activation(wqkv[:, 0, k, cols], wqkv32[:, k, cols], ACT.Copy, scale=gs[:, k:k + 1])
                ins.then_inc(s_whi, 1)
            squares(2)
            squares(3)

            def w_out_hi():
                act.wait_ge(s_small, 16 * 8)
                act.activation(wo[:, 0], wo32[:, :, :], ACT.Copy, scale=OUT_W).then_inc(s_whi, 1)

            act.wait_ge(s_rms, RSQRT_STEPS + 1)

            def program(sg):
                cur, nxt, n = sg.cur, sg.nxt, sg.n
                for kind, k in sg.steps:
                    use = sg.tu.get((kind, k))
                    if kind == "x":
                        act.wait_ge(*rt.full(sg.t, use))
                        act.activation(xT[:, 0, k, :], ps_t[:, use % 2, 0:P], ACT.Copy, scale=QKV_X).then_inc(s_xhi, 1)
                    if kind == "p" and k >= 4:
                        slot = sg.qu[kind, k] % 2
                        act.wait_ge(*rq.full(sg.q, sg.qu[kind, k]))
                        act.wait_ge(s_rope, n + 1)
                        act.activation(v[:, nxt, 8 * (k - 4):8 * (k - 4) + 8, 0:DH],
                                       ps_q[:, slot, :].rearrange("p (h d) -> p h d", h=8), ACT.Copy,
                                       scale=rms_seg[:, nxt:nxt + 1]).then_inc(rq.drained[slot], 1)
                    if kind == "r" and k % 2 == 0:
                        act.wait_ge(*rt.full(sg.t, use))
                        act.copy(qT[:, nxt, 2 * k:2 * k + 4, :], ps_t[:, use % 2, :].rearrange("p (j t) -> p j t", j=4)
                                 ).then_inc(rt.drained[use % 2], 1)
                    if kind == "s":
                        act.wait_ge(s_bias, sg.s * 8 + (k + 1))
                        for h in (2 * k, 2 * k + 1):
                            ins = act.activation(prob[:, h, :], ps_s[:, k % 2, (h % 2) * NK:(h % 2 + 1) * NK], ACT.Exp,
                                                 bias=nm[:, h:h + 1], scale=SCALE)
                        ins.then_inc(rs.drained[k % 2], 1)
                    if kind == "m":
                        act.wait_ge(*rt.full(sg.t, use))
                        act.copy(pmT[:, k, :], ps_t[:, use % 2, 0:P]).then_inc(rt.drained[use % 2], 1)
                    if kind == "t":
                        act.wait_ge(*rt.full(sg.t, use))
                        act.copy(pT[:, 4 * k:4 * k + 4, :], ps_t[:, use % 2, :].rearrange("p (h t) -> p h t", h=4)
                                 ).then_inc(rt.drained[use % 2], 1)
                    if kind == "o":
                        act.wait_ge(*rt.full(sg.t, use))
                        act.activation(oT[:, 0, 4 * k:4 * k + 4, :], ps_t[:, use % 2, :].rearrange("p (j t) -> p j t", j=4),
                                       ACT.Copy, scale=OUT_X).then_inc(s_ohi, 1)

            each_segment(act, program, w_out_hi)


def small_weights(nc, ctx, dram):
    def sb(name, shape):
        return ctx.enter_context(nc.sbuf_tensor(name, shape, F32))

    wq = sb("xw_q", [P, KD, D])
    wk = sb("xw_k", [P, 2, D])
    wv = sb("xw_v", [P, 2, D])
    wo = sb("xw_o", [P, KD, D])
    bq = sb("x_bias_q", [P, KD])
    bk = sb("x_bias_k", [P, KD])
    bv = sb("x_bias_v", [NCTX, D])
    bo = sb("x_bias_o", [P, D])
    spread = sb("key_of_flat", [NCTX, NCH * P])
    maskv = sb("head_of_flat", [P, NCH, HX // 2])
    maskk = sb("head_of_dim", [P, HX // 2])
    rev = sb("pick_order", [P, NE])
    gw = sb("router_w", [P, KD, E])
    lower = sb("rank_lower", [P, P])
    qnum = sb("tile_number", [P, NQ])
    small = [(wq[:, :, :], dram["xWq"].rearrange("(k p) n -> p k n", p=P)),
             (wk[:, 0, :], dram["xWk"][0:P, :]), (wk[0:CCTX - P, 1, :], dram["xWk"][P:CCTX, :]),
             (wv[:, 0, :], dram["xWv"][0:P, :]), (wv[0:CCTX - P, 1, :], dram["xWv"][P:CCTX, :]),
             (wo[:, :, :], dram["xWo"].rearrange("(k p) n -> p k n", p=P)),
             (bq[:, :], dram["xbq"]), (bk[:, :], dram["xbk"]),
             (bv[:, :], dram["xbv"].partition_broadcast(NCTX)), (bo[:, :], dram["xbo"].partition_broadcast(P)),
             (spread[:, :], dram["spread"]), (maskv[:, :, :], dram["maskv"]), (maskk[:, :], dram["maskk"]),
             (rev[:, :], dram["rev"]), (lower[:, :], dram["lower"]), (qnum[:, :], dram["qnum"]), (gw[:, :, :], dram["router"].rearrange("(k p) e -> p k e", p=P))]
    return [wq, wk, wv, wo, bq, bk, bv, bo, spread, maskv, maskk, rev, gw, lower, qnum], small


def cross_attention_and_experts(nc, dram, keep, y_dram, out):
    batches = dram["ctx_t"].shape[0]
    tiles = dram["x"].shape[0] // TT // batches
    ident = keep["ident"]
    with ExitStack() as ctx:
        def sb(name, shape, dt=F32):
            return ctx.enter_context(nc.sbuf_tensor(name, shape, dt))

        def sem(name):
            return ctx.enter_context(nc.semaphore(name))

        wg = sb("w_gate_split", [P, 2, KD, E, IP], F16)
        wu = sb("w_up_split", [P, 2, KD, E, IP], F16)
        wd = sb("w_down_split", [P, 2, E, len(IT), D], F16)
        wq, wk, wv, wo, bq, bk, bv, bo, spread, maskv, maskk, rev, gw, lower, qnum = keep["small"]
        s_w, small_loads = keep["small_loaded"], 16 * len(keep["small_from"])
        ctxT = sb("ctx_transposed", [P, 2, NCTX])
        kT = sb("ctx_k", [P, KD, NCTX])
        kbd = sb("ctx_k_blocks", [P, KD, HX // 2, NCTX])
        va = sb("ctx_v_and_one", [NCTX, HX, DX + 1])
        vbd = sb("ctx_v_blocks", [P, KD, NCH, OG])
        y1 = sb("y1", [P, 2, NB, D])
        SIL = 3

        def norm_buffers(name):
            return [sb(f"{name}_{part}", shape) for part, shape in (
                ("stats", [P, NB, 6]), ("mean_var", [P, NB, 2]), ("rstd", [P, NB]), ("tmp_a", [P, NB]), ("tmp_b", [P, NB]))]

        ln_attend, ln_final = norm_buffers("ln"), norm_buffers("ln_final")
        x1T = sb("x1_transposed", [P, KD, TT])
        oxT = x1T
        qT = sb("xq_transposed", [P, KD, TT])
        sc = sb("x_scores", [P, 2, KD, NCH * P])
        mx = sb("x_max", [P, 2, HX])
        pT = sb("x_probs_transposed", [P, 2, KD * NCH, P])
        rc = sb("x_recip", [P, HX])
        ox = sb("x_heads", [P, NB, D])
        x2 = sb("x2", [P, BB, D])
        x2T = x1T
        x2s = sb("x2_transposed_split", [P, 2, 2, KD, TT], F16)
        lg = sb("logits", [P, NB, E])
        top = sb("top", [P, 4, NB])
        ex = sb("expert_exp", [P, NB, NE])
        r8 = sb("router_tmp", [P, 4, NB, NE])
        gate = sb("shared_gate", [P, BB])
        sel = sb("chosen", [P, 2, BB, NE])
        wt = sb("choice_weights", [P, 2, BB])
        cum = sb("chosen_before", [P, BB + 1, NE])
        both_sel = sb("chosen_either", [P, BB, NE])
        ones = sb("ones", [P, P])
        tiles_i = sb("expert_tiles_int", [P, 2, NE], I32)
        run = sb("expert_tiles_running", [P, 2, 2 * NE])
        place = sb("place", [P, BB, NE])
        place_of = sb("place_times_choice", [P, BB, NE])
        place2 = sb("place_chosen", [P, 2, BB])
        idx = sb("pair_place", [P, 2, BB], I32)
        qcmp = sb("tile_past_expert", [P, NQ, NE])
        qexp = sb("tile_expert_f", [P, NQ])
        texp = sb("tile_expert", [P, NQ], I32)
        wt_u = sb("choice_weights_used", [P, 2, BB])
        idx_u = sb("pair_place_used", [P, 2, BB], I32)
        sil = sb("silu_gate", [P, SIL, TT])
        hS32 = sb("hidden_shared", [P, len(IT), TT])
        hS = hS32[:, :, :].bitcast(F16).rearrange("p n (z t) -> p n z t", z=2)
        hQ = sb("hidden_routed", [P, 2, 2, IP], F16)
        xin = sb("pairs_in", [P, 3, D])
        xq = sb("pairs_transposed_split", [P, 2, 2, KD, P], F16)
        eo = sb("pairs_out", [P, 2, D])
        gath = sb("pairs_gathered", [P, 2, 2, D])
        gathered = [gath[:, 0], gath[:, 1], xin[:, 0:2], eo]
        acc = sb("acc", [P, BB, D])
        fin = sb("out_tile", [P, NB, D])
        pairs_dram = nc.dram_tensor("tokens_by_expert", [NQ * P, D], F32, kind="Internal").ap()
        values_dram = nc.dram_tensor("values_by_expert", [NQ * P, D], F32, kind="Internal").ap()

        ps_t = ctx.enter_context(nc.psum_tensor("ps2_t", [P, 2, 512], F32))
        ps_q = ctx.enter_context(nc.psum_tensor("ps2_q", [P, 2, 512], F32))
        ps_m = ctx.enter_context(nc.psum_tensor("ps2_m", [P, 4, 512], F32))

        T_FIRST = {"tx": 0, "a0": 2, "a1": 5, "a2": 8, "a3": 11, "to": 14, "t2": 16}
        T_N = 18
        Q_K, Q_V, Q_VB, Q_PREP = 0, 1, 2, 6
        Q_FIRST, Q_N = {}, 0
        for step in LAYER + ["r"]:
            if step in ("q", "o", "r") or step[0] in "sw":
                Q_FIRST[step] = Q_N
                Q_N += Q_COST[step[0]]
        RANK = M_USE["rank",]
        H_N = len(IT) * tiles + NQ
        rt = Ring(sem, "x_transpose", 2)
        rq = Ring(sem, "x_project", 2)
        rm = Ring(sem, "x_matrix", 4)
        T_TURNS, Q_TURNS, M_TURNS = T_N * tiles // 2, (Q_PREP + Q_N * tiles) // 2, M_N // 4
        s_ffn = [sem(f"expert_loaded{e}") for e in range(E)]
        s_ctx = sem("ctx_loaded")
        s_static = sem("x_static_ready")
        s_y1 = [sem("y1_loaded0"), sem("y1_loaded1")]
        s_kbd = sem("ctx_k_blocks_ready")
        s_chain = sem("attention_chain")
        s_route = sem("router_chain")
        s_final = sem("final_norm_chain")
        s_step = sem("stats_waited")
        s_x1 = sem("x1_ready")
        s_x1b = sem("x1_and_bias_ready")
        s_max = sem("x_max_ready")
        s_sub = sem("x_shifted")
        s_exp = sem("x_exp_ready")
        s_recip = sem("x_recip_ready")
        s_x2 = sem("x2_ready")
        s_ex = sem("router_exp_ready")
        s_fin = sem("out_ready")
        s_whi = sem("expert_hi_ready")
        s_wlo = sem("expert_lo_ready")
        s_x2lo = sem("x2_lo_ready")
        s_pace = sem("waited")
        s_epace = sem("tile_expert_waited")
        s_adopt = sem("batch_adopted")
        s_zero = sem("pairs_zeroed")
        s_scat = sem("pairs_scattered")
        s_xin = [sem(f"pairs_loaded{n}") for n in range(3)]
        s_xqhi = sem("pairs_hi_ready")
        s_val = [sem(f"values_stored{n}") for n in range(2)]
        s_gath = [sem(f"values_gathered{n}") for n in range(GATHERS)]
        s_add = sem("values_added")
        s_hhi = sem("hidden_hi_ready")
        s_hlo = sem("hidden_lo_ready")
        s_out = sem("out_stored")
        LN_STEPS = 2 * NB + RSQRT_STEPS
        ROUTER_STEPS = 20
        CHAIN = 2 * LN_STEPS
        PLACE_STEPS = 1 + BB + 15
        ROUTE_B = ROUTER_STEPS * tiles + PLACE_STEPS
        FINAL_B = BB + 2 * LN_STEPS
        block = ctx.enter_context(nc.Block())

        class Tile:

            def __init__(self, i, off, j):
                self.i, self.off, self.j = i, off, j
                self.blocks = self.before(NB)
                self.ip, self.it, self.tQ = self.batches(Q_TURNS), self.before(T_N // 2), Q_PREP + Q_N * j
                self.chain = self.before(CHAIN)
                self.route = self.batches(ROUTE_B) + j * ROUTER_STEPS
                self.im = self.batches(M_TURNS)

            def batches(self, per):
                return self.i * per + self.off * per

            def before(self, per):
                return self.i * (per * tiles) + (self.off * tiles + self.j) * per

            def rows(self):
                return bass.ds(self.before(TT), TT)

        class Stage:

            def __init__(self, i, attend, experts, more, first=False):
                self.tiles = [Tile(i, attend, j) for j in range(tiles)] if attend is not None else []
                self.experts = Tile(i, experts, 0) if experts is not None else None
                self.more, self.first = more, first

            def following(self, a):
                if a.j + 1 < tiles:
                    return Tile(a.i, a.off, a.j + 1)
                return Tile(a.i, a.off + 1, 0) if self.more else None

            def steps(self):
                f = self.experts
                pieces = [([], None)] * CUT_LATER + [([("cut", e)], None) for e in range(E)] if self.first else []
                if f:
                    pieces = [([], f)] * LATER + [(piece, f) for piece in routed_steps()]
                work = []
                for a in self.tiles:
                    if a.j == 0:
                        work += [(step, a) for step in CONTEXT + LAYER + "t2 . r .".split()]
                    else:
                        work += [(step[1:], self.tiles[0]) if step[0] == "<" else (step, a) for step in SECOND]
                dots, dot, given = sum(step == "." for step, a in work), 0, 0
                for step, a in work:
                    if step != ".":
                        yield step, a
                        continue
                    dot += 1
                    while given < len(pieces) and (given < dot if self.first else given * dots < dot * len(pieces)):
                        yield from ((piece, pieces[given][1]) for piece in pieces[given][0])
                        given += 1
                for piece, of in pieces[given:]:
                    yield from ((step, of) for step in piece)
                combine, shared = combine_steps() if f else [], shared_steps()
                if self.tiles:
                    for step in LAST_ROUTER:
                        if step == "scatter":
                            yield ("scatter",), self.tiles[0]
                        elif step == "+":
                            yield from ((piece, self.tiles[0]) for piece in shared.pop(0))
                        elif step != "c":
                            yield step, self.tiles[-1]
                        elif combine:
                            yield from ((piece, f) for piece in combine.pop(0))
                    assert not shared, shared
                for piece in combine:
                    yield from ((step, f) for step in piece)

        def each_stage(eng, program):
            program(Stage(0, 0, None, True, first=True))
            with eng.Fori(0, batches - 2) as i:
                program(Stage(i, 1, 0, True))
            program(Stage(batches - 2, 1, 0, False))
            program(Stage(batches - 1, None, 0, False))

        def per_slot(f, n, slots, per=16):
            each = len(range(n % slots, NQ, slots))
            return f.batches(per * each) + per * (n // slots + 1)

        def staging(e):
            flat = hS32[:, :, :].rearrange("p n t -> p (n t)") if e % 2 else acc[:, 0:6, :].rearrange("p t d -> p (t d)")
            gate, up = (flat[:, w * KD * IP:(w + 1) * KD * IP].rearrange("p (k i) -> p k i", k=KD) for w in range(2))
            return gate, up, (xin if e % 2 else fin)[:, 0:len(IT), :]

        def staged(e):
            gate, up, down = staging(e)
            return [(gate, lambda d: d["w_gate"][e].rearrange("(k p) m -> p k m", p=P)),
                    (up, lambda d: d["w_up"][e].rearrange("(k p) m -> p k m", p=P)),
                    (down[:, 0:2, :], lambda d: d["w_down"][e, 0:2 * P, :].rearrange("(n p) d -> p n d", p=P)),
                    (down[0:I - 2 * P, 2, :], lambda d: d["w_down"][e, 2 * P:I, :])]

        def splits(e):
            gate, up, down = staging(e)
            last = I - 2 * P
            return [(gate, wg[:, :, :, e, :]), (up, wu[:, :, :, e, :]), (down[:, 0:2, :], wd[:, :, e, 0:2, :]),
                    (down[0:last, 2:3, :], wd[0:last, :, e, 2:3, :])]

        @block.sync
        def _(sp):
            for ring in (rt, rq, rm):
                ring.credit(sp)
            for s in (s_x1, s_x2, s_exp, s_out, s_val[0], s_val[1]):
                sp.sem_inc(s, 1)
            sp.sem_inc(s_x2lo, KD)
            sp.sem_inc(s_fin, BB)
            sp.sem_inc(s_hlo, SIL)

            def load(a):
                if a.j == 0:
                    ctx_t = dram["ctx_t"][bass.ds(a.batches(1), 1), :, :].rearrange("b c k -> (b c) k")
                    sp.dma_start(ctxT[:, 0, :], ctx_t[0:P, :]).then_inc(s_ctx, 16)
                    sp.dma_start(ctxT[0:CCTX - P, 1, :], ctx_t[P:CCTX, :]).then_inc(s_ctx, 16)
                sp.dma_start(y1[:, a.j, :, :], y_dram[a.rows(), :].rearrange("(t p) d -> p t d", p=P)).then_inc(s_y1[a.j], 16)

            load(Tile(0, 0, 0))

            def program(stage):
                if stage.first:
                    for e in range(E):
                        if e >= 2:
                            sp.wait_ge(s_wlo, e - 1)
                        for dst, part in staged(e):
                            sp.dma_start(dst, part(dram)).then_inc(s_ffn[e], 16)
                    sp.wait_ge(s_static, 6)
                    sp.dma_start(pairs_dram.rearrange("(t p) d -> p t d", p=P), bcast(gath[:, 0, 0, :], 1, NQ)).then_inc(s_zero, 16)
                for step, a in stage.steps():
                    if step == "n1s" and stage.following(a):
                        sp.wait_ge(s_x2, a.blocks + 1)
                        load(stage.following(a))
                    elif step[0] == "load":
                        q = step[1]
                        if q == 0:
                            sp.wait_ge(s_scat, a.batches(16 * 2 * BB) + 16 * 2 * BB)
                        if q >= 3:
                            sp.wait_ge(*rm.full(a.batches(M_TURNS), M_USE["turn", q - 3]))
                        sp.dma_start(xin[:, q % 3, :], pairs_dram[q * P:(q + 1) * P, :]).then_inc(s_xin[q % 3], 16)
                    elif step[0] == "back":
                        q = step[1]
                        sp.wait_ge(*rm.done(a.batches(M_TURNS), M_USE[step]))
                        sp.dma_start(values_dram[q * P:(q + 1) * P, :], eo[:, q % 2, :]).then_inc(s_val[q % 2], 16)
                    elif step[0] == "fn":
                        h = step[1]
                        sp.wait_ge(s_fin, a.batches(BB) + (BB + (h + 1) * NB))
                        sp.dma_start(out[bass.ds(a.batches(BB * P) + h * NB * P, NB * P), :].rearrange("(t p) d -> p t d", p=P),
                                     fin[:, :, :]).then_inc(s_out, 16)

            each_stage(sp, program)
            sp.wait_ge(s_out, 16 * tiles * batches + 1)

        @block.gpsimd
        def _(pool):
            pool.memset(va[:, :, DX:DX + 1], 1.0).then_inc(s_static, 1)
            pool.memset(sc[:, :, :, FLAT:NCH * P], 0.0).then_inc(s_static, 1)
            pool.memset(ones[:, :], 1.0).then_inc(s_static, 1)
            pool.memset(cum[:, 0, :], 0.0).then_inc(s_static, 1)
            pool.memset(run[:, :, 0:NE], 0.0).then_inc(s_static, 1)
            pool.memset(gath[:, 0, 0, :], 0.0).then_inc(s_static, 1)
            pool.wait_ge(s_w, small_loads)

            def program(stage):
                for step, a in stage.steps():
                    if step == "tx":
                        pool.wait_ge(*rt.full(a.it, T_FIRST["tx"] + 1))
                        for t in range(NB):
                            pool.tensor_tensor(y1[:, a.j, t, :], y1[:, a.j, t, :], bo[:, :], ALU.add).then_inc(s_x1b, 1)
                    elif step[0] == "s" and a:
                        t = int(step[1])
                        pool.wait_ge(s_max, a.blocks + (t + 1))
                        x = sc[:, t % 2, :, 0:FLAT].rearrange("p g (h k) -> p g h k", k=NCTX)
                        pool.tensor_tensor(x, x, bcast(mx[:, t % 2, :].rearrange("p (g h) -> p g h", g=KD), 3, NCTX),
                                           ALU.subtract).then_inc(s_sub, 1)
                    elif step == "t2":
                        for k in range(KD):
                            pool.wait_ge(*rt.done(a.it, T_FIRST["t2"] + k))
                            pool.tensor_tensor(x2s[:, a.j, 1, k, :], x2T[:, k, :], x2s[:, a.j, 0, k, :],
                                               ALU.subtract).then_inc(s_x2lo, 1)
                    elif step[0] == "scatter":
                        pool.wait_ge(s_zero, 16)
                        pool.wait_ge(s_route, a.batches(ROUTE_B) + ROUTE_B)
                        pool.wait_ge(s_x2, a.batches(BB) + BB + 1)
                        pool.sem_inc(s_pace, 1)
                        for t in range(BB):
                            for z in range(2):
                                pool.indirect_dma_start(pairs_dram, bass.IndirectOffsetOnAxis(ap=idx[:, z, t:t + 1], axis=0),
                                                        x2[:, t, :], None).then_inc(s_scat, 16)
                    elif step[0] == "gather":
                        t = step[1]
                        if t == 0:
                            pool.wait_ge(s_adopt, a.batches(1) + 1)
                            for n in range(2):
                                last = max(range(n, NQ, 2))
                                pool.wait_ge(s_val[n], per_slot(a, last, 2) + 1)
                        if t >= GATHERS:
                            pool.wait_ge(s_add, a.batches(BB) + (t - GATHERS + 1))
                        pool.sem_inc(s_pace, 1)
                        for z in range(2):
                            pool.indirect_dma_start(gathered[t % GATHERS][:, z, :], None, values_dram,
                                                    bass.IndirectOffsetOnAxis(ap=idx_u[:, z, t:t + 1], axis=0)
                                                    ).then_inc(s_gath[t % GATHERS], 16)

            each_stage(pool, program)

        @block.tensor
        def _(pe):
            pe.wait_ge(s_w, small_loads)
            pe.wait_ge(s_static, 6)
            rows = [P, CCTX - P]

            def program(stage):
                expert = {}

                def turn(src, use, ready):
                    for k in range(KD):
                        pe.wait_ge(*rt.free(a.it, use + k))
                        for t in range(NB):
                            if k == 0:
                                pe.wait_ge(*ready(t))
                            ins = pe.transpose(ps_t[:, (use + k) % 2, t * P:(t + 1) * P],
                                               src[:, t, k * P:(k + 1) * P], ident[:, :])
                        ins.then_inc(rt.filled[(use + k) % 2], 1)

                def turned(use):
                    for k in range(KD):
                        pe.wait_ge(*rt.done(a.it, use + k))

                def context_keys():
                    pe.wait_ge(s_ctx, a.batches(32) + 32)
                    pe.wait_ge(*rq.free(a.ip, Q_K))
                    for g in range(KD):
                        for k in range(2):
                            ins = pe.matmul(ps_q[:, 0, g * NCTX:(g + 1) * NCTX], wk[0:rows[k], k, g * P:(g + 1) * P],
                                            ctxT[0:rows[k], k, :], start=(k == 0), stop=(k == 1))
                    ins.then_inc(rq.filled[0], 1)

                def context_values():
                    pe.wait_ge(*rq.free(a.ip, Q_V))
                    for k in range(2):
                        ins = pe.matmul(ps_q[0:NCTX, 1, 0:D], ctxT[0:rows[k], k, :], wv[0:rows[k], k, :],
                                        start=(k == 0), stop=(k == 1))
                    ins.then_inc(rq.filled[1], 1)

                def value_blocks():
                    pe.wait_ge(*rq.done(a.ip, Q_V))
                    for u in range(4):
                        pe.wait_ge(*rq.free(a.ip, Q_VB + u))
                        for n in range(3 * u, min(3 * u + 3, KD * NCH)):
                            g, c = n // NCH, n % NCH
                            ins = pe.matmul(ps_q[:, u % 2, (n % 3) * OG:(n % 3 + 1) * OG], spread[:, c * P:(c + 1) * P],
                                            va[:, g * 8:g * 8 + 8, :], start=True, stop=True)
                        ins.then_inc(rq.filled[u % 2], 1)

                def queries():
                    turned(T_FIRST["tx"])
                    for g in range(KD):
                        use = a.tQ + Q_FIRST["q"] + g
                        pe.wait_ge(*rq.free(a.ip, use))
                        for k in range(KD):
                            ins = pe.matmul(ps_q[:, use % 2, :], wq[:, k, g * P:(g + 1) * P], x1T[:, k, :],
                                            start=(k == 0), stop=(k == KD - 1))
                        ins.then_inc(rq.filled[use % 2], 1)

                def scores(t):
                    if t == 0:
                        for g in range(KD):
                            pe.wait_ge(*rq.done(a.ip, a.tQ + Q_FIRST["q"] + g))
                        pe.wait_ge(s_kbd, a.batches(KD) + KD)
                    for u in range(4):
                        use = a.tQ + Q_FIRST[f"s{t}"] + u
                        pe.wait_ge(*rq.free(a.ip, use))
                        pe.matmul(ps_q[:, use % 2, 0:4 * NCTX], qT[:, u // 2, t * P:(t + 1) * P],
                                  kbd[:, u // 2, 4 * (u % 2):4 * (u % 2) + 4, :], start=True,
                                  stop=True).then_inc(rq.filled[use % 2], 1)

                def probs_transposed(t):
                    pe.wait_ge(s_exp, a.blocks + (t + 2))
                    for u in range(3):
                        use = T_FIRST[f"a{t}"] + u
                        pe.wait_ge(*rt.free(a.it, use))
                        for n in range(4 * u, min(4 * u + 4, KD * NCH)):
                            g, c = n // NCH, n % NCH
                            ins = pe.transpose(ps_t[:, use % 2, (n % 4) * P:(n % 4 + 1) * P],
                                               sc[:, t % 2, g, c * P:(c + 1) * P], ident[:, :])
                        ins.then_inc(rt.filled[use % 2], 1)

                def weigh(t):
                    if t == 0 and a.j == 0:
                        for u in range(4):
                            pe.wait_ge(*rq.done(a.ip, Q_VB + u))
                    for u in range(3):
                        pe.wait_ge(*rt.done(a.it, T_FIRST[f"a{t}"] + u))
                    use = a.tQ + Q_FIRST[f"w{t}"]
                    pe.wait_ge(*rq.free(a.ip, use))
                    for g in range(KD):
                        for c in range(NCH):
                            ins = pe.matmul(ps_q[:, use % 2, g * OG:(g + 1) * OG], pT[:, t % 2, g * NCH + c, :],
                                            vbd[:, g, c, :], start=(c == 0), stop=(c == NCH - 1))
                    ins.then_inc(rq.filled[use % 2], 1)

                def output_projection():
                    turned(T_FIRST["to"])
                    for u in range(2):
                        use = a.tQ + Q_FIRST["o"] + u
                        pe.wait_ge(*rq.free(a.ip, use))
                        for t in (2 * u, 2 * u + 1):
                            for k in range(KD):
                                ins = pe.matmul(ps_q[:, use % 2, (t % 2) * D:(t % 2 + 1) * D],
                                                oxT[:, k, t * P:(t + 1) * P], wo[:, k, :], start=(k == 0), stop=(k == KD - 1))
                        ins.then_inc(rq.filled[use % 2], 1)

                def router():
                    turned(T_FIRST["t2"])
                    use = a.tQ + Q_FIRST["r"]
                    pe.wait_ge(*rq.free(a.ip, use))
                    for t in range(NB):
                        for k in range(KD):
                            ins = pe.matmul(ps_q[:, use % 2, t * E:(t + 1) * E], x2T[:, k, t * P:(t + 1) * P],
                                            gw[:, k, :], start=(k == 0), stop=(k == KD - 1))
                    ins.then_inc(rq.filled[use % 2], 1)

                def rank():
                    pe.wait_ge(s_route, a.batches(ROUTE_B) + (ROUTER_STEPS * tiles + 1 + BB))
                    pe.wait_ge(*rm.free(a.im, RANK))
                    before, count = ps_m[:, RANK % 4, 0:BB * NE], ps_m[:, RANK % 4, BB * NE:(BB + 1) * NE]
                    pe.matmul(before, lower[:, :], both_sel[:, :, :], start=True, stop=False)
                    pe.matmul(before, ones[:, :], cum[:, 0:BB, :], start=False, stop=True)
                    pe.matmul(count, ones[:, :], cum[:, BB, :], start=True, stop=True).then_inc(rm.filled[RANK % 4], 1)

                def shared_up(j, n):
                    if n == 0:
                        pe.wait_ge(s_wlo, E)
                        pe.wait_ge(s_x2lo, a.batches(KD * tiles) + KD * (j + 2))
                    m0, m = IT[n]
                    for w, mat in enumerate((wg, wu)):
                        use = M_USE["up", j, n] + w
                        pe.wait_ge(*rm.free(a.im, use))
                        for k in range(KD):
                            for p, (zw, zx) in enumerate(PASSES):
                                ins = pe.matmul(ps_m[0:m, use % 4, :], mat[:, zw, k, NE, m0:m0 + m], x2s[:, j, zx, k, :],
                                                start=(k == 0 and p == 0), stop=(k == KD - 1 and p == 2))
                        ins.then_inc(rm.filled[use % 4], 1)

                def shared_down(j, u):
                    if u == 0:
                        pe.wait_ge(s_hlo, a.batches(len(IT) * tiles) + (len(IT) * (j + 1) + SIL))
                    use = M_USE["down", j, u]
                    pe.wait_ge(*rm.free(a.im, use))
                    for t in (2 * u, 2 * u + 1):
                        for n, (m0, m) in enumerate(IT):
                            for p, (zh, zw) in enumerate(PASSES):
                                ins = pe.matmul(ps_m[:, use % 4, (t % 2) * D:(t % 2 + 1) * D],
                                                hS[0:m, n, zh, t * P:(t + 1) * P], wd[0:m, zw, NE, n, :],
                                                start=(n == 0 and p == 0), stop=(n == len(IT) - 1 and p == 2))
                    ins.then_inc(rm.filled[use % 4], 1)

                def turn_pairs(q):
                    use = M_USE["turn", q]
                    pe.wait_ge(s_xin[q % 3], per_slot(a, q, 3))
                    pe.wait_ge(*rm.free(a.im, use))
                    for k in range(KD):
                        ins = pe.transpose(ps_m[:, use % 4, k * P:(k + 1) * P], xin[:, q % 3, k * P:(k + 1) * P], ident[:, :])
                    ins.then_inc(rm.filled[use % 4], 1)

                def routed_up(q):
                    if q == 0:
                        pe.wait_ge(s_route, a.batches(ROUTE_B) + ROUTE_B)
                        pe.sem_inc(s_epace, 1)
                    expert[q] = pe.value_load(texp[0:1, q:q + 1], min_val=0, max_val=(NE - 1) * IP)
                    pe.wait_ge(*rm.done(a.im, M_USE["turn", q]))
                    for w, mat in enumerate((wg, wu)):
                        use = M_USE["both", q] + w
                        pe.wait_ge(*rm.free(a.im, use))
                        for k in range(KD):
                            for p, (zw, zx) in enumerate(PASSES):
                                w_e = mat[:, zw, k, :, :].rearrange("p e m -> p (e m)")[:, bass.ds(expert[q], I)]
                                ins = pe.matmul(ps_m[:, use % 4, 0:I], xq[:, q % 2, zx, k, :], w_e,
                                                start=(k == 0 and p == 0), stop=(k == KD - 1 and p == 2))
                        ins.then_inc(rm.filled[use % 4], 1)

                def flip(q):
                    use = M_USE["flip", q]
                    pe.wait_ge(*rm.done(a.im, M_USE["both", q] + 1))
                    pe.wait_ge(*rm.free(a.im, use))
                    for n in range(len(IT)):
                        part = slice(n * P, (n + 1) * P)
                        ins = pe.transpose(ps_m[:, use % 4, part], sil[:, (len(IT) * tiles + q) % SIL, part], ident[:, :])
                    ins.then_inc(rm.filled[use % 4], 1)

                def routed_down(q):
                    pe.wait_ge(*rm.done(a.im, M_USE["flip", q]))
                    use = M_USE["back", q]
                    pe.wait_ge(*rm.free(a.im, use))
                    for n, (m0, m) in enumerate(IT):
                        for p, (zh, zw) in enumerate(PASSES):
                            w_t = wd[0:m, zw, :, :, :].rearrange("p e n d -> p (e n d)")[:, bass.ds(expert[q] * (len(IT) * D // IP) + n * D, D)]
                            ins = pe.matmul(ps_m[:, use % 4, 0:D], hQ[0:m, q % 2, zh, n * P:(n + 1) * P], w_t,
                                            start=(n == 0 and p == 0), stop=(n == len(IT) - 1 and p == 2))
                    ins.then_inc(rm.filled[use % 4], 1)
                    expert.pop(q)

                for step, a in stage.steps():
                    if step == "ck":
                        context_keys()
                    elif step == "cv":
                        context_values()
                    elif step == "cb":
                        value_blocks()
                    elif step == "tx":
                        turn(y1[:, a.j], T_FIRST["tx"], lambda t: (s_x1, a.blocks + (t + 2)))
                    elif step == "q":
                        queries()
                    elif step[0] == "s":
                        scores(int(step[1]))
                    elif step[0] == "a":
                        probs_transposed(int(step[1]))
                    elif step[0] == "w":
                        weigh(int(step[1]))
                    elif step == "to":
                        turn(ox, T_FIRST["to"], lambda t: rq.done(a.ip, a.tQ + Q_FIRST[f"w{t}"]))
                    elif step == "o":
                        output_projection()
                    elif step == "t2":
                        turn(x2[:, NB * a.j:NB * a.j + NB, :], T_FIRST["t2"], lambda t: (s_x2, a.blocks + (t + 2)))
                    elif step == "r":
                        router()
                    elif step == "kp":
                        rank()
                    elif step[0] == "up":
                        shared_up(*step[1:])
                    elif step[0] == "down":
                        shared_down(*step[1:])
                    elif step[0] == "turn":
                        turn_pairs(step[1])
                    elif step[0] == "both":
                        routed_up(step[1])
                    elif step[0] == "flip":
                        flip(step[1])
                    elif step[0] == "back":
                        routed_down(step[1])

            each_stage(pe, program)

        @block.vector
        def _(dve):
            def norm_stats(buffers, chain, src):
                st, ag = buffers[:2]
                for t in range(NB):
                    chain.at += 1
                    dve.bn_stats(st[:, t, :], src[:, t, :]).then_inc(chain.sem, 1)
                dve.wait_ge(chain.sem, chain.base + chain.at)
                dve.sem_inc(s_step, 1)
                for t in range(NB):
                    chain.at += 1
                    dve.bn_aggr(ag[:, t, :], st[:, t, :]).then_inc(chain.sem, 1)

            def norm_root(buffers, chain):
                _, ag, rstd, ta, tb = buffers
                dve.wait_ge(chain.sem, chain.base + chain.at)
                rsqrt_steps(dve, chain, rstd[:, :], ag[:, :, 1], LN_EPS, ta[:, :], tb[:, :])

            def norm_scale(buffers, src, dst, signal):
                _, ag, rstd, _, _ = buffers
                for t in range(NB):
                    dve.tensor_scalar(dst[:, t, :], src[:, t, :], ag[:, t, 0:1], rstd[:, t:t + 1], ALU.subtract,
                                      ALU.mult).then_inc(signal, 1)

            dve.wait_ge(s_w, small_loads)
            dve.wait_ge(s_static, 6)

            def program(stage):
                chain, route, final = Chain(s_chain, dve), Chain(s_route, dve), Chain(s_final, dve)

                def context_values():
                    dve.wait_ge(*rq.full(a.ip, Q_V))
                    dve.tensor_tensor(va[:, :, 0:DX], ps_q[0:NCTX, 1, 0:D].rearrange("p (h d) -> p h d", h=HX),
                                      bv[:, :].rearrange("p (h d) -> p h d", h=HX), ALU.add).then_inc(rq.drained[1], 1)
                    for g in range(KD):
                        dve.wait_ge(*rq.done(a.ip, Q_K))
                        dve.tensor_tensor(kbd[:, g, :, :], bcast(kT[:, g, :], 1, HX // 2), bcast(maskk[:, :], 2, NCTX),
                                          ALU.mult).then_inc(s_kbd, 1)

                def value_blocks():
                    for u in range(4):
                        dve.wait_ge(*rq.full(a.ip, Q_VB + u))
                        for n in range(3 * u, min(3 * u + 3, KD * NCH)):
                            g, c = n // NCH, n % NCH
                            ins = dve.tensor_tensor(vbd[:, g, c, :].rearrange("p (h d) -> p h d", h=HX // 2),
                                                    ps_q[:, u % 2, (n % 3) * OG:(n % 3 + 1) * OG].rearrange("p (h d) -> p h d", h=HX // 2),
                                                    bcast(maskv[:, c, :], 2, DX + 1), ALU.mult)
                        ins.then_inc(rq.drained[u % 2], 1)

                def maxima(t):
                    if t >= 2:
                        dve.wait_ge(*rt.full(a.it, T_FIRST[f"a{t - 2}"] + 2))
                    for u in range(4):
                        use = a.tQ + Q_FIRST[f"s{t}"] + u
                        dve.wait_ge(*rq.full(a.ip, use))
                        dve.tensor_scalar(sc[:, t % 2, u // 2, (u % 2) * 4 * NCTX:(u % 2 + 1) * 4 * NCTX],
                                          ps_q[:, use % 2, 0:4 * NCTX],
                                          CLAMP / XSCALE, -CLAMP / XSCALE, ALU.min, ALU.max).then_inc(rq.drained[use % 2], 1)
                    for u in (2, 3):
                        dve.wait_ge(*rq.done(a.ip, a.tQ + Q_FIRST[f"s{t}"] + u))
                    dve.tensor_reduce(mx[:, t % 2, :].rearrange("p (g h) -> p g h", g=KD),
                                      sc[:, t % 2, :, 0:FLAT].rearrange("p g (h k) -> p g h k", k=NCTX), AX.X, ALU.max
                                      ).then_inc(s_max, 1)

                def normalize(t):
                    use = a.tQ + Q_FIRST[f"w{t}"]
                    dve.wait_ge(*rq.full(a.ip, use))
                    o = ps_q[:, use % 2, 0:KD * OG].rearrange("p (h d) -> p h d", h=HX)
                    dve.reciprocal(rc[:, :], o[:, :, DX]).then_inc(s_recip, 1)
                    dve.wait_ge(s_recip, a.blocks + (t + 1))
                    dve.tensor_tensor(ox[:, t, :].rearrange("p (h d) -> p h d", h=HX), o[:, :, 0:DX],
                                      bcast(rc[:, :], 2, DX), ALU.mult).then_inc(rq.drained[use % 2], 1)

                def take(u, t):
                    use = T_FIRST[f"a{t}"] + u
                    n = min(4, KD * NCH - 4 * u)
                    dve.wait_ge(*rt.full(a.it, use))
                    dve.tensor_copy(pT[:, t % 2, 4 * u:4 * u + n, :],
                                    ps_t[:, use % 2, 0:n * P].rearrange("p (n t) -> p n t", n=n)
                                    ).then_inc(rt.drained[use % 2], 1)

                def residual():
                    for u in range(2):
                        use = a.tQ + Q_FIRST["o"] + u
                        dve.wait_ge(*rq.full(a.ip, use))
                        dve.wait_ge(s_x1b, a.blocks + (2 * u + 2))
                        dve.tensor_tensor(y1[:, a.j, 2 * u:2 * u + 2, :], y1[:, a.j, 2 * u:2 * u + 2, :],
                                          ps_q[:, use % 2, :].rearrange("p (t d) -> p t d", t=2), ALU.add
                                          ).then_inc(rq.drained[use % 2], 1)

                l8 = lg[:, :, 0:NE]
                m1, m2, pick, tmp = (top[:, n, :] for n in range(4))
                eq, e2 = r8[:, 2, :, :], r8[:, 3, :, :]

                def chosen(z):
                    return sel[:, z, NB * a.j:NB * a.j + NB, :]

                def first_of(k, vals, m):
                    route.then(dve.tensor_reduce(m, vals, AX.X, ALU.max))
                    route.then(dve.tensor_tensor(eq, vals, bcast(m, 2, NE), ALU.is_equal))
                    route.then(dve.tensor_tensor(eq, eq, bcast(rev[:, :], 1, NB), ALU.mult))
                    route.then(dve.tensor_reduce(pick, eq, AX.X, ALU.max))
                    route.then(dve.tensor_tensor(k, eq, bcast(pick, 2, NE), ALU.is_equal))

                def router_shift():
                    route.start(a.route)
                    use = a.tQ + Q_FIRST["r"]
                    dve.wait_ge(*rq.full(a.ip, use))
                    dve.tensor_scalar(lg[:, :, :], ps_q[:, use % 2, 0:NB * E].rearrange("p (t e) -> p t e", t=NB),
                                      1.0 / X_SCALE, None, ALU.mult).then_inc(rq.drained[use % 2], 1)
                    dve.wait_ge(*rq.done(a.ip, use))
                    route.then(dve.tensor_reduce(tmp, l8, AX.X, ALU.max))
                    route.then(dve.tensor_tensor(e2, l8, bcast(tmp, 2, NE), ALU.subtract))

                def router_second():
                    route.then(dve.scalar_tensor_tensor(out=e2, in0=chosen(0), scalar=-2.0, in1=ex[:, :, :], op0=ALU.mult, op1=ALU.add))
                    first_of(chosen(1), e2, m2)

                def router_weights():
                    blocks = slice(NB * a.j, NB * a.j + NB)
                    route.then(dve.tensor_tensor(tmp, m1, m2, ALU.add))
                    route.then(dve.tensor_scalar(tmp, tmp, W_SCALE * H_SCALE, None, ALU.mult))
                    route.then(dve.reciprocal(tmp, tmp))
                    route.then(dve.tensor_tensor(wt[:, 0, blocks], m1, tmp, ALU.mult))
                    route.then(dve.tensor_tensor(wt[:, 1, blocks], m2, tmp, ALU.mult))
                    route.then(dve.tensor_scalar(gate[:, blocks], gate[:, blocks], 1.0, W_SCALE * H_SCALE, ALU.add, ALU.mult))
                    route.then(dve.reciprocal(gate[:, blocks], gate[:, blocks]))
                    assert route.at == ROUTER_STEPS, route.at

                def count_before():
                    route.start(a.batches(ROUTE_B) + tiles * ROUTER_STEPS)
                    route.then(dve.tensor_tensor(both_sel[:, :, :], sel[:, 0], sel[:, 1], ALU.add))
                    for t in range(BB):
                        route.then(dve.tensor_tensor(cum[:, t + 1, :], cum[:, t, :], both_sel[:, t, :], ALU.add))

                def find_places():
                    dve.wait_ge(*rm.full(a.im, RANK))
                    route.then(dve.tensor_scalar(tiles_i[:, 0, :], ps_m[:, RANK % 4, BB * NE:(BB + 1) * NE], P - 1.0, None, ALU.add))
                    route.then(dve.tensor_scalar(tiles_i[:, 1, :], tiles_i[:, 0, :], 7, None, ALU.logical_shift_right))
                    route.then(dve.tensor_copy(run[:, 0, NE:], tiles_i[:, 1, :]))
                    for n, far in enumerate((1, 2, 4)):
                        src, dst = run[:, n % 2], run[:, (n + 1) % 2]
                        route.then(dve.tensor_tensor(dst[:, NE:], src[:, NE:], src[:, NE - far:2 * NE - far], ALU.add))
                    upto = run[:, 1]
                    dve.scalar_tensor_tensor(out=place[:, :, :], in0=bcast(upto[:, NE - 1:2 * NE - 1], 1, BB), scalar=float(P),
                                             in1=ps_m[:, RANK % 4, 0:BB * NE].rearrange("p (t e) -> p t e", t=BB),
                                             op0=ALU.mult, op1=ALU.add).then_inc(rm.drained[RANK % 4], 1)
                    dve.wait_ge(*rm.done(a.im, RANK))
                    for z in range(2):
                        route.then(dve.tensor_tensor(place_of[:, :, :], place[:, :, :], sel[:, z], ALU.mult))
                        route.then(dve.tensor_reduce(place2[:, z, :], place_of[:, :, :], AX.X, ALU.add))
                    route.then(dve.tensor_copy(idx[:, :, :], place2[:, :, :]))
                    route.then(dve.tensor_tensor(qcmp[:, :, :], bcast(qnum[:, :], 2, NE), bcast(upto[:, NE:], 1, NQ), ALU.is_ge))
                    route.then(dve.tensor_reduce(qexp[:, :], qcmp[:, :, :], AX.X, ALU.add))
                    route.then(dve.tensor_scalar(qexp[:, :], qexp[:, :], NE - 1.0, float(IP), ALU.min, ALU.mult))
                    route.then(dve.tensor_copy(texp[:, :], qexp[:, :]))
                    assert route.at == PLACE_STEPS, route.at

                def times_up(k, use, cols):
                    dve.wait_ge(*rm.done(a.im, use))
                    dve.wait_ge(*rm.full(a.im, use + 1))
                    h = sil[0:cols[0], k % SIL, 0:cols[1]]
                    dve.scalar_tensor_tensor(out=h, in0=ps_m[0:cols[0], (use + 1) % 4, 0:cols[1]], scalar=H_SCALE / (W_SCALE * X_SCALE),
                                             in1=h, op0=ALU.mult, op1=ALU.mult).then_inc(rm.drained[(use + 1) % 4], 1)

                def add_shared(j, u):
                    use = M_USE["down", j, u]
                    if u == 0:
                        dve.wait_ge(s_fin, a.batches(BB) + NB * (j + 1))
                    dve.wait_ge(*rm.full(a.im, use))
                    for t in (2 * u, 2 * u + 1):
                        n = NB * j + t
                        ins = dve.scalar_tensor_tensor(out=acc[:, n, :], in0=ps_m[:, use % 4, (t % 2) * D:(t % 2 + 1) * D],
                                                       scalar=gate[:, n:n + 1], in1=x2[:, n, :], op0=ALU.mult, op1=ALU.add)
                    ins.then_inc(rm.drained[use % 4], 1)

                def pairs_lo(q):
                    use = M_USE["turn", q]
                    if q == 0:
                        dve.tensor_copy(wt_u[:, :, :], wt[:, :, :])
                        dve.tensor_copy(idx_u[:, :, :], idx[:, :, :]).then_inc(s_adopt, 1)
                    dve.wait_ge(s_xqhi, a.batches(NQ) + (q + 1))
                    dve.scalar_tensor_tensor(out=xq[:, q % 2, 1], in0=ps_m[:, use % 4, 0:D].rearrange("p (k t) -> p k t", k=KD),
                                             scalar=X_SCALE, in1=xq[:, q % 2, 0], op0=ALU.mult, op1=ALU.subtract
                                             ).then_inc(rm.drained[use % 4], 1)

                def add_routed(t):
                    if t == 0:
                        for u in range(2):
                            for j in range(tiles):
                                dve.wait_ge(*rm.done(a.im, M_USE["down", j, u]))
                    dve.wait_ge(s_gath[t % GATHERS], a.batches(32 * BB // GATHERS) + 32 * (t // GATHERS + 1))

                    def weighted(z):
                        return dve.scalar_tensor_tensor(out=acc[:, t, :], in0=gathered[t % GATHERS][:, z, :], scalar=wt_u[:, z, t:t + 1],
                                                        in1=acc[:, t, :], op0=ALU.mult, op1=ALU.add)

                    final.then(weighted(0))
                    weighted(1).then_inc(s_add, 1)

                for step, a in stage.steps():
                    if step[0] == "cut":
                        e = step[1]
                        dve.wait_ge(s_whi, e + 1)
                        for src, dst in splits(e):
                            ins = dve.scalar_tensor_tensor(out=dst[:, 1], in0=src, scalar=W_SCALE, in1=dst[:, 0],
                                                           op0=ALU.mult, op1=ALU.subtract)
                        ins.then_inc(s_wlo, 1)
                    elif step == "cv":
                        context_values()
                    elif step == "cb":
                        value_blocks()
                    elif step == "n1s":
                        chain.start(a.chain)
                        dve.wait_ge(s_y1[a.j], a.batches(16) + 16)
                        norm_stats(ln_attend, chain, y1[:, a.j])
                    elif step == "n1r" or step == "n2r":
                        norm_root(ln_attend, chain)
                    elif step == "n1n":
                        norm_scale(ln_attend, y1[:, a.j], y1[:, a.j], s_x1)
                    elif step[0] == "s" and a:
                        maxima(int(step[1]))
                    elif step[0] == "a" and a:
                        take(1, int(step[1]))
                    elif step[0] == "w":
                        normalize(int(step[1]))
                    elif step == "o":
                        residual()
                    elif step == "n2s":
                        for u in range(2):
                            dve.wait_ge(*rq.done(a.ip, a.tQ + Q_FIRST["o"] + u))
                        norm_stats(ln_attend, chain, y1[:, a.j])
                    elif step == "n2n":
                        norm_scale(ln_attend, y1[:, a.j], x2[:, NB * a.j:NB * a.j + NB, :], s_x2)
                    elif step == "r1":
                        router_shift()
                    elif step == "r2":
                        dve.wait_ge(s_ex, a.before(2) + 2)
                        first_of(chosen(0), ex[:, :, :], m1)
                    elif step == "r3":
                        router_second()
                    elif step == "r4":
                        router_weights()
                    elif step == "k0":
                        count_before()
                    elif step == "k1":
                        find_places()
                    elif step[0] == "up":
                        _, j, n = step
                        times_up(len(IT) * j + n, M_USE[step], (IT[n][1], TT))
                    elif step[0] == "hi":
                        _, j, n = step
                        k, m = len(IT) * j + n, IT[n][1]
                        dve.wait_ge(s_hhi, a.batches(H_N) + (k + 1))
                        dve.tensor_tensor(hS[0:m, n, 1, :], sil[0:m, k % SIL, :], hS[0:m, n, 0, :], ALU.subtract
                                          ).then_inc(s_hlo, 1)
                    elif step[0] == "down":
                        add_shared(*step[1:])
                    elif step[0] == "turn":
                        pairs_lo(step[1])
                    elif step[0] == "both":
                        times_up(len(IT) * tiles + step[1], M_USE[step], (P, I))
                    elif step[0] == "flip":
                        q = step[1]
                        use = M_USE[step]
                        dve.wait_ge(s_hhi, a.batches(H_N) + (len(IT) * tiles + q + 1))
                        dve.tensor_tensor(hQ[:, q % 2, 1, :], ps_m[:, use % 4, 0:IP], hQ[:, q % 2, 0, :], ALU.subtract
                                          ).then_inc(rm.drained[use % 4], 1)
                    elif step[0] == "add":
                        if step[1] == 0:
                            final.start(a.batches(FINAL_B))
                        add_routed(step[1])
                    elif step[0] == "fs":
                        h = step[1]
                        dve.wait_ge(s_add, a.batches(BB) + NB * (h + 1))
                        norm_stats(ln_final, final, acc[:, NB * h:NB * h + NB, :])
                    elif step[0] == "fr":
                        norm_root(ln_final, final)
                    elif step[0] == "fn":
                        h = step[1]
                        dve.wait_ge(s_out, a.batches(16 * tiles) + (16 * h + 1))
                        norm_scale(ln_final, acc[:, NB * h:NB * h + NB, :], fin, s_fin)

            each_stage(dve, program)

        @block.scalar
        def _(act):
            act.wait_ge(s_w, small_loads)
            act.wait_ge(s_static, 6)

            def program(stage):

                def context_keys():
                    act.wait_ge(*rq.full(a.ip, Q_K))
                    for g in range(KD):
                        ins = act.activation(kT[:, g, :], ps_q[:, 0, g * NCTX:(g + 1) * NCTX], ACT.Identity, bias=bk[:, g:g + 1])
                    ins.then_inc(rq.drained[0], 1)

                def take_tile(dst, use):
                    for k in range(KD):
                        act.wait_ge(*rt.full(a.it, use + k))
                        act.copy(dst[:, k, :], ps_t[:, (use + k) % 2, :]).then_inc(rt.drained[(use + k) % 2], 1)

                def queries():
                    for g in range(KD):
                        use = a.tQ + Q_FIRST["q"] + g
                        act.wait_ge(*rq.full(a.ip, use))
                        act.activation(qT[:, g, :], ps_q[:, use % 2, :], ACT.Identity, bias=bq[:, g:g + 1]
                                       ).then_inc(rq.drained[use % 2], 1)

                def take(u, t):
                    use = T_FIRST[f"a{t}"] + u
                    n = min(4, KD * NCH - 4 * u)
                    act.wait_ge(*rt.full(a.it, use))
                    act.copy(pT[:, t % 2, 4 * u:4 * u + n, :],
                             ps_t[:, use % 2, 0:n * P].rearrange("p (n t) -> p n t", n=n)).then_inc(rt.drained[use % 2], 1)

                def exponential(t):
                    act.wait_ge(s_sub, a.blocks + (t + 1))
                    x = sc[:, t % 2, :, 0:FLAT]
                    act.activation(x, x, ACT.Exp, scale=XSCALE).then_inc(s_exp, 1)

                def router_exponentials():
                    act.wait_ge(s_route, a.route + 2)
                    act.activation(ex[:, :, :], r8[:, 3, :, :], ACT.Exp).then_inc(s_ex, 1)
                    act.activation(gate[:, NB * a.j:NB * a.j + NB], lg[:, :, NE], ACT.Exp, scale=-1.0).then_inc(s_ex, 1)

                def silu(k, use, cols):
                    act.wait_ge(*rm.full(a.im, use))
                    if k < len(IT) * tiles + SIL:
                        act.wait_ge(s_hlo, a.batches(len(IT) * tiles) + min(max(k + 1, SIL), len(IT) * tiles + SIL))
                    else:
                        act.wait_ge(*rm.full(a.im, M_USE["flip", k - len(IT) * tiles - SIL]))
                    act.activation(sil[0:cols[0], k % SIL, 0:cols[1]], ps_m[0:cols[0], use % 4, 0:cols[1]], ACT.Silu,
                                   scale=1.0 / (W_SCALE * X_SCALE)).then_inc(rm.drained[use % 4], 1)

                def pairs_hi(q):
                    use = M_USE["turn", q]
                    act.wait_ge(*rm.full(a.im, use))
                    act.activation(xq[:, q % 2, 0], ps_m[:, use % 4, 0:D].rearrange("p (k t) -> p k t", k=KD), ACT.Copy,
                                   scale=X_SCALE).then_inc(s_xqhi, 1)

                def values(q):
                    use = M_USE["back", q]
                    if q < 2:
                        act.wait_ge(s_val[q % 2], per_slot(a, q, 2) - 16 + 1)
                    else:
                        act.wait_ge(s_val[q % 2], per_slot(a, q - 2, 2) + 1)
                    act.wait_ge(*rm.full(a.im, use))
                    act.copy(eo[:, q % 2, :], ps_m[:, use % 4, 0:D]).then_inc(rm.drained[use % 4], 1)

                for step, a in stage.steps():
                    if step[0] == "cut":
                        e = step[1]
                        act.wait_ge(s_ffn[e], 16 * 4)
                        for src, dst in splits(e):
                            ins = act.activation(dst[:, 0], src, ACT.Copy, scale=W_SCALE)
                        ins.then_inc(s_whi, 1)
                    elif step == "ck":
                        context_keys()
                    elif step == "tx":
                        act.wait_ge(s_x2lo, a.before(KD) + KD)
                        take_tile(x1T, T_FIRST["tx"])
                    elif step == "q":
                        queries()
                    elif step[0] == "e":
                        exponential(int(step[1]))
                    elif step[0] == "a" and a:
                        take(0, int(step[1])), take(2, int(step[1]))
                    elif step == "to":
                        take_tile(oxT, T_FIRST["to"])
                    elif step == "t2":
                        for k in range(KD):
                            use = T_FIRST["t2"] + k
                            act.wait_ge(*rt.full(a.it, use))
                            for dst in (x2T[:, k, :], x2s[:, a.j, 0, k, :]):
                                ins = act.activation(dst, ps_t[:, use % 2, :], ACT.Copy, scale=X_SCALE)
                            ins.then_inc(rt.drained[use % 2], 1)
                    elif step == "re":
                        router_exponentials()
                    elif step[0] == "up":
                        _, j, n = step
                        silu(len(IT) * j + n, M_USE[step], (IT[n][1], TT))
                    elif step[0] == "hi":
                        _, j, n = step
                        k, m = len(IT) * j + n, IT[n][1]
                        act.wait_ge(*rm.done(a.im, M_USE["up", j, n] + 1))
                        act.copy(hS[0:m, n, 0, :], sil[0:m, k % SIL, :]).then_inc(s_hhi, 1)
                    elif step[0] == "turn":
                        pairs_hi(step[1])
                    elif step[0] == "both":
                        silu(len(IT) * tiles + step[1], M_USE[step], (P, I))
                    elif step[0] == "flip":
                        q = step[1]
                        act.wait_ge(*rm.full(a.im, M_USE[step]))
                        act.copy(hQ[:, q % 2, 0, :], ps_m[:, M_USE[step] % 4, 0:IP]).then_inc(s_hhi, 1)
                    elif step[0] == "back":
                        values(step[1])

            each_stage(act, program)


def decoder_layer(nc, dram, out):
    y_dram = nc.dram_tensor("x_and_attention", [dram["x"].shape[0], D], F32, kind="Internal").ap()
    with ExitStack() as ctx:
        buffers, sources = small_weights(nc, ctx, dram)
        keep = {"ident": ctx.enter_context(nc.sbuf_tensor("identity", [P, P], F32)), "small": buffers, "small_from": sources,
                "small_loaded": ctx.enter_context(nc.semaphore("x_weights_loaded"))}
        self_attention(nc, dram, keep, y_dram)
        cross_attention_and_experts(nc, dram, keep, y_dram, out)


def constants(np, n):
    inv = (1.0 / np.float32(10000.0) ** (np.arange(0, DH, 2, dtype=np.float32) / np.float32(DH))).astype(np.float32)
    angle = (np.arange(n, dtype=np.float32)[:, None] * inv[None, :]).astype(np.float32)
    cos, sin = np.cos(angle), np.sin(angle)
    key, query = np.arange(NK)[None, :], np.arange(SEG)[:, None]
    bf16 = mybir.dt.np(BF16)
    causal = np.where((key >= SEG) | (key <= query), 0.0, -1e30).astype(bf16)
    flat = np.arange(NCH * P)
    real = flat < FLAT
    head = flat.reshape(NCH, P).T[:, :, None] // NCTX
    return {
        "rope": np.stack([cos, sin, -sin], axis=1).astype(np.float32),
        "ident": np.eye(P, dtype=np.float32),
        "identb": np.eye(P, dtype=np.float32).astype(bf16),
        "causal": np.ascontiguousarray(np.broadcast_to(causal[:, None, :], (SEG, 2, NK))),
        "spread": ((flat[None, :] % NCTX == np.arange(NCTX)[:, None]) & real).astype(np.float32),
        "maskv": (head == np.arange(HX // 2)).astype(np.float32),
        "maskk": (np.arange(P)[:, None] // DX == np.arange(HX // 2)).astype(np.float32),
        "lower": np.triu(np.ones((P, P), np.float32), 1),
        "qnum": np.ascontiguousarray(np.broadcast_to(np.arange(NQ, dtype=np.float32), (P, NQ))),
        "rev": np.ascontiguousarray(np.broadcast_to(np.arange(NE, 0, -1, dtype=np.float32), (P, NE))),
    }


def laid_out(np, a):
    x = a["x"]
    qkv = a["L0_attn_w_qkv"].reshape(3, 2, 8, DH // 2, 2, D)
    qk = qkv[:2].transpose(5, 0, 1, 4, 2, 3).reshape(D, 2 * H * DH)
    v = qkv[2].reshape(H * DH, D).T
    mk = a["L0_attn_pm"][0].reshape(H // 2, 2, MEM, DH // 2, 2)
    mem_k = np.zeros((2, DH, H // 2, 2, MEM), np.float32)
    for z in range(2):
        mem_k[z, :, :, z, :] = mk[:, z].transpose(3, 2, 0, 1).reshape(DH, H // 2, MEM)
    mv = a["L0_attn_pm"][1].reshape(2, 8, MEM, DH)
    mem_v = np.zeros((2, 8, MEM, 8, DH + 1), np.float32)
    for h in range(8):
        mem_v[:, h, :, h, :DH] = mv[:, h]
        mem_v[:, h, :, h, DH] = 1.0
    pos = constants(np, x.shape[1])
    rope = np.concatenate([pos.pop("rope")] * x.shape[0])
    join = lambda routed, shared: np.concatenate([routed, shared[None]])
    padded = lambda w: np.pad(w, ((0, 0), (0, 0), (0, IP - I)))
    return {
        "x": x.reshape(-1, D), "rope": rope, **pos,
        "attn_g": a["L0_attn_g"].reshape(KD, P).T, "w_qkv": np.concatenate([qk, v], axis=1),
        "w_out": a["L0_attn_w_out"].T, "mem_k": mem_k.reshape(P, H // 2, 2, MEM), "mem_v": mem_v.reshape(2, P, 8, DH + 1),
        "ctx_t": a["ctx_768"].transpose(0, 2, 1),
        "xWq": a["L0_xattn_Wq"], "xWk": a["L0_xattn_Wk"], "xWv": a["L0_xattn_Wv"], "xWo": a["L0_xattn_Wo"],
        "xbq": a["L0_xattn_bq"].reshape(KD, P).T, "xbk": a["L0_xattn_bk"].reshape(KD, P).T,
        "xbv": a["L0_xattn_bv"], "xbo": a["L0_xattn_bo"],
        "router": np.concatenate([a["L0_ffn_gate_w"], a["L0_ffn_shared_gate_w"]]).T,
        "w_gate": padded(join(a["L0_ffn_w_gate"], a["L0_ffn_sw_gate"])), "w_up": padded(join(a["L0_ffn_w_up"], a["L0_ffn_sw_up"])),
        "w_down": join(a["L0_ffn_w_down"], a["L0_ffn_sw_down"]),
    }


def kernel(**inputs):
    import numpy as np
    import concourse.bacc as bacc
    from concourse.bass_utils import run_bass_kernel_spmd

    given = {k: np.asarray(v) for k, v in inputs.items()}
    arrays = {f"in_{k}": np.ascontiguousarray(v) for k, v in laid_out(np, given).items()}
    nc = bacc.Bacc("TRN2", target_bir_lowering=False, num_devices=1)
    dram = {k[3:]: nc.dram_tensor(k, v.shape, mybir.dt.from_np(v.dtype), kind="ExternalInput").ap() for k, v in arrays.items()}
    out = nc.dram_tensor("out", arrays["in_x"].shape, F32, kind="ExternalOutput").ap()
    decoder_layer(nc, dram, out)
    r = run_bass_kernel_spmd(nc, [arrays], core_ids=[0])
    return r.results[0]["out"].reshape(given["x"].shape)
```
